# Optimizing a Trainium2 kernel written in Bass

```python
import numpy as np
import jax
import jax.numpy as jnp

def _softmax(x, axis=-1):
    return jax.nn.softmax(x, axis=axis)

def _gelu(x):
    return jax.nn.gelu(x, approximate=True)

def _silu(x):
    return jax.nn.silu(x)

def _sigmoid(x):
    return jax.nn.sigmoid(x)

def _layernorm(x, axis=-1, eps=1e-05):
    m = jnp.mean(x, axis=axis, keepdims=True)
    v = jnp.var(x, axis=axis, keepdims=True)
    return (x - m) / jnp.sqrt(v + eps)

def _scatter_add(tgt, idx, src, axis=0):
    return tgt.at[idx].add(src)

def _segment_sum(src, seg, n):
    return jax.ops.segment_sum(src, seg, n)
kernel_name = 'mk_decoder_postln_d2_seqx_r8_714a7e'

def setup_inputs(seed: int=0):
    np.random.seed(seed)
    _w = jnp.asarray

    def _rec_inputs():
        import jax
        import jax.numpy as jnp
        _rk = jax.random.key(seed)
        x = 0.0003765 + 1 * jax.random.normal(jax.random.fold_in(_rk, 1), (8, 128, 256), jnp.float32)
        _lenS = 128 - jax.random.randint(jax.random.fold_in(_rk, 7), (8,), 0, max(1, 128 // 4) + 1, jnp.int32)
        _lenS2 = 128 - jax.random.randint(jax.random.fold_in(_rk, 8), (8,), 0, max(1, 128 // 4) + 1, jnp.int32)
        _ctx_2048P = jax.random.normal(jax.random.fold_in(_rk, 11), (8, 16, 256), jnp.float32)
        _ctx_2048c = jax.random.dirichlet(jax.random.fold_in(_rk, 511), 0.3 * jnp.ones((16,), jnp.float32), (8, 128))
        _ctx_2048t = jnp.einsum('bsk,bkd->bsd', _ctx_2048c, _ctx_2048P)
        _ctx_2048t = _ctx_2048t * jax.lax.rsqrt(jnp.mean(jnp.square(_ctx_2048t)) + 1e-12) * 0.953939
        ctx_2048 = -0.000292821 + 1.00034 * (_ctx_2048t + 0.3 * jax.random.normal(jax.random.fold_in(_rk, 611), (8, 128, 256), jnp.float32))
        fside_S2_0 = -0.00337071 + 1.01897 * jax.random.normal(jax.random.fold_in(_rk, 12), (128,), jnp.float32)
        return (x, ctx_2048, fside_S2_0)
    x, ctx_2048, fside_S2_0 = _rec_inputs()

    def _L0_attn_setup():
        import jax, jax.numpy as jnp
        import numpy as np
        B, S, H_DIM = (2, 256, 256)
        N_HEADS, D_HEAD = (16, 128)
        key = jax.random.key(seed)
        k1, k2, k3 = jax.random.split(key, 3)
        x = jax.random.normal(k1, (B, S, H_DIM), dtype=jnp.float32)
        w_qkv = jax.random.normal(k2, (H_DIM, 3 * N_HEADS * D_HEAD), dtype=jnp.float32) * 0.02
        w_o = jax.random.normal(k3, (N_HEADS * D_HEAD, H_DIM), dtype=jnp.float32) * 0.02
        return {'x': x, 'w_qkv': w_qkv, 'w_o': w_o}
    _L0_attn_all = _L0_attn_setup()
    _L0_attn_in = {k: v for k, v in _L0_attn_all.items() if k in ('w_qkv', 'w_o')}
    del _L0_attn_all

    def _L0_xattn_setup():
        import jax, jax.numpy as jnp
        import numpy as np
        key = jax.random.key(seed)
        k1, k2, k3, k4, k5 = jax.random.split(key, 5)
        B, D_MODEL, L = (2, 128, 256)
        HEAD_DIM = 8
        H = D_MODEL // HEAD_DIM
        return {'k': jax.random.normal(k1, (B, D_MODEL, L), dtype=jnp.float32), 'v': jax.random.normal(k2, (B, D_MODEL, L), dtype=jnp.float32), 'q': jax.random.normal(k3, (B, D_MODEL, L), dtype=jnp.float32), 'ssm_kernel': jax.random.normal(k4, (H, L), dtype=jnp.float32), 'D': jax.random.normal(k5, (H,), dtype=jnp.float32), 'head_dim': HEAD_DIM}
    _L0_xattn_all = _L0_xattn_setup()
    _L0_xattn_in = {k: v for k, v in _L0_xattn_all.items() if k in ('ssm_kernel', 'D')}
    del _L0_xattn_all

    def _L0_ffn_setup():
        import jax, jax.numpy as jnp
        import numpy as np
        NUM_EXPERTS = 32
        TOP_K = 4
        HIDDEN = 256
        INTER = 96
        key = jax.random.key(seed)
        k1, k2, k3, k4 = jax.random.split(key, 4)
        hidden_states = jax.random.normal(k1, (4, 64, HIDDEN), dtype=jnp.float32)
        gate = jax.random.normal(k2, (HIDDEN, NUM_EXPERTS), dtype=jnp.float32) * 0.02
        gate_up_proj = jax.random.normal(k3, (NUM_EXPERTS, HIDDEN, 2 * INTER), dtype=jnp.float32) * 0.02
        down_proj = jax.random.normal(k4, (NUM_EXPERTS, INTER, HIDDEN), dtype=jnp.float32) * 0.02
        return {'hidden_states': hidden_states, 'gate': gate, 'gate_up_proj': gate_up_proj, 'down_proj': down_proj}
    _L0_ffn_all = _L0_ffn_setup()
    _L0_ffn_in = {k: v for k, v in _L0_ffn_all.items() if k in ('gate', 'gate_up_proj', 'down_proj')}
    del _L0_ffn_all

    def _L1_attn_setup():
        import jax, jax.numpy as jnp
        import numpy as np
        import math
        D = 256
        H = 32
        HKV = 8
        HD = D // H
        ROPE_BASE = 10000.0

        def _rope_cache(T, hd, base=ROPE_BASE):
            theta = 1.0 / base ** (jnp.arange(0, hd, 2, dtype=jnp.float32) / hd)
            t = jnp.arange(T, dtype=jnp.float32)
            freqs = t[:, None] * theta[None, :]
            return (jnp.cos(freqs), jnp.sin(freqs))

        def _apply_rope(x, cos, sin):
            B, Hh, T, hd = x.shape
            x_ = x.reshape(B, Hh, T, hd // 2, 2)
            x1, x2 = (x_[..., 0], x_[..., 1])
            c = cos[None, None, :, :]
            s = sin[None, None, :, :]
            rx1 = x1 * c - x2 * s
            rx2 = x1 * s + x2 * c
            return jnp.stack([rx1, rx2], axis=-1).reshape(B, Hh, T, hd)
        key = jax.random.key(seed)
        ks = jax.random.split(key, 5)
        B, T = (1, 256)
        sc = 0.02
        return {'x': jax.random.normal(ks[0], (B, T, D), dtype=jnp.float32), 'wq': jax.random.normal(ks[1], (D, D), dtype=jnp.float32) * sc, 'wk': jax.random.normal(ks[2], (HKV * HD, D), dtype=jnp.float32) * sc, 'wv': jax.random.normal(ks[3], (HKV * HD, D), dtype=jnp.float32) * sc, 'wo': jax.random.normal(ks[4], (D, D), dtype=jnp.float32) * sc}
    _L1_attn_all = _L1_attn_setup()
    _L1_attn_in = {k: v for k, v in _L1_attn_all.items() if k in ('wq', 'wk', 'wv', 'wo')}
    del _L1_attn_all

    def _L1_xattn_setup():
        import jax, jax.numpy as jnp
        import numpy as np
        key = jax.random.key(seed)
        ks = jax.random.split(key, 5)
        B, D, L, NH = (2, 128, 256, 8)
        H = D // NH
        return {'v': jax.random.normal(ks[0], (B, D, L), jnp.float32), 'k': jax.random.normal(ks[1], (H, L), jnp.float32) * 0.1, 'bias': jax.random.normal(ks[2], (D,), jnp.float32), 'x1': jax.random.normal(ks[3], (B, D, L), jnp.float32), 'x2': jax.random.normal(ks[4], (B, D, L), jnp.float32), 'num_heads': NH}
    _L1_xattn_all = _L1_xattn_setup()
    _L1_xattn_in = {k: v for k, v in _L1_xattn_all.items() if k in ('k',)}
    del _L1_xattn_all

    def _L1_ffn_setup():
        import jax, jax.numpy as jnp
        import numpy as np
        B, S, D = (4, 256, 256)
        DFF = 704
        E, K, R = (8, 2, 16)
        SCALING = 32.0 / 16.0
        key = jax.random.key(seed)
        ks = jax.random.split(key, 12)
        s = lambda k, shape, scale: jax.random.normal(k, shape, dtype=jnp.float32) * scale
        return {'x': s(ks[0], (B, S, D), 1.0), 'Wg': s(ks[1], (DFF, D), 0.02), 'Wu': s(ks[2], (DFF, D), 0.02), 'Wd': s(ks[3], (D, DFF), 0.02), 'Wr': s(ks[4], (E, D), 0.02), 'Ag': s(ks[5], (E, R, D), 0.02), 'Bg': s(ks[6], (E, DFF, R), 0.02), 'Au': s(ks[7], (E, R, D), 0.02), 'Bu': s(ks[8], (E, DFF, R), 0.02), 'Ad': s(ks[9], (E, R, DFF), 0.02), 'Bd': s(ks[10], (E, D, R), 0.02)}
    _L1_ffn_all = _L1_ffn_setup()
    _L1_ffn_in = {k: v for k, v in _L1_ffn_all.items() if k in ('Wg', 'Wu', 'Wd', 'Wr', 'Ag', 'Bg', 'Au', 'Bu', 'Ad', 'Bd')}
    del _L1_ffn_all
    return {'x': x, 'ctx_2048': ctx_2048, 'fside_S2_0': fside_S2_0, 'L0_attn_w_qkv': _L0_attn_in['w_qkv'], 'L0_attn_w_o': _L0_attn_in['w_o'], 'L0_xattn_ssm_kernel': _L0_xattn_in['ssm_kernel'], 'L0_xattn_D': _L0_xattn_in['D'], 'L0_ffn_gate': _L0_ffn_in['gate'], 'L0_ffn_gate_up_proj': _L0_ffn_in['gate_up_proj'], 'L0_ffn_down_proj': _L0_ffn_in['down_proj'], 'L1_attn_wq': _L1_attn_in['wq'], 'L1_attn_wk': _L1_attn_in['wk'], 'L1_attn_wv': _L1_attn_in['wv'], 'L1_attn_wo': _L1_attn_in['wo'], 'L1_xattn_k': _L1_xattn_in['k'], 'L1_ffn_Wg': _L1_ffn_in['Wg'], 'L1_ffn_Wu': _L1_ffn_in['Wu'], 'L1_ffn_Wd': _L1_ffn_in['Wd'], 'L1_ffn_Wr': _L1_ffn_in['Wr'], 'L1_ffn_Ag': _L1_ffn_in['Ag'], 'L1_ffn_Bg': _L1_ffn_in['Bg'], 'L1_ffn_Au': _L1_ffn_in['Au'], 'L1_ffn_Bu': _L1_ffn_in['Bu'], 'L1_ffn_Ad': _L1_ffn_in['Ad'], 'L1_ffn_Bd': _L1_ffn_in['Bd']}

def reference(x, ctx_2048, fside_S2_0, L0_attn_w_qkv, L0_attn_w_o, L0_xattn_ssm_kernel, L0_xattn_D, L0_ffn_gate, L0_ffn_gate_up_proj, L0_ffn_down_proj, L1_attn_wq, L1_attn_wk, L1_attn_wv, L1_attn_wo, L1_xattn_k, L1_ffn_Wg, L1_ffn_Wu, L1_ffn_Wd, L1_ffn_Wr, L1_ffn_Ag, L1_ffn_Bg, L1_ffn_Au, L1_ffn_Bu, L1_ffn_Ad, L1_ffn_Bd):
    import jax
    import jax.numpy as jnp

    def _L0_attn_ref(x, w_qkv, w_o):
        import jax, jax.numpy as jnp
        import numpy as np
        B, S, H_DIM = (2, 256, 256)
        N_HEADS, D_HEAD = (16, 128)
        b, s, _ = x.shape
        qkv = jnp.einsum('bsh,hf->bsf', x, w_qkv)
        qkv = qkv.reshape(b, s, 3, N_HEADS, D_HEAD)
        q, k, v = (qkv[:, :, 0], qkv[:, :, 1], qkv[:, :, 2])
        q = q.transpose(0, 2, 1, 3)
        k = k.transpose(0, 2, 1, 3)
        v = v.transpose(0, 2, 1, 3)
        scores = jnp.einsum('bhqd,bhkd->bhqk', q, k) / jnp.sqrt(jnp.float32(D_HEAD))
        probs = jax.nn.softmax(scores, axis=-1)
        values = jnp.einsum('bhqk,bhkd->bhkd', probs, v)
        values = values.transpose(0, 2, 1, 3).reshape(b, s, N_HEADS * D_HEAD)
        out = jnp.einsum('bsf,fh->bsh', values, w_o)
        return out

    def _L0_xattn_ref(k, v, q, ssm_kernel, D, head_dim):
        import jax, jax.numpy as jnp
        import numpy as np
        B, HD, L = k.shape
        H = HD // head_dim
        fft_size = 2 * L
        k_ = k.reshape(B, H, head_dim, L)
        v_ = v.reshape(B, H, head_dim, L)
        q_ = q.reshape(B, H, head_dim, L)
        kv = jnp.einsum('bhil,bhjl->bijhl', k_, v_)
        kv_f = jnp.fft.rfft(kv, n=fft_size)
        kernel_f = jnp.fft.rfft(ssm_kernel, n=fft_size)
        y = jnp.fft.irfft(kv_f * kernel_f, n=fft_size)[..., :L]
        out = y + kv * D[None, None, None, :, None]
        out = jnp.einsum('bijhl,bhil->bjhl', out, q_)
        out = jnp.transpose(out, (0, 2, 1, 3)).reshape(B, H * head_dim, L)
        return out.astype(k.dtype)

    def _L0_ffn_ref(hidden_states, gate, gate_up_proj, down_proj):
        import jax, jax.numpy as jnp
        import numpy as np
        NUM_EXPERTS = 32
        TOP_K = 4
        HIDDEN = 256
        INTER = 96
        batch_size = hidden_states.shape[0]
        x = hidden_states.reshape(-1, HIDDEN)
        num_tokens = x.shape[0]
        router_logits = jnp.einsum('TD,DE->TE', x, gate)
        routing_weights = jax.nn.softmax(router_logits.astype(jnp.float32), axis=-1)
        top_k_weights, top_k_indices = jax.lax.top_k(routing_weights, TOP_K)
        top_k_weights = top_k_weights / top_k_weights.sum(axis=-1, keepdims=True)
        top_k_weights = top_k_weights.astype(x.dtype)
        router_weights = jnp.zeros((num_tokens, NUM_EXPERTS), dtype=x.dtype)
        token_indices = jnp.broadcast_to(jnp.arange(num_tokens)[:, None], top_k_indices.shape)
        router_weights = router_weights.at[token_indices, top_k_indices].set(top_k_weights)
        gate_up = jnp.einsum('TD,EDF->TEF', x, gate_up_proj)
        g, u = jnp.split(gate_up, 2, axis=-1)
        gated = u * jax.nn.silu(g)
        next_states = jnp.einsum('TEF,EFD->TED', gated, down_proj)
        next_states = (next_states * router_weights[..., None]).sum(axis=1)
        return next_states.reshape(batch_size, -1, HIDDEN)

    def _L1_attn_ref(x, wq, wk, wv, wo):
        import jax, jax.numpy as jnp
        import numpy as np
        import math
        D = 256
        H = 32
        HKV = 8
        HD = D // H
        ROPE_BASE = 10000.0

        def _rope_cache(T, hd, base=ROPE_BASE):
            theta = 1.0 / base ** (jnp.arange(0, hd, 2, dtype=jnp.float32) / hd)
            t = jnp.arange(T, dtype=jnp.float32)
            freqs = t[:, None] * theta[None, :]
            return (jnp.cos(freqs), jnp.sin(freqs))

        def _apply_rope(x, cos, sin):
            B, Hh, T, hd = x.shape
            x_ = x.reshape(B, Hh, T, hd // 2, 2)
            x1, x2 = (x_[..., 0], x_[..., 1])
            c = cos[None, None, :, :]
            s = sin[None, None, :, :]
            rx1 = x1 * c - x2 * s
            rx2 = x1 * s + x2 * c
            return jnp.stack([rx1, rx2], axis=-1).reshape(B, Hh, T, hd)
        B, T, _ = x.shape
        q = (x @ wq.T).reshape(B, T, H, HD).transpose(0, 2, 1, 3)
        k = (x @ wk.T).reshape(B, T, HKV, HD).transpose(0, 2, 1, 3)
        v = (x @ wv.T).reshape(B, T, HKV, HD).transpose(0, 2, 1, 3)
        cos, sin = _rope_cache(T, HD)
        q = _apply_rope(q, cos, sin)
        k = _apply_rope(k, cos, sin)
        rep = H // HKV
        k = jnp.repeat(k, rep, axis=1)
        v = jnp.repeat(v, rep, axis=1)
        scores = jnp.einsum('bhtd,bhsd->bhts', q, k) / math.sqrt(HD)
        mask = jnp.triu(jnp.full((T, T), -jnp.inf, dtype=scores.dtype), k=1)
        scores = scores + mask[None, None, :, :]
        attn = jax.nn.softmax(scores, axis=-1)
        y = jnp.einsum('bhts,bhsd->bhtd', attn, v)
        y = y.transpose(0, 2, 1, 3).reshape(B, T, D)
        return y @ wo.T

    def _L1_xattn_ref(v, k, bias, x1, x2, num_heads):
        import jax, jax.numpy as jnp
        import numpy as np
        B, D, L = v.shape
        H = D // num_heads
        fft_size = 2 * L
        vr = v.reshape(B, H, num_heads, L)
        x1r = x1.reshape(B, H, num_heads, L)
        x2r = x2.reshape(B, H, num_heads, L)
        kv = vr[:, :, :, None, :] * x2r[:, :, None, :, :]
        k_f = jnp.fft.rfft(k.astype(jnp.float32), n=fft_size)
        y = jnp.fft.irfft(jnp.fft.rfft(kv, n=fft_size) * k_f[None, :, None, None, :], n=fft_size)[..., :L]
        skip = bias.astype(jnp.float32).reshape(H, num_heads)[None, :, :, None, None]
        y = y + kv * skip
        out = jnp.einsum('bhijl,bhil->bhjl', y, x1r)
        return out.reshape(B, D, L)

    def _L1_ffn_ref(x, Wg, Wu, Wd, Wr, Ag, Bg, Au, Bu, Ad, Bd):
        import jax, jax.numpy as jnp
        import numpy as np
        B, S, D = (4, 256, 256)
        DFF = 704
        E, K, R = (8, 2, 16)
        SCALING = 32.0 / 16.0
        b, s, d = x.shape
        xf = x.reshape(-1, d)
        gate_base = xf @ Wg.T
        up_base = xf @ Wu.T
        base_out = jax.nn.silu(gate_base) * up_base @ Wd.T
        router_logits = xf @ Wr.T
        probs = jax.nn.softmax(router_logits.astype(jnp.float32), axis=-1)
        topw, topi = jax.lax.top_k(probs, K)
        topw = topw.astype(x.dtype)
        expert_w = jnp.sum(jax.nn.one_hot(topi, E, dtype=x.dtype) * topw[..., None], axis=1)

        def expert_step(acc, params):
            Ag_e, Bg_e, Au_e, Bu_e, Ad_e, Bd_e, we = params
            g_lora = xf @ Ag_e.T @ Bg_e.T * SCALING
            u_lora = xf @ Au_e.T @ Bu_e.T * SCALING
            h = jax.nn.silu(gate_base + g_lora) * (up_base + u_lora)
            d_delta = h @ Ad_e.T @ Bd_e.T * SCALING
            return (acc + d_delta * we[:, None], None)
        acc0 = jnp.zeros_like(base_out)
        acc, _ = jax.lax.scan(expert_step, acc0, (Ag, Bg, Au, Bu, Ad, Bd, expert_w.T))
        return (base_out + acc).reshape(b, s, d)
    x = _layernorm(x + _L0_attn_ref(x, L0_attn_w_qkv, L0_attn_w_o), axis=-1)
    x = _layernorm(x + _L0_xattn_ref(ctx_2048, ctx_2048, x, L0_xattn_ssm_kernel, L0_xattn_D, 8), axis=-1)
    x = _layernorm(x + _L0_ffn_ref(x, L0_ffn_gate, L0_ffn_gate_up_proj, L0_ffn_down_proj), axis=-1)
    x = _layernorm(x + _L1_attn_ref(x, L1_attn_wq, L1_attn_wk, L1_attn_wv, L1_attn_wo), axis=-1)
    x = _layernorm(x + _L1_xattn_ref(x, L1_xattn_k, fside_S2_0, ctx_2048, ctx_2048, 8), axis=-1)
    x = _layernorm(x + _L1_ffn_ref(x, L1_ffn_Wg, L1_ffn_Wu, L1_ffn_Wd, L1_ffn_Wr, L1_ffn_Ag, L1_ffn_Bg, L1_ffn_Au, L1_ffn_Bu, L1_ffn_Ad, L1_ffn_Bd), axis=-1)
    return x

_drawn_inputs = setup_inputs


def setup_inputs(seed=0):
    import zlib

    import numpy as np

    out = dict(_drawn_inputs(seed))
    spreads = {}
    factors = {'L0_ffn_gate': 8.0,
     'L0_ffn_gate_up_proj': 8.0,
     'L0_ffn_down_proj': 8.0,
     'L1_attn_wq': 8.0,
     'L1_attn_wk': 8.0,
     'L1_ffn_Wr': 8.0,
     'L1_ffn_Ag': 8.0,
     'L1_ffn_Bg': 8.0,
     'L1_ffn_Au': 8.0,
     'L1_ffn_Bu': 8.0,
     'L1_ffn_Ad': 8.0,
     'L1_ffn_Bd': 8.0,
     'L1_ffn_Wd': 42.929}
    for name, (base, spread) in spreads.items():
        noise = np.random.default_rng([zlib.crc32(name.encode()), seed]).standard_normal(out[name].shape)
        drawn = base * np.exp(spread * noise) if base else spread * noise
        out[name] = jnp.asarray(drawn.astype(out[name].dtype))
    for name, factor in factors.items():
        out[name] = (out[name] * factor).astype(out[name].dtype)
    return out
```

```python
from contextlib import ExitStack

import concourse.bass as bass
from concourse import mybir

F32 = mybir.dt.float32
F32R = mybir.dt.float32r
BF16 = mybir.dt.bfloat16
U32 = mybir.dt.uint32
ALU = mybir.AluOpType
ACT = mybir.ActivationFunctionType
AX = mybir.AxisListType.X

P = 128
B, S, D = 8, 128, 256
DK = D // P
TOK = B * S
HALF = TOK // 2
EPS = 1e-5
NH, DH = 16, 128
CH, CI = 16, 8
NE0, TOP0, INTER = 32, 4, 96
NB0 = NE0 * INTER // P
NQ, NKV, HD = 32, 8, 8
REP = NQ // NKV
DFF, NE1, TOP1, RANK = 704, 8, 2, 16
FB = (DFF + P - 1) // P
SCALING = 2.0
MASKED = -1e30

A_WO = 3 * DK * P
C_DOWN = 2 * DK * P
F_BG = 2 * DK * P
F_BU = F_BG + P
F_WD = F_BU + P
F_AD = F_WD + D
F_COLS = F_AD + P
R_GATE, R_WR, R_AG, R_AU = 0, NE0, NE0 + NE1, NE0 + NE1 + P
R_COLS = R_AU + P
Q_W, Q_WS, K_W, K_WS, V_W, O_W = 0, D, 2 * D, 3 * D, 4 * D, 4 * D + NKV * HD
Q_COLS = O_W + D
C_ID, C_COS, C_SIN, C_CAUSAL, C_HQ, C_ROW = 0, P, 2 * P, 3 * P, 4 * P, 4 * P + REP
C_IOTA = C_ROW + NE1
CONST_COLS = C_IOTA + NE0


def count(value):
    return max(value, 0) if isinstance(value, int) else value


def settle(eng, sem):
    eng.sem_inc(sem, 1)


def two_at_a_time(eng, n, body):
    body(0, 0)
    body(1, 1)
    with eng.Fori(1, n // 2 - 1) as i:
        body(2 * i, 0)
        body(2 * i + 1, 1)
    body(n - 2, 0)
    body(n - 1, 1)


def decoder_layers(nc, x_nat, x_t, ctx_t, w_attn0, wo_attn0, toep0, skip0, w_res, w_moe, w_down0, sel3, w_attn1, toep1, bias1,
                   w_ffn1, w_bd, consts, out):
    with ExitStack() as ctx:
        def sb(name, shape, dt=F32):
            return ctx.enter_context(nc.sbuf_tensor(name, shape, dt))

        def sem(name):
            return ctx.enter_context(nc.semaphore(name))

        bank = ctx.enter_context(nc.psum_tensor("bank", [P, 8, 512], F32))

        xN = sb("xN", [P, B, D])
        rN = sb("rN", [P, B, D])
        xT = sb("xT", [P, DK, TOK])
        xTh = sb("xTh", [P, DK, TOK], F32R)
        xTl = sb("xTl", [P, DK, TOK], F32R)
        cT = sb("cT", [P, DK, B, S])
        cst = sb("cst", [P, CONST_COLS])
        wres = sb("wres", [P, DK, R_COLS])
        wq1 = sb("wq1", [P, DK, Q_COLS])
        bd = sb("bd", [P, D])
        ring = sb("ring", [P, 2, F_COLS])
        outring = sb("outring", [P, 2, D])
        ringh = sb("ringh", [P, 2, A_WO], F32R)
        ringl = sb("ringl", [P, 2, A_WO], F32R)
        st = sb("st", [P, B, 6])
        mv = sb("mv", [P, B, 2])
        ve = sb("ve", [P, B])
        sd = sb("sd", [P, B])
        rstd = sb("rstd", [P, B])
        ident = cst[:, C_ID:C_ID + P]
        arena = sb("arena", [P, 16384])
        cut = [0]

        def take(cols, fresh=False):
            if fresh:
                cut[0] = 0
            a = arena[:, cut[0]:cut[0] + cols]
            cut[0] += cols
            assert cut[0] <= 16384
            return a

        QT = take(2 * TOK, True).rearrange("p (s t) -> p s t", s=2)
        KT = take(2 * TOK).rearrange("p (s t) -> p s t", s=2)
        VT = take(2 * TOK).rearrange("p (s t) -> p s t", s=2)
        VTc = take(TOK)
        E = take(TOK)
        nmax = sb("nmax", [P, B])
        mx = sb("mx", [P, B])
        rowsum = sb("rowsum", [P, B])
        rinv = sb("rinv", [P, B])
        oT = take(2 * TOK, True).rearrange("p (l b s) -> p l b s", l=2, b=B)
        kv = take(4 * 512).rearrange("p (s m n) -> p s m n", s=2, m=2)
        prod = take(2 * 512).rearrange("p (s n) -> p s n", s=2)
        bx1 = take(2 * TOK).rearrange("p (l b s) -> p l b s", l=2, b=B)
        bx1v = take(2 * TOK).rearrange("p (l b s) -> p l b s", l=2, b=B)
        skr = take(2 * B * CH).rearrange("p (l n) -> p l n", l=2)
        toep = sb("toep", [P, 2, D])
        dskip = sb("dskip", [P, CH])
        bias_bc = sb("bias_bc", [P, S])
        SG = take(2 * 512, True).rearrange("p (s n) -> p s n", s=2)
        H1 = take(2 * 512).rearrange("p (s n) -> p s n", s=2)
        HT = take(2 * 512).rearrange("p (s n) -> p s n", s=2)
        e0 = take(B * NE0).rearrange("p (b e) -> p b e", b=B)
        rest = take(B * NE0).rearrange("p (b e) -> p b e", b=B)
        hit = take(B * NE0).rearrange("p (b e) -> p b e", b=B)
        rw = take(B * NE0).rearrange("p (b e) -> p b e", b=B)
        rwT = sb("rwT", [P, TOK], BF16)
        rw3 = sb("rw3", [P, B, 3, NE0], BF16)
        sel = sb("sel", [P, NB0 * P], BF16)
        selstage = take(NB0 * P)
        identb = sb("identb", [P, P], BF16)
        causalb = sb("causalb", [P, P], BF16)
        m1 = sb("m1", [P, B])
        r1 = sb("r1", [P, B])
        s1 = sb("s1", [P, B])
        top8 = sb("top8", [P, B, 8])
        idx8 = sb("idx8", [P, B, 8], U32)
        idxf = sb("idxf", [P, B, 8])
        we1 = sb("we1", [P, B, NE1])
        hit1 = sb("hit1", [P, B, NE1])
        rest1 = sb("rest1", [P, B, NE1])
        TC = take(4 * TOK, True).rearrange("p (w r b t) -> p w r b t", w=2, r=2, b=B)
        TS = take(4 * TOK).rearrange("p (w r b t) -> p w r b t", w=2, r=2, b=B)
        qb = take(2 * 2 * S).rearrange("p (s r t) -> p s r t", s=2, r=2)
        kb = take(2 * 2 * S).rearrange("p (s r t) -> p s r t", s=2, r=2)
        ke = take(2 * 2 * 512).rearrange("p (s r q t) -> p s r q t", s=2, r=2, q=REP)
        Pe = take(4 * 512).rearrange("p (s n) -> p s n", s=4)
        PT = take(2 * 512).rearrange("p (s n) -> p s n", s=2)
        mx1 = sb("mx1", [P, 4, REP])
        Vn = sb("Vn", [P, B, NKV, HD + 1])
        yr = sb("yr", [P, 2, NQ])
        yN = rN
        yT = TC[:, 0, :, :, :]
        aexp = take(2 * NE1 * TOK, True).rearrange("p (g e t) -> p g e t", g=2, e=NE1)
        SF = sb("SF", [P, 2, 512])
        HF = sb("HF", [P, 2, 512])

        x_in = sem("x_in")
        xt_in = sem("xt_in")
        const_in = sem("const_in")
        ctx_in = sem("ctx_in")
        wres_in = sem("wres_in")
        wq1_in = sem("wq1_in")
        bd_in = sem("bd_in")
        sel_in = sem("sel_in")
        skip0_in = sem("skip0_in")
        bias1_in = sem("bias1_in")
        x_split = sem("x_split")
        w_split = sem("w_split")
        proj_done = sem("proj_done")
        act_evac = sem("act_evac")
        dve_evac = sem("dve_evac")
        s_done = sem("s_done")
        mx_done = sem("mx_done")
        nmax_done = sem("nmax_done")
        exp_done = sem("exp_done")
        rinv_done = sem("rinv_done")
        csum_done = sem("csum_done")
        vc_done = sem("vc_done")
        out0_done = sem("out0_done")
        sum_done = sem("sum_done")
        ln_var = sem("ln_var")
        ln_sd = sem("ln_sd")
        ln_x = sem("ln_x")
        xt_psum = sem("xt_psum")
        xt_act = sem("xt_act")
        xt_hl = sem("xt_hl")
        toep_fix = sem("toep_fix")
        kv_done = sem("kv_done")
        conv_done = sem("conv_done")
        prod_done = sem("prod_done")
        osum_done = sem("osum_done")
        ot_psum = sem("ot_psum")
        bx1_done = sem("bx1_done")
        bx1v_done = sem("bx1v_done")
        skr_done = sem("skr_done")
        skip_add = sem("skip_add")
        logit_done = sem("logit_done")
        m_sub = sem("m_sub")
        e_exp = sem("e_exp")
        rw3_done = sem("rw3_done")
        rwt_psum = sem("rwt_psum")
        rwt_done = sem("rwt_done")
        g_done = sem("g_done")
        u_done = sem("u_done")
        r_done = sem("r_done")
        silu_done = sem("silu_done")
        gu_done = sem("gu_done")
        h_done = sem("h_done")
        down_done = sem("down_done")
        qkv_psum = sem("qkv_psum")
        rope_done = sem("rope_done")
        v_psum = sem("v_psum")
        v_copy = sem("v_copy")
        qk_ready = sem("qk_ready")
        kb_done = sem("kb_done")
        q_done = sem("q_done")
        sS = sem("sS")
        sM = sem("sM")
        sP = sem("sP")
        sE = sem("sE")
        sT = sem("sT")
        sV = sem("sV")
        sY = sem("sY")
        y_rec = sem("y_rec")
        yn = sem("yn")
        y_psum = sem("y_psum")
        yt_evac = sem("yt_evac")
        wo_done = sem("wo_done")
        l1_done = sem("l1_done")
        l1_sub = sem("l1_sub")
        l1_exp = sem("l1_exp")
        a_psum = sem("a_psum")
        a_evac = sem("a_evac")
        aexp_done = sem("aexp_done")
        fG = sem("fG")
        fU = sem("fU")
        f_silu = sem("f_silu")
        f_mul = sem("f_mul")
        f_down = sem("f_down")
        dw_done = sem("dw_done")
        dwt_psum = sem("dwt_psum")
        dwt_evac = sem("dwt_evac")
        bd_done = sem("bd_done")
        dve_chain = sem("dve_chain")
        out_done = sem("out_done")
        hi_done = sem("hi_done")
        const_conv = sem("const_conv")
        pool_settled = sem("pool_settled")
        sp_settled = sem("sp_settled")
        ring_in = [sem("ring_in0"), sem("ring_in1")]
        toep_in = [sem("toep_in0"), sem("toep_in1")]
        outring_in = [sem("outring_in0"), sem("outring_in1")]


        block = ctx.enter_context(nc.Block())

        @block.sync
        def _(sp):
            sp.dma_start(xT[:], x_t.rearrange("(k p) t -> p k t", p=P)).then_inc(xt_in, 16)

            def load_attn0(h, slot):
                sp.wait_ge(w_split, count(h - 1))
                settle(sp, sp_settled)
                sp.dma_start(ring[:, slot, 0:A_WO], w_attn0[h, :, :]).then_inc(ring_in[slot], 16)
                sp.wait_ge(out0_done, count(h - 1))
                settle(sp, sp_settled)
                sp.dma_start(outring[:, slot, :], wo_attn0[h, :, :]).then_inc(outring_in[slot], 16)

            load_attn0(0, 0)
            load_attn0(1, 1)
            sp.dma_start(xN[:], x_nat).then_inc(x_in, 16)
            sp.dma_start(cst[:], consts).then_inc(const_in, 16)
            sp.dma_start(cT[:], ctx_t.rearrange("(k p) b s -> p k b s", p=P)).then_inc(ctx_in, 16)
            sp.dma_start(wres[:], w_res).then_inc(wres_in, 16)
            sp.dma_start(wq1[:], w_attn1).then_inc(wq1_in, 16)
            sp.dma_start(bd[:], w_bd).then_inc(bd_in, 16)
            sp.dma_start(dskip[:], skip0.partition_broadcast(P)).then_inc(skip0_in, 16)
            sp.dma_start(bias_bc[:], bias1.partition_broadcast(P)).then_inc(bias1_in, 16)
            with sp.Fori(1, NH // 2) as i:
                load_attn0(2 * i, 0)
                load_attn0(2 * i + 1, 1)

            def load_toep(src, layer, h, slot):
                sp.wait_ge(conv_done, count(2 * (CH * layer + h - 1)))
                settle(sp, sp_settled)
                flat = src[h, :, :]
                sp.dma_start(toep[:, slot, :], flat).then_inc(toep_in[slot], 16)

            def load_moe(n, slot):
                sp.wait_ge(w_split, NH + n - 1)
                settle(sp, sp_settled)
                sp.dma_start(ring[:, slot, 0:C_DOWN], w_moe[n, :, :]).then_inc(ring_in[slot], 16)
                if isinstance(n, int) and n < 2:
                    sp.wait_ge(out0_done, NH + n - 1)
                else:
                    sp.wait_ge(down_done, 2 * (n - 1))
                settle(sp, sp_settled)
                sp.dma_start(outring[:, slot, :], w_down0[n, :, :]).then_inc(outring_in[slot], 16)

            def load_ffn1(f, slot):
                if isinstance(f, int) and f < 2:
                    sp.wait_ge(down_done, count(2 * (NB0 + f - 1)))
                    settle(sp, sp_settled)
                    sp.wait_ge(w_split, count(NH + NB0 + f - 1))
                    settle(sp, sp_settled)
                else:
                    sp.wait_ge(f_down, count(18 * (f - 1)))
                    settle(sp, sp_settled)
                sp.dma_start(ring[:, slot, :], w_ffn1[f, :, :]).then_inc(ring_in[slot], 16)

            load_toep(toep0, 0, 0, 0)
            load_toep(toep0, 0, 1, 1)
            load_moe(0, 0)
            load_moe(1, 1)
            with sp.Fori(1, CH // 2) as i:
                load_toep(toep0, 0, 2 * i, 0)
                load_toep(toep0, 0, 2 * i + 1, 1)
            sp.wait_ge(ot_psum, 4)
            sp.dma_start(selstage[0:3 * NE0, :], sel3).then_inc(sel_in, 16)
            load_toep(toep1, 1, 0, 0)
            load_toep(toep1, 1, 1, 1)
            with sp.Fori(1, NB0 // 2) as i:
                load_moe(2 * i, 0)
                load_moe(2 * i + 1, 1)
            load_ffn1(0, 0)
            load_ffn1(1, 1)
            with sp.Fori(1, CH // 2) as i:
                load_toep(toep1, 1, 2 * i, 0)
                load_toep(toep1, 1, 2 * i + 1, 1)
            with sp.Fori(1, FB // 2) as i:
                load_ffn1(2 * i, 0)
                load_ffn1(2 * i + 1, 1)
            sp.wait_ge(ln_x, 6 * B)
            sp.dma_start(out, xN[:]).then_inc(out_done, 16)
            sp.wait_ge(out_done, 16)

        @block.gpsimd
        def _(pool):
            def split_attn0(h, slot):
                pool.wait_ge(ring_in[slot], count(8 * (h - slot) + 16))
                pool.wait_ge(proj_done, count(6 * (h - 1)))
                settle(pool, pool_settled)
                pool.tensor_copy(ringh[:, slot, :], ring[:, slot, 0:A_WO]).then_inc(hi_done, 1)
                pool.wait_ge(hi_done, h + 1)
                pool.tensor_tensor(ringl[:, slot, :], ring[:, slot, 0:A_WO], ringh[:, slot, :].bitcast(F32),
                                   ALU.subtract).then_inc(w_split, 1)

            split_attn0(0, 0)
            split_attn0(1, 1)
            with pool.Fori(1, NH // 2) as i:
                split_attn0(2 * i, 0)
                split_attn0(2 * i + 1, 1)

            def split_moe(n, slot):
                pool.wait_ge(ring_in[slot], count(8 * (NH + n - slot) + 16))
                if isinstance(n, int) and n < 2:
                    pool.wait_ge(proj_done, 6 * NH)
                else:
                    pool.wait_ge(u_done, count(2 * (n - 1)))
                settle(pool, pool_settled)
                pool.tensor_copy(ringh[:, slot, 0:C_DOWN], ring[:, slot, 0:C_DOWN]).then_inc(hi_done, 1)
                pool.wait_ge(hi_done, NH + n + 1)
                pool.tensor_tensor(ringl[:, slot, 0:C_DOWN], ring[:, slot, 0:C_DOWN],
                                   ringh[:, slot, 0:C_DOWN].bitcast(F32), ALU.subtract).then_inc(w_split, 1)

            def conv_products(layer, h, slot, left, right):
                pool.wait_ge(conv_done, count(2 * (CH * layer + h - 1)))
                for m in range(DK):
                    a = left[:, m, :, bass.ds(CI * h, CI)].unsqueeze(3).broadcast_to([P, B, CI, CI])
                    c = right[:, m, :, bass.ds(CI * h, CI)].unsqueeze(2).broadcast_to([P, B, CI, CI])
                    o = kv[:, slot, m, :].rearrange("p (b i j) -> p b i j", b=B, i=CI)
                    pool.tensor_tensor(o, a, c, ALU.mult).then_inc(kv_done, 1)

            xTv = xT[:].rearrange("p k (b s) -> p k b s", b=B)
            pool.wait_ge(ctx_in, 16)
            pool.wait_ge(out0_done, NH)
            conv_products(0, 0, 0, cT, cT)
            conv_products(0, 1, 1, cT, cT)
            with pool.Fori(1, CH // 2) as i:
                conv_products(0, 2 * i, 0, cT, cT)
                conv_products(0, 2 * i + 1, 1, cT, cT)
            split_moe(0, 0)
            split_moe(1, 1)
            with pool.Fori(1, NB0 // 2) as i:
                split_moe(2 * i, 0)
                split_moe(2 * i + 1, 1)

            hq = cst[:, C_HQ:C_HQ + REP].unsqueeze(2).broadcast_to([P, REP, S])

            def spread(b, slot):
                pool.wait_ge(sS, count(NKV * (b - 1)))
                pool.tensor_tensor(kb[:, slot, :, :], TC[:, 1, :, b, :], TS[:, 1, :, b, :], ALU.add)\
                    .then_inc(kb_done, 1)
                pool.tensor_tensor(qb[:, slot, :, :], TC[:, 0, :, b, :], TS[:, 0, :, b, :], ALU.add)\
                    .then_inc(q_done, 1)
                pool.wait_ge(kb_done, b + 1)
                for r in range(2):
                    k1 = kb[:, slot, r, :].unsqueeze(1).broadcast_to([P, REP, S])
                    ins = pool.tensor_tensor(ke[:, slot, r, :, :], k1, hq, ALU.mult)
                ins.then_inc(qk_ready, 1)

            pool.wait_ge(rope_done, 16)
            spread(0, 0)
            spread(1, 1)
            with pool.Fori(1, B // 2) as i:
                spread(2 * i, 0)
                spread(2 * i + 1, 1)

            pool.wait_ge(wo_done, 4)
            pool.wait_ge(bias1_in, 16)
            bb = bias_bc[:].unsqueeze(1).broadcast_to([P, B, S])
            for m in range(DK):
                ins = pool.tensor_tensor(bx1[:, m, :, :], cT[:, m, :, :], bb, ALU.mult)
            ins.then_inc(bx1_done, 1)
            pool.wait_ge(xt_act, 16)
            pool.wait_ge(bx1_done, 1)
            conv_products(1, 0, 0, xTv, cT)
            conv_products(1, 1, 1, xTv, cT)
            for m in range(DK):
                ins = pool.tensor_tensor(bx1v[:, m, :, :], bx1[:, m, :, :], xTv[:, m, :, :], ALU.mult)
            ins.then_inc(bx1v_done, 1)
            with pool.Fori(1, CH // 2) as i:
                conv_products(1, 2 * i, 0, xTv, cT)
                conv_products(1, 2 * i + 1, 1, xTv, cT)
            pool.wait_ge(skr_done, 1)
            for m in range(DK):
                sk = skr[:, m, :].unsqueeze(2).broadcast_to([P, B * CH, CI])
                ins = pool.tensor_tensor(bx1[:, m, :, :].rearrange("p b (h j) -> p (b h) j", j=CI),
                                         cT[:, m, :, :].rearrange("p b (h j) -> p (b h) j", j=CI), sk, ALU.mult)
            ins.then_inc(skip_add, 1)

        @block.scalar
        def _(act):
            def evac_q(h, slot, j):
                act.wait_ge(proj_done, 6 * h + 1 + j)
                act.wait_ge(s_done, count(2 * (h - 1)))
                act.activation(QT[:, slot, j * HALF:(j + 1) * HALF], bank[:, j, :], ACT.Copy)\
                    .then_inc(act_evac, 1)

            def evac_v(h, slot, j):
                act.wait_ge(proj_done, 6 * h + 5 + j)
                act.wait_ge(vc_done, count(2 * (h - 1)))
                act.activation(VT[:, slot, j * HALF:(j + 1) * HALF], bank[:, j, :], ACT.Copy)\
                    .then_inc(act_evac, 1)

            def exps(h, j):
                act.wait_ge(nmax_done, 2 * h + j + 1)
                for b in range(4 * j, 4 * j + 4):
                    ins = act.activation(E[:, b * S:(b + 1) * S], bank[:, 2 + j, (b % 4) * S:(b % 4 + 1) * S], ACT.Exp,
                                         bias=nmax[:, b:b + 1], scale=DH ** -0.5, accum_out=rowsum[:, b:b + 1])
                ins.then_inc(exp_done, 1)

            def head(h, slot, last=False):
                if not last:
                    evac_q(h + 1, 1 - slot, 0)
                exps(h, 0)
                if not last:
                    evac_q(h + 1, 1 - slot, 1)
                exps(h, 1)
                if not last:
                    evac_v(h + 1, 1 - slot, 0)
                    evac_v(h + 1, 1 - slot, 1)

            for j in range(2):
                evac_q(0, 0, j)
            for j in range(2):
                evac_v(0, 0, j)
            head(0, 0)
            with act.Fori(0, (NH - 2) // 2) as i:
                head(2 * i + 1, 1)
                head(2 * i + 2, 0)
            head(NH - 1, 1, last=True)

            def norm_and_turn(layer_norm, turn=True):
                act.wait_ge(ln_var, layer_norm + 1)
                act.activation(sd[:], ve[:], ACT.Sqrt).then_inc(ln_sd, 1)
                if not turn:
                    return
                for n, (k, j) in enumerate(((0, 0), (1, 0), (0, 1), (1, 1))):
                    act.wait_ge(xt_psum, 4 * layer_norm + n + 1)
                    act.activation(xT[:, k, j * HALF:(j + 1) * HALF], bank[:, 2 * k + j, :], ACT.Copy)\
                        .then_inc(xt_act, 1)

            norm_and_turn(0)
            norm_and_turn(1)

            act.wait_ge(m_sub, 1)
            act.activation(e0, e0, ACT.Exp).then_inc(e_exp, 1)

            def silus(n, slot):
                for j in range(2):
                    s = 2 * n + j
                    act.wait_ge(g_done, s + 1)
                    act.wait_ge(gu_done, count(s - 1))
                    act.activation(SG[:, j, :], bank[:, 3 * j, :], ACT.Silu).then_inc(silu_done, 1)

            two_at_a_time(act, NB0, silus)
            norm_and_turn(2)

            def evac_pt(b, g):
                t = NKV * b + g
                act.wait_ge(sT, t + 1)
                act.wait_ge(sY, count(t - 1))
                act.activation(PT[:, g % 2, :], bank[:, 6 + g % 2, :], ACT.Copy).then_inc(sV, 1)

            def attn1(b, slot):
                for g in range(NKV):
                    t = NKV * b + g
                    act.wait_ge(sP, t + 1)
                    act.activation(Pe[:, g % 4, :], Pe[:, g % 4, :], ACT.Exp, scale=HD ** -0.5).then_inc(sE, 1)
                    if g > 1:
                        evac_pt(b, g - 2)
                    elif not isinstance(b, int) or b > 0:
                        evac_pt(b - 1, NKV - 2 + g)

            two_at_a_time(act, B, attn1)
            evac_pt(B - 1, NKV - 2)
            evac_pt(B - 1, NKV - 1)
            for n, (k, j) in enumerate(((0, 0), (1, 0), (0, 1), (1, 1))):
                act.wait_ge(y_psum, n + 1)
                act.activation(yT[:, k, 4 * j:4 * j + 4, :], bank[:, 2 * k + j, :].rearrange("p (b t) -> p b t", b=4),
                               ACT.Copy).then_inc(yt_evac, 1)
            norm_and_turn(3)
            norm_and_turn(4)
            act.wait_ge(l1_sub, 1)
            act.activation(we1[:], we1[:], ACT.Exp).then_inc(l1_exp, 1)

            def silus1(f, slot):
                for c in range(2):
                    for e in range(NE1 + 1):
                        k = 18 * f + 9 * c + e
                        act.wait_ge(fG, k + 1)
                        act.wait_ge(f_mul, count(k - 1))
                        act.activation(SF[:, (c + e) % 2, :], bank[:, 0, :], ACT.Silu).then_inc(f_silu, 1)

            two_at_a_time(act, FB, silus1)
            norm_and_turn(5, turn=False)

        @block.vector
        def _(dve):
            chained = [0]

            def link(ins):
                chained[0] += 1
                ins.then_inc(dve_chain, 1)
                dve.wait_ge(dve_chain, chained[0])

            dve.wait_ge(xt_in, 16)
            for k in range(DK):
                ins = dve.tensor_copy(xTh[:, k, :], xT[:, k, :])
            link(ins)
            for k in range(DK):
                ins = dve.tensor_tensor(xTl[:, k, :], xT[:, k, :], xTh[:, k, :].bitcast(F32), ALU.subtract)
            ins.then_inc(x_split, 1)
            dve.memset(Vn[:], 1.0).then_inc(v_copy, 1)

            def evac_k(h, slot, j):
                dve.wait_ge(proj_done, 6 * h + 3 + j)
                dve.wait_ge(s_done, count(2 * (h - 1)))
                dve.tensor_copy(KT[:, slot, j * HALF:(j + 1) * HALF], bank[:, j, :]).then_inc(dve_evac, 1)

            def row_max(h, j):
                dve.wait_ge(s_done, 2 * h + j + 1)
                dve.tensor_reduce(mx[:, 4 * j:4 * j + 4], bank[:, 2 + j, :].rearrange("p (b k) -> p b k", b=4),
                                  AX, ALU.max).then_inc(mx_done, 1)
                dve.wait_ge(mx_done, 2 * h + j + 1)
                dve.tensor_scalar(nmax[:, 4 * j:4 * j + 4], mx[:, 4 * j:4 * j + 4], -(DH ** -0.5), None, ALU.mult)\
                    .then_inc(nmax_done, 1)

            def recip(h, j):
                dve.wait_ge(exp_done, 2 * h + j + 1)
                dve.reciprocal(rinv[:, 4 * j:4 * j + 4], rowsum[:, 4 * j:4 * j + 4]).then_inc(rinv_done, 1)

            def scale_v(h, slot, j):
                dve.wait_ge(csum_done, 2 * h + j + 1)
                dve.wait_ge(act_evac, 4 * h + 3 + j)
                dve.tensor_tensor(VTc[:, j * HALF:(j + 1) * HALF], bank[:, 2 + j, :],
                                  VT[:, slot, j * HALF:(j + 1) * HALF], ALU.mult).then_inc(vc_done, 1)

            def head(h, slot, last=False):
                row_max(h, 0)
                row_max(h, 1)
                recip(h, 0)
                if not last:
                    evac_k(h + 1, 1 - slot, 0)
                recip(h, 1)
                scale_v(h, slot, 0)
                if not last:
                    evac_k(h + 1, 1 - slot, 1)
                scale_v(h, slot, 1)

            evac_k(0, 0, 0)
            evac_k(0, 0, 1)
            head(0, 0)
            with dve.Fori(0, (NH - 2) // 2) as i:
                head(2 * i + 1, 1)
                head(2 * i + 2, 0)
            head(NH - 1, 1, last=True)

            def norm(layer_norm, produced, steps, first_bank=4):
                if layer_norm == 0:
                    dve.wait_ge(x_in, 16)
                for q in range(4):
                    dve.wait_ge(produced, steps[q])
                    ins = dve.tensor_tensor(rN[:, 2 * q:2 * q + 2, :],
                                            bank[:, first_bank + q, :].rearrange("p (b d) -> p b d", b=2),
                                            xN[:, 2 * q:2 * q + 2, :], ALU.add)
                link(ins)
                for b in range(B):
                    ins = dve.bn_stats(st[:, b, :], rN[:, b, :])
                link(ins)
                for b in range(B):
                    ins = dve.bn_aggr(mv[:, b, :], st[:, b, :])
                link(ins)
                dve.tensor_scalar(ve[:], mv[:, :, 1], EPS, None, ALU.add).then_inc(ln_var, 1)
                dve.wait_ge(ln_sd, layer_norm + 1)
                link(dve.reciprocal(rstd[:], sd[:]))
                for b in range(B):
                    dve.tensor_scalar(xN[:, b, :], rN[:, b, :], mv[:, b, 0:1], rstd[:, b:b + 1],
                                      ALU.subtract, ALU.mult).then_inc(ln_x, 1)

            def split_x(layer_norm):
                for n, (k, j) in enumerate(((0, 0), (1, 0), (0, 1), (1, 1))):
                    dve.wait_ge(xt_act, 4 * layer_norm + n + 1)
                    half = slice(j * HALF, (j + 1) * HALF)
                    link(dve.tensor_copy(xTh[:, k, half], xT[:, k, half]))
                    dve.tensor_tensor(xTl[:, k, half], xT[:, k, half], xTh[:, k, half].bitcast(F32), ALU.subtract)\
                        .then_inc(xt_hl, 1)

            norm(0, out0_done, [NH] * 4)

            def conv_fix(layer, h, slot):
                dve.wait_ge(toep_in[slot], count(8 * (CH * layer + h - slot) + 16))
                dve.scalar_tensor_tensor(toep[:, slot, 0:P], ident, dskip[:, bass.ds(h, 1)], toep[:, slot, 0:P],
                                         ALU.mult, ALU.add).then_inc(toep_fix, 1)

            def conv_reduce(layer, h, slot, gate):
                for l in range(DK):
                    s = 2 * (CH * layer + h) + l
                    dve.wait_ge(conv_done, s + 1)
                    dve.wait_ge(osum_done, count(s - 1))
                    g = gate[:, l, :, bass.ds(CI * h, CI)].unsqueeze(3).broadcast_to([P, B, CI, CI])
                    dve.tensor_tensor(prod[:, l, :].rearrange("p (b j i) -> p b i j", b=B, j=CI),
                                      bank[:, 2 * slot + l, :].rearrange("p (b i j) -> p b i j", b=B, i=CI),
                                      g, ALU.mult).then_inc(prod_done, 1)
                for l in range(DK):
                    s = 2 * (CH * layer + h) + l
                    dve.wait_ge(prod_done, s + 1)
                    dve.tensor_reduce(oT[:, l, :, bass.ds(CI * h, CI)],
                                      prod[:, l, :].rearrange("p (b j i) -> p b j i", b=B, j=CI), AX, ALU.add)\
                        .then_inc(osum_done, 1)

            xTv = xT[:].rearrange("p k (b s) -> p k b s", b=B)
            dve.wait_ge(skip0_in, 16)
            conv_fix(0, 0, 0)
            conv_fix(0, 1, 1)
            dve.wait_ge(xt_act, 4)

            def conv0(h, slot):
                conv_reduce(0, h, slot, xTv)

            conv0(0, 0)
            conv0(1, 1)
            with dve.Fori(1, CH // 2) as i:
                conv_fix(0, 2 * i, 0)
                conv_fix(0, 2 * i + 1, 1)
                conv0(2 * i, 0)
                conv0(2 * i + 1, 1)
            norm(1, ot_psum, [1, 2, 3, 4])
            split_x(1)

            dve.wait_ge(sel_in, 16)
            dve.tensor_copy(sel[0:3 * NE0, :], selstage[0:3 * NE0, :]).then_inc(const_conv, 1)
            dve.tensor_copy(causalb[:], cst[:, C_CAUSAL:C_CAUSAL + P]).then_inc(const_conv, 1)
            link(dve.tensor_copy(identb[:], ident))

            def chosen(values, n, top, mask, scratch):
                for b in range(B):
                    ins = dve.max(top8[:, b, :], values[:, b, :])
                link(ins)
                for b in range(B):
                    ins = dve.max_index(idx8[:, b, :], top8[:, b, :], values[:, b, :])
                link(ins)
                link(dve.tensor_copy(idxf[:], idx8[:]))
                iota = cst[:, C_IOTA:C_IOTA + n].unsqueeze(1).broadcast_to([P, B, n])
                for r in range(top):
                    at = idxf[:, :, r:r + 1].broadcast_to([P, B, n])
                    link(dve.tensor_tensor(scratch if r else mask, iota, at, ALU.is_equal))
                    if r:
                        link(dve.tensor_tensor(mask, mask, scratch, ALU.add))

            dve.wait_ge(logit_done, 1)
            lg = bank[:, 0, 0:B * NE0].rearrange("p (b e) -> p b e", b=B)
            link(dve.tensor_reduce(m1[:], lg, AX, ALU.max))
            dve.tensor_tensor(e0, lg, m1[:].unsqueeze(2).broadcast_to([P, B, NE0]), ALU.subtract)\
                .then_inc(m_sub, 1)
            dve.wait_ge(e_exp, 1)
            chosen(e0, NE0, TOP0, hit, rest)
            link(dve.tensor_tensor(rw, hit, e0, ALU.mult))
            link(dve.tensor_reduce(s1[:], rw, AX, ALU.add))
            link(dve.reciprocal(r1[:], s1[:]))
            link(dve.tensor_tensor(rw, rw, r1[:].unsqueeze(2).broadcast_to([P, B, NE0]), ALU.mult))
            link(dve.tensor_copy(rw3[:, :, 0, :], rw))
            link(dve.tensor_tensor(rest, rw, rw3[:, :, 0, :], ALU.subtract))
            link(dve.tensor_copy(rw3[:, :, 1, :], rest))
            dve.tensor_tensor(rw3[:, :, 2, :], rest, rw3[:, :, 1, :], ALU.subtract).then_inc(rw3_done, 1)
            dve.wait_ge(rwt_psum, 1)
            dve.tensor_copy(rwT[0:3 * NE0, :], bank[0:3 * NE0, 1, :].bitcast(BF16)).then_inc(rwt_done, 1)

            def experts(n, slot):
                for j in range(2):
                    s = 2 * n + j
                    dve.wait_ge(silu_done, s + 1)
                    dve.wait_ge(u_done, s + 1)
                    dve.tensor_tensor(H1[:, j, :], bank[:, 1, :], SG[:, j, :], ALU.mult).then_inc(gu_done, 1)
                    dve.wait_ge(r_done, s + 1)
                    dve.wait_ge(down_done, count(s - 1))
                    dve.wait_ge(gu_done, s + 1)
                    dve.tensor_tensor(HT[:, j, :], bank[:, 2, :], H1[:, j, :], ALU.mult).then_inc(h_done, 1)

            two_at_a_time(dve, NB0, experts)
            norm(2, down_done, [2 * NB0] * 4)

            dve.wait_ge(wq1_in, 16)
            cos = cst[:, C_COS:C_COS + P].unsqueeze(1).broadcast_to([P, 4, S])
            sin = cst[:, C_SIN:C_SIN + P].unsqueeze(1).broadcast_to([P, 4, S])
            n = 0
            for w in range(2):
                for r in range(2):
                    for j in range(2):
                        for dst, table in ((TC, cos), (TS, sin)):
                            dve.wait_ge(qkv_psum, n + 1)
                            dve.tensor_tensor(dst[:, w, r, 4 * j:4 * j + 4, :],
                                              bank[:, n % 4, :].rearrange("p (b t) -> p b t", b=4),
                                              table, ALU.mult).then_inc(rope_done, 1)
                            n += 1
            dve.wait_ge(v_psum, 1)
            dve.wait_ge(v_copy, 1)
            dve.tensor_copy(Vn[:, :, :, 0:HD], bank[:, 6, :].rearrange("p (b g d) -> p b g d", b=B, g=NKV))\
                .then_inc(yn, 1)

            def norm_y(b, slot):
                dve.wait_ge(sY, NKV * b + NKV)
                y = bank[:, 4 + slot, 0:NQ * (HD + 1)].rearrange("p (h d) -> p h d", h=NQ)
                dve.reciprocal(yr[:, slot, :], y[:, :, HD]).then_inc(y_rec, 1)
                dve.wait_ge(y_rec, b + 1)
                dve.tensor_tensor(yN[:, b, :].rearrange("p (h d) -> p h d", h=NQ), y[:, :, 0:HD],
                                  yr[:, slot, :].unsqueeze(2).broadcast_to([P, NQ, HD]), ALU.mult)\
                    .then_inc(yn, 1)

            def attn1(b, slot):
                for g in range(NKV):
                    t = NKV * b + g
                    sc = bank[:, g % 4, :].rearrange("p (q s) -> p q s", q=REP)
                    dve.wait_ge(sS, t + 1)
                    dve.tensor_reduce(mx1[:, g % 4, :], sc, AX, ALU.max).then_inc(sM, 1)
                    dve.wait_ge(sM, t + 1)
                    dve.wait_ge(sT, count(t - 3))
                    dve.tensor_tensor(Pe[:, g % 4, :].rearrange("p (q s) -> p q s", q=REP), sc,
                                      mx1[:, g % 4, :].unsqueeze(2).broadcast_to([P, REP, S]), ALU.subtract)\
                        .then_inc(sP, 1)
                    if g == 5 and (not isinstance(b, int) or b > 0):
                        norm_y(b - 1, 1 - slot)

            two_at_a_time(dve, B, attn1)
            norm_y(B - 1, 1)
            norm(3, wo_done, [1, 2, 3, 4])

            dve.wait_ge(xt_act, 16)

            def conv1(h, slot):
                conv_reduce(1, h, slot, cT)

            conv1(0, 0)
            conv1(1, 1)
            dve.wait_ge(bx1v_done, 1)
            for m in range(DK):
                ins = dve.tensor_reduce(skr[:, m, :], bx1v[:, m, :, :].rearrange("p b (h i) -> p (b h) i", i=CI),
                                        AX, ALU.add)
            ins.then_inc(skr_done, 1)
            with dve.Fori(1, CH // 2) as i:
                conv1(2 * i, 0)
                conv1(2 * i + 1, 1)
            dve.wait_ge(skip_add, 1)
            dve.wait_ge(osum_done, 4 * CH)
            for m in range(DK):
                ins = dve.tensor_tensor(oT[:, m, :, :], oT[:, m, :, :], bx1[:, m, :, :], ALU.add)
            ins.then_inc(sum_done, 1)
            norm(4, ot_psum, [5, 6, 7, 8])

            dve.wait_ge(l1_done, 1)
            lg1 = bank[:, 4, 0:B * NE1].rearrange("p (b e) -> p b e", b=B)
            link(dve.tensor_reduce(m1[:], lg1, AX, ALU.max))
            dve.tensor_tensor(we1[:], lg1, m1[:].unsqueeze(2).broadcast_to([P, B, NE1]), ALU.subtract)\
                .then_inc(l1_sub, 1)
            for n in range(4):
                g, j = n // 2, n % 2
                dve.wait_ge(a_psum, n + 1)
                dve.tensor_copy(HF[:, j, :], bank[:, n, :]).then_inc(a_evac, 1)
                dve.wait_ge(a_evac, n + 1)
                for e in range(NE1):
                    ins = dve.tensor_scalar(aexp[:, g, e, j * HALF:(j + 1) * HALF], HF[:, j, :],
                                            cst[:, C_ROW + e:C_ROW + e + 1], None, ALU.mult)
            ins.then_inc(aexp_done, 1)
            dve.wait_ge(l1_exp, 1)
            link(dve.tensor_reduce(s1[:], we1[:], AX, ALU.add))
            link(dve.reciprocal(r1[:], s1[:]))
            link(dve.tensor_scalar(r1[:], r1[:], SCALING, None, ALU.mult))
            chosen(we1[:], NE1, TOP1, hit1[:], rest1[:])
            link(dve.tensor_tensor(we1[:], we1[:], hit1[:], ALU.mult))
            link(dve.tensor_tensor(we1[:], we1[:], r1[:].unsqueeze(2).broadcast_to([P, B, NE1]), ALU.mult))

            def gated(f, slot):
                for c in range(2):
                    for e in range(NE1 + 1):
                        k = 18 * f + 9 * c + e
                        dve.wait_ge(f_silu, k + 1)
                        dve.wait_ge(fU, k + 1)
                        dve.wait_ge(f_down, count(k - 1))
                        dve.tensor_tensor(HF[:, (c + e) % 2, :], bank[:, 1, :], SF[:, (c + e) % 2, :], ALU.mult)\
                            .then_inc(f_mul, 1)

            two_at_a_time(dve, FB, gated)
            dve.wait_ge(f_down, 18 * FB)
            for c in range(2):
                dve.tensor_tensor(rN[:, 2 * c:2 * c + 2, :].rearrange("p b (t e r) -> p (b t) e r", t=2, e=NE1),
                                  bank[:, 6 + c, :].rearrange("p (t e r) -> p t e r", t=4, e=NE1),
                                  we1[:, 4 * c:4 * c + 4, :].unsqueeze(3).broadcast_to([P, 4, NE1, RANK]),
                                  ALU.mult).then_inc(dw_done, 1)
            for c in range(2):
                dve.wait_ge(dwt_psum, c + 1)
                dve.tensor_copy(xT[:, 0, c * HALF:(c + 1) * HALF], bank[:, c, :]).then_inc(dwt_evac, 1)
            norm(5, bd_done, [1, 2, 3, 4], first_bank=2)

        @block.tensor
        def _(pe):
            halves = [slice(0, HALF), slice(HALF, TOK)]

            def split_product(o, slot, col, j):
                for k in range(DK):
                    wc = slice(col + k * P, col + (k + 1) * P)
                    pe.matmul(o, ringh[:, slot, wc], xTh[:, k, halves[j]], start=(k == 0), stop=False)
                    pe.matmul(o, ringh[:, slot, wc], xTl[:, k, halves[j]], start=False, stop=False)
                    ins = pe.matmul(o, ringl[:, slot, wc], xTh[:, k, halves[j]], start=False, stop=(k == DK - 1))
                return ins

            def project(h, slot, c):
                if c == 0:
                    pe.wait_ge(w_split, h + 1)
                if c < 4:
                    pe.wait_ge(act_evac, count(4 * h - 1 + c))
                else:
                    pe.wait_ge(dve_evac, count(2 * h + c - 3))
                split_product(bank[:, c % 2, :], slot, (c // 2) * DK * P, c % 2).then_inc(proj_done, 1)

            def scores(h, slot, j):
                pe.wait_ge(act_evac, 4 * h + 1 + j)
                pe.wait_ge(dve_evac, 2 * h + 1 + j)
                pe.wait_ge(vc_done, count(2 * h - 1 + j))
                for b in range(4 * j, 4 * j + 4):
                    t = slice(b * S, (b + 1) * S)
                    ins = pe.matmul(bank[:, 2 + j, (b % 4) * S:(b % 4 + 1) * S], QT[:, slot, t], KT[:, slot, t],
                                    start=True, stop=True)
                ins.then_inc(s_done, 1)

            def key_weights(h, j):
                pe.wait_ge(rinv_done, 2 * h + j + 1)
                for b in range(4 * j, 4 * j + 4):
                    ins = pe.matmul(bank[:, 2 + j, (b % 4) * S:(b % 4 + 1) * S],
                                    rinv[:, b:b + 1].broadcast_to([P, P]), E[:, b * S:(b + 1) * S],
                                    start=True, stop=True)
                ins.then_inc(csum_done, 1)

            def attn_out(h, slot):
                pe.wait_ge(outring_in[slot], 8 * (h - slot) + 16)
                for b in range(B):
                    if b % 4 == 0:
                        pe.wait_ge(vc_done, 2 * h + b // 4 + 1)
                    ins = pe.matmul(bank[:, 4 + b // 2, (b % 2) * D:(b % 2 + 1) * D], VTc[:, b * S:(b + 1) * S],
                                    outring[:, slot, :],
                                    start=(isinstance(h, int) and h == 0 and b % 2 == 0),
                                    stop=(isinstance(h, int) and h == NH - 1), skip_group_check=True)
                ins.then_inc(out0_done, 1)

            def head(h, slot, last=False):
                def ahead(c):
                    if not last:
                        project(h + 1, 1 - slot, c)
                scores(h, slot, 0)
                ahead(0)
                scores(h, slot, 1)
                ahead(1)
                ahead(2)
                key_weights(h, 0)
                ahead(3)
                key_weights(h, 1)
                ahead(4)
                ahead(5)
                attn_out(h, slot)

            pe.wait_ge(x_split, 1)
            for c in range(6):
                project(0, 0, c)
            head(0, 0)
            with pe.Fori(0, (NH - 2) // 2) as i:
                head(2 * i + 1, 1)
                head(2 * i + 2, 0)
            head(NH - 1, 1, last=True)

            def turn(layer_norm):
                for b in range(B):
                    pe.wait_ge(ln_x, B * layer_norm + b + 1)
                    for k in range(DK):
                        ins = pe.transpose(bank[:, 2 * k + b // 4, (b % 4) * S:(b % 4 + 1) * S],
                                           xN[:, b, k * P:(k + 1) * P], ident)
                        if b % 4 == 3:
                            ins.then_inc(xt_psum, 1)

            pe.wait_ge(const_in, 16)
            turn(0)

            def conv(layer, h, slot):
                n = CH * layer + h
                if layer == 0:
                    pe.wait_ge(toep_fix, h + 1)
                else:
                    pe.wait_ge(toep_in[slot], count(8 * (n - slot) + 16))
                pe.wait_ge(kv_done, 2 * n + 1)
                pe.wait_ge(prod_done, count(2 * n - 2))
                diag, off = toep[:, slot, 0:P], toep[:, slot, P:D]
                pe.matmul(bank[:, 2 * slot, :], diag, kv[:, slot, 0, :], start=True, stop=True)\
                    .then_inc(conv_done, 1)
                pe.matmul(bank[:, 2 * slot + 1, :], off, kv[:, slot, 0, :], start=True, stop=False)
                pe.wait_ge(kv_done, 2 * n + 2)
                pe.matmul(bank[:, 2 * slot + 1, :], diag, kv[:, slot, 1, :], start=False, stop=True)\
                    .then_inc(conv_done, 1)

            def turn_back():
                for b in range(B):
                    for l in range(DK):
                        ins = pe.transpose(bank[:, 4 + b // 2, (b % 2) * D + l * P:(b % 2) * D + (l + 1) * P],
                                           oT[:, l, b, :], ident)
                    if b % 2 == 1:
                        ins.then_inc(ot_psum, 1)

            def conv_layer(layer):
                conv(layer, 0, 0)
                conv(layer, 1, 1)
                with pe.Fori(1, CH // 2) as i:
                    conv(layer, 2 * i, 0)
                    conv(layer, 2 * i + 1, 1)

            pe.wait_ge(xt_act, 4)
            conv_layer(0)
            pe.wait_ge(osum_done, 2 * CH)
            turn_back()
            turn(1)

            pe.wait_ge(wres_in, 16)
            pe.wait_ge(xt_act, 8)
            for b in range(B):
                for k in range(DK):
                    ins = pe.matmul(bank[:, 0, b * NE0:(b + 1) * NE0], xT[:, k, b * S:(b + 1) * S],
                                    wres[:, k, R_GATE:R_GATE + NE0], start=(k == 0), stop=(k == DK - 1))
            ins.then_inc(logit_done, 1)
            pe.wait_ge(rw3_done, 1)
            rwt = bank[0:3 * NE0, 1, :].bitcast(BF16)
            for b in range(B):
                ins = pe.transpose(rwt[:, b * S:(b + 1) * S], rw3[:, b, :, :].rearrange("p c e -> p (c e)"),
                                   identb[:])
            ins.then_inc(rwt_psum, 1)

            def down(n, slot, j):
                s = 2 * n + j
                if j == 0:
                    pe.wait_ge(outring_in[slot], 8 * (NH + n - slot) + 16)
                pe.wait_ge(h_done, s + 1)
                for b in range(4 * j, 4 * j + 4):
                    ins = pe.matmul(bank[:, 4 + b // 2, (b % 2) * D:(b % 2 + 1) * D],
                                    HT[:, j, (b % 4) * S:(b % 4 + 1) * S], outring[:, slot, :],
                                    start=(isinstance(n, int) and n == 0 and b % 2 == 0),
                                    stop=(isinstance(n, int) and n == NB0 - 1), skip_group_check=True)
                ins.then_inc(down_done, 1)

            def experts(n, slot):
                pe.wait_ge(w_split, NH + n + 1)
                for j in range(2):
                    s = 2 * n + j
                    pe.wait_ge(silu_done, count(s - 1))
                    split_product(bank[:, 3 * j, :], slot, 0, j).then_inc(g_done, 1)
                    pe.wait_ge(gu_done, s)
                    split_product(bank[:, 1, :], slot, DK * P, j).then_inc(u_done, 1)
                    pe.wait_ge(h_done, s)
                    pe.matmul(bank[:, 2, :], sel[0:3 * NE0, bass.ds(n * P, P)], rwT[0:3 * NE0, halves[j]],
                              start=True, stop=True).then_inc(r_done, 1)
                    if j == 1:
                        down(n, slot, 0)
                    elif not isinstance(n, int) or n > 0:
                        down(n - 1, 1 - slot, 1)

            pe.wait_ge(rwt_done, 1)
            pe.wait_ge(xt_hl, 4)
            two_at_a_time(pe, NB0, experts)
            down(NB0 - 1, 1, 1)
            turn(2)

            pe.wait_ge(wq1_in, 16)
            pe.wait_ge(xt_act, 12)
            n = 0
            for w in range(2):
                for r in range(2):
                    for j in range(2):
                        for col in ((Q_W, Q_WS), (K_W, K_WS))[w]:
                            pe.wait_ge(rope_done, count(n - 3))
                            for k in range(DK):
                                ins = pe.matmul(bank[:, n % 4, :], wq1[:, k, col + r * P:col + (r + 1) * P],
                                                xT[:, k, halves[j]], start=(k == 0), stop=(k == DK - 1))
                            ins.then_inc(qkv_psum, 1)
                            n += 1
            for b in range(B):
                for k in range(DK):
                    ins = pe.matmul(bank[:, 6, b * NKV * HD:(b + 1) * NKV * HD], xT[:, k, b * S:(b + 1) * S],
                                    wq1[:, k, V_W:V_W + NKV * HD], start=(k == 0), stop=(k == DK - 1))
            ins.then_inc(v_psum, 1)
            pe.wait_ge(v_copy, 1)
            pe.wait_ge(yn, 1)
            causal4 = causalb[:].unsqueeze(1).broadcast_to([P, REP, S])

            def scores1(b, slot, g):
                t = NKV * b + g
                if g == 0:
                    pe.wait_ge(qk_ready, b + 1)
                pe.wait_ge(sP, count(t - 3))
                rows = slice(32 * (g % 4), 32 * (g % 4) + 32)
                o = bank[:, g % 4, :]
                pe.matmul(o, qb[rows, slot, g // 4, :], ke[rows, slot, g // 4, :, :].rearrange("p q t -> p (q t)"),
                          start=True, stop=False)
                pe.matmul(o.rearrange("p (q s) -> p q s", q=REP), identb[:], causal4, start=False, stop=True)\
                    .then_inc(sS, 1)

            def turn_probs(b, slot, g):
                t = NKV * b + g
                pe.wait_ge(sE, t + 1)
                pe.wait_ge(sV, count(t - 1))
                for q in range(REP):
                    ins = pe.transpose(bank[:, 6 + g % 2, q * S:(q + 1) * S], Pe[:, g % 4, q * S:(q + 1) * S], ident)
                ins.then_inc(sT, 1)

            def weigh(b, slot, g):
                t = NKV * b + g
                pe.wait_ge(sV, t + 1)
                if g == 0:
                    pe.wait_ge(yn, b)
                for q in range(REP):
                    c = (REP * g + q) * (HD + 1)
                    ins = pe.matmul(bank[:, 4 + slot, c:c + HD + 1], PT[:, g % 2, q * S:(q + 1) * S],
                                    Vn[:, b, g, :], start=(g == 0 and q == 0), stop=(g == NKV - 1 and q == REP - 1),
                                    skip_group_check=True)
                ins.then_inc(sY, 1)

            def earlier(step, b, slot, g, back):
                if g >= back:
                    step(b, slot, g - back)
                elif not isinstance(b, int) or b > 0:
                    step(b - 1, 1 - slot, g - back + NKV)

            def attn1(b, slot):
                for g in range(NKV):
                    scores1(b, slot, g)
                    earlier(turn_probs, b, slot, g, 2)
                    earlier(weigh, b, slot, g, 3)

            two_at_a_time(pe, B, attn1)
            turn_probs(B - 1, 1, NKV - 2)
            weigh(B - 1, 1, NKV - 3)
            turn_probs(B - 1, 1, NKV - 1)
            weigh(B - 1, 1, NKV - 2)
            weigh(B - 1, 1, NKV - 1)
            for b in range(B):
                pe.wait_ge(yn, b + 2)
                for k in range(DK):
                    ins = pe.transpose(bank[:, 2 * k + b // 4, (b % 4) * S:(b % 4 + 1) * S],
                                       yN[:, b, k * P:(k + 1) * P], ident)
                    if b % 4 == 3:
                        ins.then_inc(y_psum, 1)
            for b in range(B):
                pe.wait_ge(yt_evac, 2 + 2 * (b // 4))
                for k in range(DK):
                    ins = pe.matmul(bank[:, 4 + b // 2, (b % 2) * D:(b % 2 + 1) * D], yT[:, k, b, :],
                                    wq1[:, k, O_W:O_W + D], start=(k == 0), stop=(k == DK - 1))
                if b % 2 == 1:
                    ins.then_inc(wo_done, 1)
            turn(3)

            pe.wait_ge(xt_act, 16)
            conv_layer(1)
            pe.wait_ge(sum_done, 1)
            turn_back()
            turn(4)

            pe.wait_ge(xt_act, 20)
            for b in range(B):
                for k in range(DK):
                    ins = pe.matmul(bank[:, 4, b * NE1:(b + 1) * NE1], xT[:, k, b * S:(b + 1) * S],
                                    wres[:, k, R_WR:R_WR + NE1], start=(k == 0), stop=(k == DK - 1))
            ins.then_inc(l1_done, 1)
            for n in range(4):
                col = (R_AG, R_AU)[n // 2]
                for k in range(DK):
                    ins = pe.matmul(bank[:, n, :], wres[:, k, col:col + P], xT[:, k, halves[n % 2]],
                                    start=(k == 0), stop=(k == DK - 1))
                ins.then_inc(a_psum, 1)
            pe.wait_ge(a_evac, 4)
            pe.wait_ge(l1_sub, 1)

            def down1(f, slot, c, e):
                pe.wait_ge(f_mul, 18 * f + 9 * c + e + 1)
                for b in range(4 * c, 4 * c + 4):
                    hs = HF[:, (c + e) % 2, (b % 4) * S:(b % 4 + 1) * S]
                    first = isinstance(f, int) and f == 0
                    if e == 0:
                        ins = pe.matmul(bank[:, 2 + b // 2, (b % 2) * D:(b % 2 + 1) * D], hs,
                                        ring[:, slot, F_WD:F_WD + D], start=(first and b % 2 == 0), stop=False,
                                        skip_group_check=True)
                    else:
                        col = (b % 4) * P + (e - 1) * RANK
                        w = F_AD + (e - 1) * RANK
                        ins = pe.matmul(bank[:, 6 + c, col:col + RANK], hs, ring[:, slot, w:w + RANK],
                                        start=(first and e == 1 and b % 4 == 0),
                                        stop=(isinstance(f, int) and f == FB - 1), skip_group_check=True)
                ins.then_inc(f_down, 1)

            def before(f, slot, c, e):
                if e > 0:
                    return f, slot, c, e - 1
                if c > 0:
                    return f, slot, 0, NE1
                return None if isinstance(f, int) and f == 0 else (f - 1, 1 - slot, 1, NE1)

            def ffn1(f, slot):
                pe.wait_ge(ring_in[slot], count(8 * (NH + NB0 + f - slot) + 16))
                for c in range(2):
                    for e in range(NE1 + 1):
                        k = 18 * f + 9 * c + e
                        pe.wait_ge(f_silu, k)
                        for g, done, low in ((0, fG, F_BG), (1, fU, F_BU)):
                            if g == 1:
                                pe.wait_ge(f_mul, k)
                            if e == 0:
                                for d in range(DK):
                                    w = (DK * g + d) * P
                                    ins = pe.matmul(bank[:, g, :], ring[:, slot, w:w + P], xT[:, d, halves[c]],
                                                    start=(d == 0), stop=(d == DK - 1), skip_group_check=True)
                            else:
                                ins = pe.matmul(bank[:, g, :], ring[:, slot, low:low + P],
                                                aexp[:, g, e - 1, halves[c]], start=False, stop=True,
                                                skip_group_check=True)
                            ins.then_inc(done, 1)
                        last = before(f, slot, c, e)
                        if last:
                            down1(*last)

            pe.wait_ge(aexp_done, 1)
            two_at_a_time(pe, FB, ffn1)
            down1(FB - 1, 1, 1, NE1)
            for c in range(2):
                pe.wait_ge(dw_done, c + 1)
                dw = rN[:, 2 * c:2 * c + 2, :].rearrange("p a d -> p (a d)")
                for t in range(4):
                    ins = pe.transpose(bank[:, c, t * P:(t + 1) * P], dw[:, t * P:(t + 1) * P], ident)
                ins.then_inc(dwt_psum, 1)
            pe.wait_ge(bd_in, 16)
            for b in range(B):
                pe.wait_ge(dwt_evac, b // 4 + 1)
                ins = pe.matmul(bank[:, 2 + b // 2, (b % 2) * D:(b % 2 + 1) * D], xT[:, 0, b * S:(b + 1) * S], bd[:],
                                start=False, stop=True, skip_group_check=True)
                if b % 2 == 1:
                    ins.then_inc(bd_done, 1)


def kernel(**inputs):
    import numpy as np
    import concourse.bacc as bacc
    from concourse.bass_utils import run_bass_kernel_spmd

    a = {k: np.asarray(v) for k, v in inputs.items()}

    def blocks(w, n):
        return w.reshape(DK, P, n).transpose(1, 0, 2)

    def toeplitz(k):
        padded = np.zeros((CH, P - 1 + D), np.float32)
        padded[:, P - 1:] = k
        at = P - 1 - np.arange(P)[:, None] + np.arange(D)[None, :]
        return padded[:, at]

    w_attn0 = a["L0_attn_w_qkv"].reshape(DK, P, 3, NH, DH).transpose(3, 1, 2, 0, 4).reshape(NH, P, A_WO)

    gu = a["L0_ffn_gate_up_proj"].reshape(NE0, D, 2, INTER).transpose(2, 1, 0, 3).reshape(2, DK, P, NB0, P)
    w_moe = gu.transpose(3, 2, 0, 1, 4).reshape(NB0, P, C_DOWN)

    swap = np.arange(D) ^ 1
    wq, wo = a["L1_attn_wq"], a["L1_attn_wo"]
    wk = np.repeat(a["L1_attn_wk"].reshape(NKV, 1, HD, D), REP, axis=1).reshape(D, D)
    w_attn1 = np.concatenate([blocks(m.T, m.shape[0]) for m in (wq, wq[swap], wk, wk[swap], a["L1_attn_wv"], wo)],
                             axis=2)
    w_res = np.concatenate([blocks(a["L0_ffn_gate"], NE0), blocks(a["L1_ffn_Wr"].T, NE1),
                            blocks(a["L1_ffn_Ag"].reshape(P, D).T, P), blocks(a["L1_ffn_Au"].reshape(P, D).T, P)],
                           axis=2)

    def padded(m):
        z = np.zeros((FB * P, m.shape[1]), np.float32)
        z[:DFF] = m
        return z.reshape(FB, P, m.shape[1])

    def stationary(m):
        return padded(m).reshape(FB, P, DK, P).transpose(0, 3, 2, 1).reshape(FB, P, DK * P)

    low_up = [padded(a[k].transpose(1, 0, 2).reshape(DFF, P)).transpose(0, 2, 1) for k in ("L1_ffn_Bg", "L1_ffn_Bu")]
    w_ffn1 = np.concatenate([stationary(a["L1_ffn_Wg"]), stationary(a["L1_ffn_Wu"]), *low_up,
                             padded(a["L1_ffn_Wd"].T), padded(a["L1_ffn_Ad"].reshape(P, DFF).T)], axis=2)
    w_bd = a["L1_ffn_Bd"].transpose(0, 2, 1).reshape(P, D)

    consts = np.zeros((P, CONST_COLS), np.float32)
    consts[:, C_ID:C_ID + P] = np.eye(P)
    theta = np.float32(1.0) / np.float32(10000.0) ** (np.arange(0, HD, 2, dtype=np.float32) / np.float32(HD))
    freqs = np.arange(S, dtype=np.float32)[None, :] * theta[(np.arange(P) % HD) // 2][:, None]
    consts[:, C_COS:C_COS + P] = np.cos(freqs)
    consts[:, C_SIN:C_SIN + P] = np.sin(freqs) * np.where(np.arange(P) % 2 == 0, -1, 1)[:, None]
    consts[:, C_CAUSAL:C_CAUSAL + P] = np.where(np.arange(P)[None, :] > np.arange(P)[:, None], MASKED, 0)
    consts[:, C_HQ:C_HQ + REP] = (np.arange(P) % 32 // HD)[:, None] == np.arange(REP)[None, :]
    expert = (np.arange(P) // RANK)[:, None]
    consts[:, C_ROW:C_ROW + NE1] = SCALING * (expert == np.arange(NE1)) - SCALING * (expert == np.arange(NE1) - 1)
    consts[:, C_IOTA:C_IOTA + NE0] = np.arange(NE0)
    sel3 = np.tile((np.arange(NE0)[:, None] == np.arange(NB0 * P)[None, :] // INTER).astype(np.float32), (3, 1))

    arrays = {
        "x_nat": a["x"].transpose(1, 0, 2), "x_t": a["x"].reshape(TOK, D).T,
        "ctx_t": a["ctx_2048"].transpose(2, 0, 1), "w_attn0": w_attn0,
        "wo_attn0": a["L0_attn_w_o"].reshape(NH, DH, D),
        "toep0": toeplitz(a["L0_xattn_ssm_kernel"]), "skip0": a["L0_xattn_D"],
        "w_res": w_res, "w_moe": w_moe, "w_down0": a["L0_ffn_down_proj"].reshape(NB0, P, D), "sel3": sel3, "w_attn1": w_attn1,
        "toep1": toeplitz(a["L1_xattn_k"]), "bias1": a["fside_S2_0"], "w_ffn1": w_ffn1, "w_bd": w_bd,
        "consts": consts,
    }
    arrays = {k: np.ascontiguousarray(v) for k, v in arrays.items()}
    nc = bacc.Bacc("TRN2", target_bir_lowering=False, num_devices=1)
    args = [nc.dram_tensor(k, v.shape, mybir.dt.from_np(v.dtype), kind="ExternalInput").ap() for k, v in arrays.items()]
    out = nc.dram_tensor("out", (P, B, D), F32, kind="ExternalOutput").ap()
    decoder_layers(nc, *args, out)
    result = run_bass_kernel_spmd(nc, [arrays], core_ids=[0])
    return np.ascontiguousarray(result.results[0]["out"].transpose(1, 0, 2))
```

```python
from contextlib import ExitStack

import concourse.bass as bass
from concourse import mybir

F32 = mybir.dt.float32
F32R = mybir.dt.float32r
BF16 = mybir.dt.bfloat16
U32 = mybir.dt.uint32
ALU = mybir.AluOpType
ACT = mybir.ActivationFunctionType
AX = mybir.AxisListType.X

P = 128
B, S, D = 8, 128, 256
DK = D // P
TOK = B * S
HALF = TOK // 2
EPS = 1e-5
NH, DH = 16, 128
CH, CI = 16, 8
NE0, TOP0, INTER = 32, 4, 96
NB0 = NE0 * INTER // P
NQ, NKV, HD = 32, 8, 8
REP = NQ // NKV
DFF, NE1, TOP1, RANK = 704, 8, 2, 16
FB = (DFF + P - 1) // P
SCALING = 2.0
MASKED = -1e30

A_WO = 3 * DK * P
C_DOWN = 2 * DK * P
F_BASE = 2 * DK * P
F_WD = F_BASE
F_AD = F_WD + D
F_COLS = F_AD + P
LOW = 2 * NE1 * P
R_GATE, R_WR, R_AG, R_AU = 0, NE0, NE0 + NE1, NE0 + NE1 + P
R_COLS = R_AU + P
Q_W, Q_WS, K_W, K_WS, V_W, O_W = 0, D, 2 * D, 3 * D, 4 * D, 4 * D + NKV * HD
Q_COLS = O_W + D
C_ID, C_COS, C_SIN, C_CAUSAL, C_HQ = 0, P, 2 * P, 3 * P, 4 * P
C_GROUP = C_HQ + REP
C_IOTA = C_GROUP + NKV // 2
CONST_COLS = C_IOTA + NE0


def count(value):
    return max(value, 0) if isinstance(value, int) else value


def settle(eng, sem):
    eng.sem_inc(sem, 1)


def two_at_a_time(eng, n, body):
    body(0, 0)
    body(1, 1)
    with eng.Fori(1, n // 2 - 1) as i:
        body(2 * i, 0)
        body(2 * i + 1, 1)
    body(n - 2, 0)
    body(n - 1, 1)


def decoder_layers(nc, x_nat, x_t, ctx_t, w_attn0, wo_attn0, toep0, skip0, w_res, w_moe, w_down0, sel3, w_attn1, toep1, bias1,
                   w_ffn1, w_low, sel_low, w_bd, consts, out):
    with ExitStack() as ctx:
        def sb(name, shape, dt=F32):
            return ctx.enter_context(nc.sbuf_tensor(name, shape, dt))

        def sem(name):
            return ctx.enter_context(nc.semaphore(name))

        bank = ctx.enter_context(nc.psum_tensor("bank", [P, 8, 512], F32))

        xN = sb("xN", [P, B, D])
        rN = sb("rN", [P, B, D])
        xT = sb("xT", [P, DK, TOK])
        xTh = sb("xTh", [P, DK, TOK], F32R)
        xTl = sb("xTl", [P, DK, TOK], F32R)
        cst = sb("cst", [P, CONST_COLS])
        wres = sb("wres", [P, DK, R_COLS])
        bd = sb("bd", [P, D])
        ring = sb("ring", [P, 2, F_COLS])
        outring = sb("outring", [P, 2, D])
        ringh = sb("ringh", [P, 2, A_WO], F32R)
        ringl = sb("ringl", [P, 2, A_WO], F32R)
        st = sb("st", [P, B, 6])
        mv = sb("mv", [P, B, 2])
        ve = sb("ve", [P, B])
        sd = sb("sd", [P, B])
        rstd = sb("rstd", [P, B])
        ident = cst[:, C_ID:C_ID + P]
        lowraw = sb("lowraw", [P, 2, LOW])
        SF = sb("SF", [P, 2, 512])
        HF = sb("HF", [P, 2, 512])

        m1 = sb("m1", [P, B])
        r1 = sb("r1", [P, B])
        s1 = sb("s1", [P, B])
        top8 = sb("top8", [P, B, 8])
        idx8 = sb("idx8", [P, B, 8], U32)
        idxf = sb("idxf", [P, B, 8])
        we1 = sb("we1", [P, B, NE1])
        hit1 = sb("hit1", [P, B, NE1])
        rest1 = sb("rest1", [P, B, NE1])

        wrep = rN[:, 0:B // 2, :].rearrange("p n (c r) -> p (n c) r", r=RANK)
        with ExitStack() as last_stage:
            def sb_last(name, shape, dt=F32):
                return last_stage.enter_context(nc.sbuf_tensor(name, shape, dt))
            astk = sb_last("astk", [P, 2, NE1, TOK], F32R)
            bstk = sb_last("bstk", [P, 2, LOW], F32R)
            ahl = sb_last("ahl", [P, 2, 2, HALF], F32R)
            selp = sb_last("selp", [P, NE1, 2, P], F32R)
            adp = sb_last("adp", [P, 2, NE1, P])

        cT = sb("cT", [P, DK, B, S])
        wq1 = sb("wq1", [P, DK, Q_COLS])
        arena = sb("arena", [P, 16384])
        cut = [0]

        def take(cols, fresh=False):
            if fresh:
                cut[0] = 0
            a = arena[:, cut[0]:cut[0] + cols]
            cut[0] += cols
            assert cut[0] <= 16384
            return a

        QT = take(2 * TOK, True).rearrange("p (s t) -> p s t", s=2)
        KT = take(2 * TOK).rearrange("p (s t) -> p s t", s=2)
        VT = take(2 * TOK).rearrange("p (s t) -> p s t", s=2)
        VTc = take(TOK)
        E = take(TOK)
        nmax = sb("nmax", [P, B])
        mx = sb("mx", [P, B])
        rowsum = sb("rowsum", [P, B])
        rinv = sb("rinv", [P, B])
        oT = take(2 * TOK, True).rearrange("p (l b s) -> p l b s", l=2, b=B)
        kv = take(4 * 512).rearrange("p (s m n) -> p s m n", s=2, m=2)
        prod = take(2 * 512).rearrange("p (s n) -> p s n", s=2)
        bx1 = take(2 * TOK).rearrange("p (l b s) -> p l b s", l=2, b=B)
        bx1v = take(2 * TOK).rearrange("p (l b s) -> p l b s", l=2, b=B)
        skr = take(2 * B * CH).rearrange("p (l n) -> p l n", l=2)
        toep = sb("toep", [P, 2, D])
        dskip = sb("dskip", [P, CH])
        bias_bc = sb("bias_bc", [P, S])
        SG = take(2 * 512, True).rearrange("p (s n) -> p s n", s=2)
        H1 = take(2 * 512).rearrange("p (s n) -> p s n", s=2)
        HT = take(2 * 512).rearrange("p (s n) -> p s n", s=2)
        e0 = take(B * NE0).rearrange("p (b e) -> p b e", b=B)
        rest = take(B * NE0).rearrange("p (b e) -> p b e", b=B)
        hit = take(B * NE0).rearrange("p (b e) -> p b e", b=B)
        rw = take(B * NE0).rearrange("p (b e) -> p b e", b=B)
        rwT = sb("rwT", [P, TOK], BF16)
        rw3 = sb("rw3", [P, B, 3, NE0], BF16)
        sel = sb("sel", [P, NB0 * P], BF16)
        selstage = take(NB0 * P)
        identb = sb("identb", [P, P], BF16)
        causalb = sb("causalb", [P, P], BF16)
        TC = take(4 * TOK, True).rearrange("p (w r b t) -> p w r b t", w=2, r=2, b=B)
        TS = take(4 * TOK).rearrange("p (w r b t) -> p w r b t", w=2, r=2, b=B)
        qb = take(2 * 2 * S).rearrange("p (s r t) -> p s r t", s=2, r=2)
        kb = take(2 * 2 * S).rearrange("p (s r t) -> p s r t", s=2, r=2)
        qe = take(2 * 2 * 512).rearrange("p (s r g t) -> p s r g t", s=2, r=2, g=NKV // 2)
        ke = take(2 * 2 * 512).rearrange("p (s r q t) -> p s r q t", s=2, r=2, q=REP)
        Pe = take(4 * 512).rearrange("p (s n) -> p s n", s=4)
        PT = take(2 * 512).rearrange("p (s n) -> p s n", s=2)
        mx1 = sb("mx1", [P, 4, REP])
        Vn = sb("Vn", [P, B, NKV, HD + 1])
        yr = sb("yr", [P, 2, NQ])
        yN = rN
        yT = TC[:, 0, :, :, :]

        x_in = sem("x_in")
        xt_in = sem("xt_in")
        const_in = sem("const_in")
        ctx_in = sem("ctx_in")
        wres_in = sem("wres_in")
        wq1_in = sem("wq1_in")
        bd_in = sem("bd_in")
        sel_in = sem("sel_in")
        skip0_in = sem("skip0_in")
        bias1_in = sem("bias1_in")
        x_split = sem("x_split")
        w_split = sem("w_split")
        proj_done = sem("proj_done")
        act_evac = sem("act_evac")
        dve_evac = sem("dve_evac")
        s_done = sem("s_done")
        mx_done = sem("mx_done")
        nmax_done = sem("nmax_done")
        exp_done = sem("exp_done")
        rinv_done = sem("rinv_done")
        csum_done = sem("csum_done")
        vc_done = sem("vc_done")
        out0_done = sem("out0_done")
        sum_done = sem("sum_done")
        ln_var = sem("ln_var")
        ln_sd = sem("ln_sd")
        ln_x = sem("ln_x")
        xt_psum = sem("xt_psum")
        xt_act = sem("xt_act")
        xt_hl = sem("xt_hl")
        toep_fix = sem("toep_fix")
        kv_done = sem("kv_done")
        conv_done = sem("conv_done")
        prod_done = sem("prod_done")
        osum_done = sem("osum_done")
        ot_psum = sem("ot_psum")
        bx1_done = sem("bx1_done")
        bx1v_done = sem("bx1v_done")
        skr_done = sem("skr_done")
        skip_add = sem("skip_add")
        logit_done = sem("logit_done")
        m_sub = sem("m_sub")
        e_exp = sem("e_exp")
        rw3_done = sem("rw3_done")
        rwt_psum = sem("rwt_psum")
        rwt_done = sem("rwt_done")
        g_done = sem("g_done")
        u_done = sem("u_done")
        r_done = sem("r_done")
        silu_done = sem("silu_done")
        gu_done = sem("gu_done")
        h_done = sem("h_done")
        down_done = sem("down_done")
        qkv_psum = sem("qkv_psum")
        rope_done = sem("rope_done")
        v_psum = sem("v_psum")
        v_copy = sem("v_copy")
        qk_ready = sem("qk_ready")
        kb_done = sem("kb_done")
        q_done = sem("q_done")
        sS = sem("sS")
        sM = sem("sM")
        sP = sem("sP")
        sE = sem("sE")
        sT = sem("sT")
        sV = sem("sV")
        sY = sem("sY")
        y_rec = sem("y_rec")
        yn = sem("yn")
        y_psum = sem("y_psum")
        yt_evac = sem("yt_evac")
        wo_done = sem("wo_done")
        l1_done = sem("l1_done")
        l1_sub = sem("l1_sub")
        l1_exp = sem("l1_exp")
        a_psum = sem("a_psum")
        a_hi = sem("a_hi")
        a_lo = sem("a_lo")
        stack_psum = sem("stack_psum")
        stack_act = sem("stack_act")
        stack_dve = sem("stack_dve")
        sel_low_in = sem("sel_low_in")
        sel_low_done = sem("sel_low_done")
        low_hi = sem("low_hi")
        low_split = sem("low_split")
        fG = sem("fG")
        fU = sem("fU")
        f_silu = sem("f_silu")
        f_mul = sem("f_mul")
        f_down = sem("f_down")
        adp_zero = sem("adp_zero")
        adp_done = sem("adp_done")
        we1_done = sem("we1_done")
        wrep_done = sem("wrep_done")
        wt_psum = sem("wt_psum")
        wt_evac = sem("wt_evac")
        dw_done = sem("dw_done")
        bd_done = sem("bd_done")
        dve_chain = sem("dve_chain")
        out_done = sem("out_done")
        hi_done = sem("hi_done")
        const_conv = sem("const_conv")
        pool_settled = sem("pool_settled")
        sp_settled = sem("sp_settled")
        ring_in = [sem("ring_in0"), sem("ring_in1")]
        toep_in = [sem("toep_in0"), sem("toep_in1")]
        lowraw_in = [sem("lowraw_in0"), sem("lowraw_in1")]
        outring_in = [sem("outring_in0"), sem("outring_in1")]


        block = ctx.enter_context(nc.Block())

        @block.sync
        def _(sp):
            sp.dma_start(xT[:], x_t.rearrange("(k p) t -> p k t", p=P)).then_inc(xt_in, 16)

            def load_attn0(h, slot):
                sp.wait_ge(w_split, count(h - 1))
                settle(sp, sp_settled)
                sp.dma_start(ring[:, slot, 0:A_WO], w_attn0[h, :, :]).then_inc(ring_in[slot], 16)
                sp.wait_ge(out0_done, count(h - 1))
                settle(sp, sp_settled)
                sp.dma_start(outring[:, slot, :], wo_attn0[h, :, :]).then_inc(outring_in[slot], 16)

            load_attn0(0, 0)
            load_attn0(1, 1)
            sp.dma_start(xN[:], x_nat).then_inc(x_in, 16)
            sp.dma_start(cst[:], consts).then_inc(const_in, 16)
            sp.dma_start(cT[:], ctx_t.rearrange("(k p) b s -> p k b s", p=P)).then_inc(ctx_in, 16)
            sp.dma_start(wres[:], w_res).then_inc(wres_in, 16)
            sp.dma_start(wq1[:], w_attn1).then_inc(wq1_in, 16)
            sp.dma_start(bd[:], w_bd).then_inc(bd_in, 16)
            sp.dma_start(dskip[:], skip0.partition_broadcast(P)).then_inc(skip0_in, 16)
            sp.dma_start(bias_bc[:], bias1.partition_broadcast(P)).then_inc(bias1_in, 16)
            with sp.Fori(1, NH // 2) as i:
                load_attn0(2 * i, 0)
                load_attn0(2 * i + 1, 1)

            def load_toep(src, layer, h, slot):
                sp.wait_ge(conv_done, count(2 * (CH * layer + h - 1)))
                settle(sp, sp_settled)
                flat = src[h, :, :]
                sp.dma_start(toep[:, slot, :], flat).then_inc(toep_in[slot], 16)

            def load_moe(n, slot):
                sp.wait_ge(w_split, NH + n - 1)
                settle(sp, sp_settled)
                sp.dma_start(ring[:, slot, 0:C_DOWN], w_moe[n, :, :]).then_inc(ring_in[slot], 16)
                if isinstance(n, int) and n < 2:
                    sp.wait_ge(out0_done, NH + n - 1)
                else:
                    sp.wait_ge(down_done, 2 * (n - 1))
                settle(sp, sp_settled)
                sp.dma_start(outring[:, slot, :], w_down0[n, :, :]).then_inc(outring_in[slot], 16)

            def load_ffn1(f, slot):
                if isinstance(f, int) and f < 2:
                    sp.wait_ge(w_split, NH + NB0 + f - 1)
                else:
                    sp.wait_ge(f_down, 18 * (f - 1))
                settle(sp, sp_settled)
                sp.dma_start(ring[:, slot, :], w_ffn1[f, :, :]).then_inc(ring_in[slot], 16)

            def load_low(f, slot):
                sp.wait_ge(low_split, count(f - 1))
                settle(sp, sp_settled)
                sp.dma_start(lowraw[:, slot, :], w_low[f, :, :]).then_inc(lowraw_in[slot], 16)

            load_toep(toep0, 0, 0, 0)
            load_toep(toep0, 0, 1, 1)
            load_moe(0, 0)
            load_moe(1, 1)
            with sp.Fori(1, CH // 2) as i:
                load_toep(toep0, 0, 2 * i, 0)
                load_toep(toep0, 0, 2 * i + 1, 1)
            sp.wait_ge(ot_psum, 4)
            sp.dma_start(selstage[0:3 * NE0, :], sel3).then_inc(sel_in, 16)
            load_toep(toep1, 1, 0, 0)
            load_toep(toep1, 1, 1, 1)
            with sp.Fori(1, NB0 // 2) as i:
                load_moe(2 * i, 0)
                load_moe(2 * i + 1, 1)
            load_ffn1(0, 0)
            load_ffn1(1, 1)
            sp.dma_start(lowraw[:, 1, :], sel_low).then_inc(sel_low_in, 16)
            load_low(0, 0)
            with sp.Fori(1, CH // 2) as i:
                load_toep(toep1, 1, 2 * i, 0)
                load_toep(toep1, 1, 2 * i + 1, 1)
            sp.wait_ge(sel_low_done, 1)
            load_low(1, 1)
            with sp.Fori(1, FB // 2) as i:
                load_low(2 * i, 0)
                load_ffn1(2 * i, 0)
                load_low(2 * i + 1, 1)
                load_ffn1(2 * i + 1, 1)
            sp.wait_ge(ln_x, 6 * B)
            sp.dma_start(out, xN[:]).then_inc(out_done, 16)
            sp.wait_ge(out_done, 16)

        @block.gpsimd
        def _(pool):
            def split_attn0(h, slot):
                pool.wait_ge(ring_in[slot], count(8 * (h - slot) + 16))
                pool.wait_ge(proj_done, count(6 * (h - 1)))
                settle(pool, pool_settled)
                pool.tensor_copy(ringh[:, slot, :], ring[:, slot, 0:A_WO]).then_inc(hi_done, 1)
                pool.wait_ge(hi_done, h + 1)
                pool.tensor_tensor(ringl[:, slot, :], ring[:, slot, 0:A_WO], ringh[:, slot, :].bitcast(F32),
                                   ALU.subtract).then_inc(w_split, 1)

            split_attn0(0, 0)
            split_attn0(1, 1)
            with pool.Fori(1, NH // 2) as i:
                split_attn0(2 * i, 0)
                split_attn0(2 * i + 1, 1)

            def split_moe(n, slot):
                pool.wait_ge(ring_in[slot], count(8 * (NH + n - slot) + 16))
                if isinstance(n, int) and n < 2:
                    pool.wait_ge(proj_done, 6 * NH)
                else:
                    pool.wait_ge(u_done, count(2 * (n - 1)))
                settle(pool, pool_settled)
                pool.tensor_copy(ringh[:, slot, 0:C_DOWN], ring[:, slot, 0:C_DOWN]).then_inc(hi_done, 1)
                pool.wait_ge(hi_done, NH + n + 1)
                pool.tensor_tensor(ringl[:, slot, 0:C_DOWN], ring[:, slot, 0:C_DOWN],
                                   ringh[:, slot, 0:C_DOWN].bitcast(F32), ALU.subtract).then_inc(w_split, 1)

            def conv_products(layer, h, slot, left, right):
                pool.wait_ge(conv_done, count(2 * (CH * layer + h - 1)))
                for m in range(DK):
                    a = left[:, m, :, bass.ds(CI * h, CI)].unsqueeze(3).broadcast_to([P, B, CI, CI])
                    c = right[:, m, :, bass.ds(CI * h, CI)].unsqueeze(2).broadcast_to([P, B, CI, CI])
                    o = kv[:, slot, m, :].rearrange("p (b i j) -> p b i j", b=B, i=CI)
                    pool.tensor_tensor(o, a, c, ALU.mult).then_inc(kv_done, 1)

            xTv = xT[:].rearrange("p k (b s) -> p k b s", b=B)
            pool.wait_ge(ctx_in, 16)
            pool.wait_ge(out0_done, NH)
            conv_products(0, 0, 0, cT, cT)
            conv_products(0, 1, 1, cT, cT)
            with pool.Fori(1, CH // 2) as i:
                conv_products(0, 2 * i, 0, cT, cT)
                conv_products(0, 2 * i + 1, 1, cT, cT)
            split_moe(0, 0)
            split_moe(1, 1)
            with pool.Fori(1, NB0 // 2) as i:
                split_moe(2 * i, 0)
                split_moe(2 * i + 1, 1)

            group = cst[:, C_GROUP:C_GROUP + NKV // 2].unsqueeze(2).broadcast_to([P, NKV // 2, S])
            hq = cst[:, C_HQ:C_HQ + REP].unsqueeze(2).broadcast_to([P, REP, S])

            def spread(b, slot):
                pool.wait_ge(sS, count(NKV * (b - 1)))
                pool.tensor_tensor(kb[:, slot, :, :], TC[:, 1, :, b, :], TS[:, 1, :, b, :], ALU.add)\
                    .then_inc(kb_done, 1)
                pool.tensor_tensor(qb[:, slot, :, :], TC[:, 0, :, b, :], TS[:, 0, :, b, :], ALU.add)\
                    .then_inc(q_done, 1)
                pool.wait_ge(kb_done, b + 1)
                pool.wait_ge(q_done, b + 1)
                for r in range(2):
                    q1 = qb[:, slot, r, :].unsqueeze(1).broadcast_to([P, NKV // 2, S])
                    pool.tensor_tensor(qe[:, slot, r, :, :], q1, group, ALU.mult)
                    k1 = kb[:, slot, r, :].unsqueeze(1).broadcast_to([P, REP, S])
                    ins = pool.tensor_tensor(ke[:, slot, r, :, :], k1, hq, ALU.mult)
                ins.then_inc(qk_ready, 1)

            pool.wait_ge(rope_done, 16)
            spread(0, 0)
            spread(1, 1)
            with pool.Fori(1, B // 2) as i:
                spread(2 * i, 0)
                spread(2 * i + 1, 1)

            pool.wait_ge(wo_done, 4)
            pool.wait_ge(bias1_in, 16)
            bb = bias_bc[:].unsqueeze(1).broadcast_to([P, B, S])
            for m in range(DK):
                ins = pool.tensor_tensor(bx1[:, m, :, :], cT[:, m, :, :], bb, ALU.mult)
            ins.then_inc(bx1_done, 1)
            pool.wait_ge(xt_act, 16)
            pool.wait_ge(bx1_done, 1)
            conv_products(1, 0, 0, xTv, cT)
            conv_products(1, 1, 1, xTv, cT)
            for m in range(DK):
                ins = pool.tensor_tensor(bx1v[:, m, :, :], bx1[:, m, :, :], xTv[:, m, :, :], ALU.mult)
            ins.then_inc(bx1v_done, 1)
            with pool.Fori(1, CH // 2) as i:
                conv_products(1, 2 * i, 0, xTv, cT)
                conv_products(1, 2 * i + 1, 1, xTv, cT)
            pool.wait_ge(skr_done, 1)
            for m in range(DK):
                sk = skr[:, m, :].unsqueeze(2).broadcast_to([P, B * CH, CI])
                ins = pool.tensor_tensor(bx1[:, m, :, :].rearrange("p b (h j) -> p (b h) j", j=CI),
                                         cT[:, m, :, :].rearrange("p b (h j) -> p (b h) j", j=CI), sk, ALU.mult)
            ins.then_inc(skip_add, 1)

            pool.wait_ge(a_psum, 1)
            pool.memset(adp[:], 0.0).then_inc(adp_zero, 1)
            pool.wait_ge(adp_zero, 1)

            def split_ffn1(f, slot):
                pool.wait_ge(ring_in[slot], 8 * (NH + NB0 + f - slot) + 16)
                pool.wait_ge(fU, count(18 * (f - 1)))
                settle(pool, pool_settled)
                pool.tensor_copy(ringh[:, slot, 0:F_BASE], ring[:, slot, 0:F_BASE]).then_inc(hi_done, 1)
                pool.wait_ge(hi_done, NH + NB0 + f + 1)
                pool.tensor_tensor(ringl[:, slot, 0:F_BASE], ring[:, slot, 0:F_BASE],
                                   ringh[:, slot, 0:F_BASE].bitcast(F32), ALU.subtract).then_inc(w_split, 1)
                pool.wait_ge(f_down, count(18 * (f - 1)))
                settle(pool, pool_settled)
                pool.tensor_copy(adp[:, slot, :, :].rearrange("p e (c r) -> p (e c) r", r=RANK)[:, ::NE1 + 1, :],
                                 ring[:, slot, F_AD:F_AD + P].rearrange("p (e r) -> p e r", r=RANK))\
                    .then_inc(adp_done, 1)

            split_ffn1(0, 0)
            split_ffn1(1, 1)
            with pool.Fori(1, FB // 2) as i:
                split_ffn1(2 * i, 0)
                split_ffn1(2 * i + 1, 1)

        @block.scalar
        def _(act):
            def evac_q(h, slot, j):
                act.wait_ge(proj_done, 6 * h + 1 + j)
                act.wait_ge(s_done, count(2 * (h - 1)))
                act.activation(QT[:, slot, j * HALF:(j + 1) * HALF], bank[:, j, :], ACT.Copy)\
                    .then_inc(act_evac, 1)

            def evac_v(h, slot, j):
                act.wait_ge(proj_done, 6 * h + 5 + j)
                act.wait_ge(vc_done, count(2 * (h - 1)))
                act.activation(VT[:, slot, j * HALF:(j + 1) * HALF], bank[:, j, :], ACT.Copy)\
                    .then_inc(act_evac, 1)

            def exps(h, j):
                act.wait_ge(nmax_done, 2 * h + j + 1)
                for b in range(4 * j, 4 * j + 4):
                    ins = act.activation(E[:, b * S:(b + 1) * S], bank[:, 2 + j, (b % 4) * S:(b % 4 + 1) * S], ACT.Exp,
                                         bias=nmax[:, b:b + 1], scale=DH ** -0.5, accum_out=rowsum[:, b:b + 1])
                ins.then_inc(exp_done, 1)

            def head(h, slot, last=False):
                if not last:
                    evac_q(h + 1, 1 - slot, 0)
                exps(h, 0)
                if not last:
                    evac_q(h + 1, 1 - slot, 1)
                exps(h, 1)
                if not last:
                    evac_v(h + 1, 1 - slot, 0)
                    evac_v(h + 1, 1 - slot, 1)

            for j in range(2):
                evac_q(0, 0, j)
            for j in range(2):
                evac_v(0, 0, j)
            head(0, 0)
            with act.Fori(0, (NH - 2) // 2) as i:
                head(2 * i + 1, 1)
                head(2 * i + 2, 0)
            head(NH - 1, 1, last=True)

            def norm_and_turn(layer_norm, turn=True):
                act.wait_ge(ln_var, layer_norm + 1)
                act.activation(sd[:], ve[:], ACT.Sqrt).then_inc(ln_sd, 1)
                if not turn:
                    return
                for n, (k, j) in enumerate(((0, 0), (1, 0), (0, 1), (1, 1))):
                    act.wait_ge(xt_psum, 4 * layer_norm + n + 1)
                    act.activation(xT[:, k, j * HALF:(j + 1) * HALF], bank[:, 2 * k + j, :], ACT.Copy)\
                        .then_inc(xt_act, 1)

            norm_and_turn(0)
            norm_and_turn(1)

            act.wait_ge(m_sub, 1)
            act.activation(e0, e0, ACT.Exp).then_inc(e_exp, 1)

            def silus(n, slot):
                for j in range(2):
                    s = 2 * n + j
                    act.wait_ge(g_done, s + 1)
                    act.wait_ge(gu_done, count(s - 1))
                    act.activation(SG[:, j, :], bank[:, 3 * j, :], ACT.Silu).then_inc(silu_done, 1)

            two_at_a_time(act, NB0, silus)
            norm_and_turn(2)

            def evac_pt(b, g):
                t = NKV * b + g
                act.wait_ge(sT, t + 1)
                act.wait_ge(sY, count(t - 1))
                act.activation(PT[:, g % 2, :], bank[:, 6 + g % 2, :], ACT.Copy).then_inc(sV, 1)

            def attn1(b, slot):
                for g in range(NKV):
                    t = NKV * b + g
                    act.wait_ge(sP, t + 1)
                    act.activation(Pe[:, g % 4, :], Pe[:, g % 4, :], ACT.Exp, scale=HD ** -0.5).then_inc(sE, 1)
                    if g > 1:
                        evac_pt(b, g - 2)
                    elif not isinstance(b, int) or b > 0:
                        evac_pt(b - 1, NKV - 2 + g)

            two_at_a_time(act, B, attn1)
            evac_pt(B - 1, NKV - 2)
            evac_pt(B - 1, NKV - 1)
            for n, (k, j) in enumerate(((0, 0), (1, 0), (0, 1), (1, 1))):
                act.wait_ge(y_psum, n + 1)
                act.activation(yT[:, k, 4 * j:4 * j + 4, :], bank[:, 2 * k + j, :].rearrange("p (b t) -> p b t", b=4),
                               ACT.Copy).then_inc(yt_evac, 1)
            norm_and_turn(3)
            norm_and_turn(4)
            act.wait_ge(l1_sub, 1)
            act.activation(we1[:], we1[:], ACT.Exp).then_inc(l1_exp, 1)
            for n in range(4):
                act.wait_ge(a_psum, n + 1)
                act.wait_ge(stack_psum, count(NE1 * (n - 1)))
                act.activation(ahl[:, n % 2, 0, :], bank[:, n, :], ACT.Copy).then_inc(a_hi, 1)
                for e in range(0, NE1, 2):
                    act.wait_ge(stack_psum, NE1 * n + e + 1)
                    act.activation(astk[:, n // 2, e, (n % 2) * HALF:(n % 2 + 1) * HALF], bank[:, 4 + e % 4, :],
                                   ACT.Copy).then_inc(stack_act, 1)

            def silus1(f, slot):
                for c in range(2):
                    for e in range(NE1 + 1):
                        k = 18 * f + 9 * c + e
                        act.wait_ge(fG, k + 1)
                        act.wait_ge(f_mul, count(k - 1))
                        act.activation(SF[:, (c + e) % 2, :], bank[:, 0, :], ACT.Silu).then_inc(f_silu, 1)

            two_at_a_time(act, FB, silus1)
            for c in range(2):
                act.wait_ge(wt_psum, c + 1)
                act.activation(SF[:, c, :], bank[:, c, :], ACT.Copy).then_inc(wt_evac, 1)
            norm_and_turn(5, turn=False)

        @block.vector
        def _(dve):
            chained = [0]

            def link(ins):
                chained[0] += 1
                ins.then_inc(dve_chain, 1)
                dve.wait_ge(dve_chain, chained[0])

            dve.wait_ge(xt_in, 16)
            for k in range(DK):
                ins = dve.tensor_copy(xTh[:, k, :], xT[:, k, :])
            link(ins)
            for k in range(DK):
                ins = dve.tensor_tensor(xTl[:, k, :], xT[:, k, :], xTh[:, k, :].bitcast(F32), ALU.subtract)
            ins.then_inc(x_split, 1)
            dve.memset(Vn[:], 1.0).then_inc(v_copy, 1)

            def evac_k(h, slot, j):
                dve.wait_ge(proj_done, 6 * h + 3 + j)
                dve.wait_ge(s_done, count(2 * (h - 1)))
                dve.tensor_copy(KT[:, slot, j * HALF:(j + 1) * HALF], bank[:, j, :]).then_inc(dve_evac, 1)

            def row_max(h, j):
                dve.wait_ge(s_done, 2 * h + j + 1)
                dve.tensor_reduce(mx[:, 4 * j:4 * j + 4], bank[:, 2 + j, :].rearrange("p (b k) -> p b k", b=4),
                                  AX, ALU.max).then_inc(mx_done, 1)
                dve.wait_ge(mx_done, 2 * h + j + 1)
                dve.tensor_scalar(nmax[:, 4 * j:4 * j + 4], mx[:, 4 * j:4 * j + 4], -(DH ** -0.5), None, ALU.mult)\
                    .then_inc(nmax_done, 1)

            def recip(h, j):
                dve.wait_ge(exp_done, 2 * h + j + 1)
                dve.reciprocal(rinv[:, 4 * j:4 * j + 4], rowsum[:, 4 * j:4 * j + 4]).then_inc(rinv_done, 1)

            def scale_v(h, slot, j):
                dve.wait_ge(csum_done, 2 * h + j + 1)
                dve.wait_ge(act_evac, 4 * h + 3 + j)
                dve.tensor_tensor(VTc[:, j * HALF:(j + 1) * HALF], bank[:, 2 + j, :],
                                  VT[:, slot, j * HALF:(j + 1) * HALF], ALU.mult).then_inc(vc_done, 1)

            def head(h, slot, last=False):
                row_max(h, 0)
                row_max(h, 1)
                recip(h, 0)
                if not last:
                    evac_k(h + 1, 1 - slot, 0)
                recip(h, 1)
                scale_v(h, slot, 0)
                if not last:
                    evac_k(h + 1, 1 - slot, 1)
                scale_v(h, slot, 1)

            evac_k(0, 0, 0)
            evac_k(0, 0, 1)
            head(0, 0)
            with dve.Fori(0, (NH - 2) // 2) as i:
                head(2 * i + 1, 1)
                head(2 * i + 2, 0)
            head(NH - 1, 1, last=True)

            def norm(layer_norm, produced, steps, first_bank=4):
                if layer_norm == 0:
                    dve.wait_ge(x_in, 16)
                for q in range(4):
                    dve.wait_ge(produced, steps[q])
                    ins = dve.tensor_tensor(rN[:, 2 * q:2 * q + 2, :],
                                            bank[:, first_bank + q, :].rearrange("p (b d) -> p b d", b=2),
                                            xN[:, 2 * q:2 * q + 2, :], ALU.add)
                link(ins)
                for b in range(B):
                    ins = dve.bn_stats(st[:, b, :], rN[:, b, :])
                link(ins)
                for b in range(B):
                    ins = dve.bn_aggr(mv[:, b, :], st[:, b, :])
                link(ins)
                dve.tensor_scalar(ve[:], mv[:, :, 1], EPS, None, ALU.add).then_inc(ln_var, 1)
                dve.wait_ge(ln_sd, layer_norm + 1)
                link(dve.reciprocal(rstd[:], sd[:]))
                for b in range(B):
                    dve.tensor_scalar(xN[:, b, :], rN[:, b, :], mv[:, b, 0:1], rstd[:, b:b + 1],
                                      ALU.subtract, ALU.mult).then_inc(ln_x, 1)

            def split_x(layer_norm):
                for n, (k, j) in enumerate(((0, 0), (1, 0), (0, 1), (1, 1))):
                    dve.wait_ge(xt_act, 4 * layer_norm + n + 1)
                    half = slice(j * HALF, (j + 1) * HALF)
                    link(dve.tensor_copy(xTh[:, k, half], xT[:, k, half]))
                    dve.tensor_tensor(xTl[:, k, half], xT[:, k, half], xTh[:, k, half].bitcast(F32), ALU.subtract)\
                        .then_inc(xt_hl, 1)

            norm(0, out0_done, [NH] * 4)

            def conv_fix(layer, h, slot):
                dve.wait_ge(toep_in[slot], count(8 * (CH * layer + h - slot) + 16))
                dve.scalar_tensor_tensor(toep[:, slot, 0:P], ident, dskip[:, bass.ds(h, 1)], toep[:, slot, 0:P],
                                         ALU.mult, ALU.add).then_inc(toep_fix, 1)

            def conv_reduce(layer, h, slot, gate):
                for l in range(DK):
                    s = 2 * (CH * layer + h) + l
                    dve.wait_ge(conv_done, s + 1)
                    dve.wait_ge(osum_done, count(s - 1))
                    g = gate[:, l, :, bass.ds(CI * h, CI)].unsqueeze(3).broadcast_to([P, B, CI, CI])
                    dve.tensor_tensor(prod[:, l, :].rearrange("p (b j i) -> p b i j", b=B, j=CI),
                                      bank[:, 2 * slot + l, :].rearrange("p (b i j) -> p b i j", b=B, i=CI),
                                      g, ALU.mult).then_inc(prod_done, 1)
                for l in range(DK):
                    s = 2 * (CH * layer + h) + l
                    dve.wait_ge(prod_done, s + 1)
                    dve.tensor_reduce(oT[:, l, :, bass.ds(CI * h, CI)],
                                      prod[:, l, :].rearrange("p (b j i) -> p b j i", b=B, j=CI), AX, ALU.add)\
                        .then_inc(osum_done, 1)

            xTv = xT[:].rearrange("p k (b s) -> p k b s", b=B)
            dve.wait_ge(skip0_in, 16)
            conv_fix(0, 0, 0)
            conv_fix(0, 1, 1)
            dve.wait_ge(xt_act, 4)

            def conv0(h, slot):
                conv_reduce(0, h, slot, xTv)

            conv0(0, 0)
            conv0(1, 1)
            with dve.Fori(1, CH // 2) as i:
                conv_fix(0, 2 * i, 0)
                conv_fix(0, 2 * i + 1, 1)
                conv0(2 * i, 0)
                conv0(2 * i + 1, 1)
            norm(1, ot_psum, [1, 2, 3, 4])
            split_x(1)

            dve.wait_ge(sel_in, 16)
            dve.tensor_copy(sel[0:3 * NE0, :], selstage[0:3 * NE0, :]).then_inc(const_conv, 1)
            dve.tensor_copy(causalb[:], cst[:, C_CAUSAL:C_CAUSAL + P]).then_inc(const_conv, 1)
            link(dve.tensor_copy(identb[:], ident))

            def chosen(values, n, top, mask, scratch):
                for b in range(B):
                    ins = dve.max(top8[:, b, :], values[:, b, :])
                link(ins)
                for b in range(B):
                    ins = dve.max_index(idx8[:, b, :], top8[:, b, :], values[:, b, :])
                link(ins)
                link(dve.tensor_copy(idxf[:], idx8[:]))
                iota = cst[:, C_IOTA:C_IOTA + n].unsqueeze(1).broadcast_to([P, B, n])
                for r in range(top):
                    at = idxf[:, :, r:r + 1].broadcast_to([P, B, n])
                    link(dve.tensor_tensor(scratch if r else mask, iota, at, ALU.is_equal))
                    if r:
                        link(dve.tensor_tensor(mask, mask, scratch, ALU.add))

            dve.wait_ge(logit_done, 1)
            lg = bank[:, 0, 0:B * NE0].rearrange("p (b e) -> p b e", b=B)
            link(dve.tensor_reduce(m1[:], lg, AX, ALU.max))
            dve.tensor_tensor(e0, lg, m1[:].unsqueeze(2).broadcast_to([P, B, NE0]), ALU.subtract)\
                .then_inc(m_sub, 1)
            dve.wait_ge(e_exp, 1)
            chosen(e0, NE0, TOP0, hit, rest)
            link(dve.tensor_tensor(rw, hit, e0, ALU.mult))
            link(dve.tensor_reduce(s1[:], rw, AX, ALU.add))
            link(dve.reciprocal(r1[:], s1[:]))
            link(dve.tensor_tensor(rw, rw, r1[:].unsqueeze(2).broadcast_to([P, B, NE0]), ALU.mult))
            link(dve.tensor_copy(rw3[:, :, 0, :], rw))
            link(dve.tensor_tensor(rest, rw, rw3[:, :, 0, :], ALU.subtract))
            link(dve.tensor_copy(rw3[:, :, 1, :], rest))
            dve.tensor_tensor(rw3[:, :, 2, :], rest, rw3[:, :, 1, :], ALU.subtract).then_inc(rw3_done, 1)
            dve.wait_ge(rwt_psum, 1)
            dve.tensor_copy(rwT[0:3 * NE0, :], bank[0:3 * NE0, 1, :].bitcast(BF16)).then_inc(rwt_done, 1)

            def experts(n, slot):
                for j in range(2):
                    s = 2 * n + j
                    dve.wait_ge(silu_done, s + 1)
                    dve.wait_ge(u_done, s + 1)
                    dve.tensor_tensor(H1[:, j, :], bank[:, 1, :], SG[:, j, :], ALU.mult).then_inc(gu_done, 1)
                    dve.wait_ge(r_done, s + 1)
                    dve.wait_ge(down_done, count(s - 1))
                    dve.wait_ge(gu_done, s + 1)
                    dve.tensor_tensor(HT[:, j, :], bank[:, 2, :], H1[:, j, :], ALU.mult).then_inc(h_done, 1)

            two_at_a_time(dve, NB0, experts)
            norm(2, down_done, [2 * NB0] * 4)

            dve.wait_ge(wq1_in, 16)
            cos = cst[:, C_COS:C_COS + P].unsqueeze(1).broadcast_to([P, 4, S])
            sin = cst[:, C_SIN:C_SIN + P].unsqueeze(1).broadcast_to([P, 4, S])
            n = 0
            for w in range(2):
                for r in range(2):
                    for j in range(2):
                        for dst, table in ((TC, cos), (TS, sin)):
                            dve.wait_ge(qkv_psum, n + 1)
                            dve.tensor_tensor(dst[:, w, r, 4 * j:4 * j + 4, :],
                                              bank[:, n % 4, :].rearrange("p (b t) -> p b t", b=4),
                                              table, ALU.mult).then_inc(rope_done, 1)
                            n += 1
            dve.wait_ge(v_psum, 1)
            dve.wait_ge(v_copy, 1)
            dve.tensor_copy(Vn[:, :, :, 0:HD], bank[:, 6, :].rearrange("p (b g d) -> p b g d", b=B, g=NKV))\
                .then_inc(yn, 1)

            def norm_y(b, slot):
                dve.wait_ge(sY, NKV * b + NKV)
                y = bank[:, 4 + slot, 0:NQ * (HD + 1)].rearrange("p (h d) -> p h d", h=NQ)
                dve.reciprocal(yr[:, slot, :], y[:, :, HD]).then_inc(y_rec, 1)
                dve.wait_ge(y_rec, b + 1)
                dve.tensor_tensor(yN[:, b, :].rearrange("p (h d) -> p h d", h=NQ), y[:, :, 0:HD],
                                  yr[:, slot, :].unsqueeze(2).broadcast_to([P, NQ, HD]), ALU.mult)\
                    .then_inc(yn, 1)

            def attn1(b, slot):
                for g in range(NKV):
                    t = NKV * b + g
                    sc = bank[:, g % 4, :].rearrange("p (q s) -> p q s", q=REP)
                    dve.wait_ge(sS, t + 1)
                    dve.tensor_reduce(mx1[:, g % 4, :], sc, AX, ALU.max).then_inc(sM, 1)
                    dve.wait_ge(sM, t + 1)
                    dve.wait_ge(sT, count(t - 3))
                    dve.tensor_tensor(Pe[:, g % 4, :].rearrange("p (q s) -> p q s", q=REP), sc,
                                      mx1[:, g % 4, :].unsqueeze(2).broadcast_to([P, REP, S]), ALU.subtract)\
                        .then_inc(sP, 1)
                    if g == 5 and (not isinstance(b, int) or b > 0):
                        norm_y(b - 1, 1 - slot)

            two_at_a_time(dve, B, attn1)
            norm_y(B - 1, 1)
            norm(3, wo_done, [1, 2, 3, 4])

            dve.wait_ge(xt_act, 16)

            def conv1(h, slot):
                conv_reduce(1, h, slot, cT)

            conv1(0, 0)
            conv1(1, 1)
            dve.wait_ge(bx1v_done, 1)
            for m in range(DK):
                ins = dve.tensor_reduce(skr[:, m, :], bx1v[:, m, :, :].rearrange("p b (h i) -> p (b h) i", i=CI),
                                        AX, ALU.add)
            ins.then_inc(skr_done, 1)
            with dve.Fori(1, CH // 2) as i:
                conv1(2 * i, 0)
                conv1(2 * i + 1, 1)
            dve.wait_ge(skip_add, 1)
            dve.wait_ge(osum_done, 4 * CH)
            for m in range(DK):
                ins = dve.tensor_tensor(oT[:, m, :, :], oT[:, m, :, :], bx1[:, m, :, :], ALU.add)
            ins.then_inc(sum_done, 1)
            norm(4, ot_psum, [5, 6, 7, 8])

            split_x(4)
            dve.wait_ge(l1_done, 1)
            lg1 = bank[:, 4, 0:B * NE1].rearrange("p (b e) -> p b e", b=B)
            link(dve.tensor_reduce(m1[:], lg1, AX, ALU.max))
            dve.tensor_tensor(we1[:], lg1, m1[:].unsqueeze(2).broadcast_to([P, B, NE1]), ALU.subtract)\
                .then_inc(l1_sub, 1)
            dve.wait_ge(sel_low_in, 16)
            dve.tensor_copy(selp[:].rearrange("p e h c -> p (e h c)"), lowraw[:, 1, :]).then_inc(sel_low_done, 1)
            for n in range(4):
                dve.wait_ge(a_hi, n + 1)
                dve.tensor_tensor(ahl[:, n % 2, 1, :], bank[:, n, :], ahl[:, n % 2, 0, :].bitcast(F32),
                                  ALU.subtract).then_inc(a_lo, 1)
                for e in range(1, NE1, 2):
                    dve.wait_ge(stack_psum, NE1 * n + e + 1)
                    dve.tensor_copy(astk[:, n // 2, e, (n % 2) * HALF:(n % 2 + 1) * HALF], bank[:, 4 + e % 4, :])\
                        .then_inc(stack_dve, 1)
            dve.wait_ge(l1_exp, 1)
            link(dve.tensor_reduce(s1[:], we1[:], AX, ALU.add))
            link(dve.reciprocal(r1[:], s1[:]))
            link(dve.tensor_scalar(r1[:], r1[:], SCALING, None, ALU.mult))
            chosen(we1[:], NE1, TOP1, hit1[:], rest1[:])
            link(dve.tensor_tensor(we1[:], we1[:], hit1[:], ALU.mult))
            dve.tensor_tensor(we1[:], we1[:], r1[:].unsqueeze(2).broadcast_to([P, B, NE1]), ALU.mult)\
                .then_inc(we1_done, 1)
            dve.wait_ge(we1_done, 1)
            dve.tensor_copy(wrep.rearrange("p (b e) r -> p b e r", b=B),
                            we1[:].unsqueeze(3).broadcast_to([P, B, NE1, RANK])).then_inc(wrep_done, 1)

            def low_high(f, slot):
                dve.wait_ge(lowraw_in[slot], 8 * (f - slot) + 16)
                dve.wait_ge(fU, count(18 * (f - 1)))
                dve.tensor_copy(bstk[:, slot, :], lowraw[:, slot, :]).then_inc(low_hi, 1)
                dve.wait_ge(low_hi, f + 1)
                low = bstk[P // 2:P, slot, :]
                dve.tensor_tensor(low, lowraw[P // 2:P, slot, :], low.bitcast(F32), ALU.subtract)\
                    .then_inc(low_split, 1)

            def gated(f, slot):
                if not isinstance(f, int) or f + 1 < FB:
                    low_high(f + 1, 1 - slot)
                for c in range(2):
                    for e in range(NE1 + 1):
                        k = 18 * f + 9 * c + e
                        dve.wait_ge(f_silu, k + 1)
                        dve.wait_ge(fU, k + 1)
                        dve.wait_ge(f_down, count(k - 1))
                        dve.tensor_tensor(HF[:, (c + e) % 2, :], bank[:, 1, :], SF[:, (c + e) % 2, :], ALU.mult)\
                            .then_inc(f_mul, 1)

            low_high(0, 0)
            two_at_a_time(dve, FB, gated)
            dve.wait_ge(f_down, 18 * FB)
            for c in range(2):
                dve.wait_ge(wt_evac, c + 1)
                dve.tensor_tensor(xT[:, 0, c * HALF:(c + 1) * HALF], bank[:, 6 + c, :], SF[:, c, :], ALU.mult)\
                    .then_inc(dw_done, 1)
            norm(5, bd_done, [1, 2, 3, 4], first_bank=2)

        @block.tensor
        def _(pe):
            halves = [slice(0, HALF), slice(HALF, TOK)]

            def split_product(o, slot, col, j):
                for k in range(DK):
                    wc = slice(col + k * P, col + (k + 1) * P)
                    pe.matmul(o, ringh[:, slot, wc], xTh[:, k, halves[j]], start=(k == 0), stop=False)
                    pe.matmul(o, ringh[:, slot, wc], xTl[:, k, halves[j]], start=False, stop=False)
                    ins = pe.matmul(o, ringl[:, slot, wc], xTh[:, k, halves[j]], start=False, stop=(k == DK - 1))
                return ins

            def project(h, slot, c):
                if c == 0:
                    pe.wait_ge(w_split, h + 1)
                if c < 4:
                    pe.wait_ge(act_evac, count(4 * h - 1 + c))
                else:
                    pe.wait_ge(dve_evac, count(2 * h + c - 3))
                split_product(bank[:, c % 2, :], slot, (c // 2) * DK * P, c % 2).then_inc(proj_done, 1)

            def scores(h, slot, j):
                pe.wait_ge(act_evac, 4 * h + 1 + j)
                pe.wait_ge(dve_evac, 2 * h + 1 + j)
                pe.wait_ge(vc_done, count(2 * h - 1 + j))
                for b in range(4 * j, 4 * j + 4):
                    t = slice(b * S, (b + 1) * S)
                    ins = pe.matmul(bank[:, 2 + j, (b % 4) * S:(b % 4 + 1) * S], QT[:, slot, t], KT[:, slot, t],
                                    start=True, stop=True)
                ins.then_inc(s_done, 1)

            def key_weights(h, j):
                pe.wait_ge(rinv_done, 2 * h + j + 1)
                for b in range(4 * j, 4 * j + 4):
                    ins = pe.matmul(bank[:, 2 + j, (b % 4) * S:(b % 4 + 1) * S],
                                    rinv[:, b:b + 1].broadcast_to([P, P]), E[:, b * S:(b + 1) * S],
                                    start=True, stop=True)
                ins.then_inc(csum_done, 1)

            def attn_out(h, slot):
                pe.wait_ge(outring_in[slot], 8 * (h - slot) + 16)
                for b in range(B):
                    if b % 4 == 0:
                        pe.wait_ge(vc_done, 2 * h + b // 4 + 1)
                    ins = pe.matmul(bank[:, 4 + b // 2, (b % 2) * D:(b % 2 + 1) * D], VTc[:, b * S:(b + 1) * S],
                                    outring[:, slot, :],
                                    start=(isinstance(h, int) and h == 0 and b % 2 == 0),
                                    stop=(isinstance(h, int) and h == NH - 1), skip_group_check=True)
                ins.then_inc(out0_done, 1)

            def head(h, slot, last=False):
                def ahead(c):
                    if not last:
                        project(h + 1, 1 - slot, c)
                scores(h, slot, 0)
                ahead(0)
                scores(h, slot, 1)
                ahead(1)
                ahead(2)
                key_weights(h, 0)
                ahead(3)
                key_weights(h, 1)
                ahead(4)
                ahead(5)
                attn_out(h, slot)

            pe.wait_ge(x_split, 1)
            for c in range(6):
                project(0, 0, c)
            head(0, 0)
            with pe.Fori(0, (NH - 2) // 2) as i:
                head(2 * i + 1, 1)
                head(2 * i + 2, 0)
            head(NH - 1, 1, last=True)

            def turn(layer_norm):
                for b in range(B):
                    pe.wait_ge(ln_x, B * layer_norm + b + 1)
                    for k in range(DK):
                        ins = pe.transpose(bank[:, 2 * k + b // 4, (b % 4) * S:(b % 4 + 1) * S],
                                           xN[:, b, k * P:(k + 1) * P], ident)
                        if b % 4 == 3:
                            ins.then_inc(xt_psum, 1)

            pe.wait_ge(const_in, 16)
            turn(0)

            def conv(layer, h, slot):
                n = CH * layer + h
                if layer == 0:
                    pe.wait_ge(toep_fix, h + 1)
                else:
                    pe.wait_ge(toep_in[slot], count(8 * (n - slot) + 16))
                pe.wait_ge(kv_done, 2 * n + 1)
                pe.wait_ge(prod_done, count(2 * n - 2))
                diag, off = toep[:, slot, 0:P], toep[:, slot, P:D]
                pe.matmul(bank[:, 2 * slot, :], diag, kv[:, slot, 0, :], start=True, stop=True)\
                    .then_inc(conv_done, 1)
                pe.matmul(bank[:, 2 * slot + 1, :], off, kv[:, slot, 0, :], start=True, stop=False)
                pe.wait_ge(kv_done, 2 * n + 2)
                pe.matmul(bank[:, 2 * slot + 1, :], diag, kv[:, slot, 1, :], start=False, stop=True)\
                    .then_inc(conv_done, 1)

            def turn_back():
                for b in range(B):
                    for l in range(DK):
                        ins = pe.transpose(bank[:, 4 + b // 2, (b % 2) * D + l * P:(b % 2) * D + (l + 1) * P],
                                           oT[:, l, b, :], ident)
                    if b % 2 == 1:
                        ins.then_inc(ot_psum, 1)

            def conv_layer(layer):
                conv(layer, 0, 0)
                conv(layer, 1, 1)
                with pe.Fori(1, CH // 2) as i:
                    conv(layer, 2 * i, 0)
                    conv(layer, 2 * i + 1, 1)

            pe.wait_ge(xt_act, 4)
            conv_layer(0)
            pe.wait_ge(osum_done, 2 * CH)
            turn_back()
            turn(1)

            pe.wait_ge(wres_in, 16)
            pe.wait_ge(xt_act, 8)
            for b in range(B):
                for k in range(DK):
                    ins = pe.matmul(bank[:, 0, b * NE0:(b + 1) * NE0], xT[:, k, b * S:(b + 1) * S],
                                    wres[:, k, R_GATE:R_GATE + NE0], start=(k == 0), stop=(k == DK - 1))
            ins.then_inc(logit_done, 1)
            pe.wait_ge(rw3_done, 1)
            rwt = bank[0:3 * NE0, 1, :].bitcast(BF16)
            for b in range(B):
                ins = pe.transpose(rwt[:, b * S:(b + 1) * S], rw3[:, b, :, :].rearrange("p c e -> p (c e)"),
                                   identb[:])
            ins.then_inc(rwt_psum, 1)

            def down(n, slot, j):
                s = 2 * n + j
                if j == 0:
                    pe.wait_ge(outring_in[slot], 8 * (NH + n - slot) + 16)
                pe.wait_ge(h_done, s + 1)
                for b in range(4 * j, 4 * j + 4):
                    ins = pe.matmul(bank[:, 4 + b // 2, (b % 2) * D:(b % 2 + 1) * D],
                                    HT[:, j, (b % 4) * S:(b % 4 + 1) * S], outring[:, slot, :],
                                    start=(isinstance(n, int) and n == 0 and b % 2 == 0),
                                    stop=(isinstance(n, int) and n == NB0 - 1), skip_group_check=True)
                ins.then_inc(down_done, 1)

            def experts(n, slot):
                pe.wait_ge(w_split, NH + n + 1)
                for j in range(2):
                    s = 2 * n + j
                    pe.wait_ge(silu_done, count(s - 1))
                    split_product(bank[:, 3 * j, :], slot, 0, j).then_inc(g_done, 1)
                    pe.wait_ge(gu_done, s)
                    split_product(bank[:, 1, :], slot, DK * P, j).then_inc(u_done, 1)
                    pe.wait_ge(h_done, s)
                    pe.matmul(bank[:, 2, :], sel[0:3 * NE0, bass.ds(n * P, P)], rwT[0:3 * NE0, halves[j]],
                              start=True, stop=True).then_inc(r_done, 1)
                    if j == 1:
                        down(n, slot, 0)
                    elif not isinstance(n, int) or n > 0:
                        down(n - 1, 1 - slot, 1)

            pe.wait_ge(rwt_done, 1)
            pe.wait_ge(xt_hl, 4)
            two_at_a_time(pe, NB0, experts)
            down(NB0 - 1, 1, 1)
            turn(2)

            pe.wait_ge(wq1_in, 16)
            pe.wait_ge(xt_act, 12)
            n = 0
            for w in range(2):
                for r in range(2):
                    for j in range(2):
                        for col in ((Q_W, Q_WS), (K_W, K_WS))[w]:
                            pe.wait_ge(rope_done, count(n - 3))
                            for k in range(DK):
                                ins = pe.matmul(bank[:, n % 4, :], wq1[:, k, col + r * P:col + (r + 1) * P],
                                                xT[:, k, halves[j]], start=(k == 0), stop=(k == DK - 1))
                            ins.then_inc(qkv_psum, 1)
                            n += 1
            for b in range(B):
                for k in range(DK):
                    ins = pe.matmul(bank[:, 6, b * NKV * HD:(b + 1) * NKV * HD], xT[:, k, b * S:(b + 1) * S],
                                    wq1[:, k, V_W:V_W + NKV * HD], start=(k == 0), stop=(k == DK - 1))
            ins.then_inc(v_psum, 1)
            pe.wait_ge(v_copy, 1)
            pe.wait_ge(yn, 1)
            causal4 = causalb[:].unsqueeze(1).broadcast_to([P, REP, S])

            def scores1(b, slot, g):
                t = NKV * b + g
                if g == 0:
                    pe.wait_ge(qk_ready, b + 1)
                pe.wait_ge(sP, count(t - 3))
                o = bank[:, g % 4, :]
                pe.matmul(o, qe[:, slot, g // 4, g % 4, :], ke[:, slot, g // 4, :, :].rearrange("p q t -> p (q t)"),
                          start=True, stop=False)
                pe.matmul(o.rearrange("p (q s) -> p q s", q=REP), identb[:], causal4, start=False, stop=True)\
                    .then_inc(sS, 1)

            def turn_probs(b, slot, g):
                t = NKV * b + g
                pe.wait_ge(sE, t + 1)
                pe.wait_ge(sV, count(t - 1))
                for q in range(REP):
                    ins = pe.transpose(bank[:, 6 + g % 2, q * S:(q + 1) * S], Pe[:, g % 4, q * S:(q + 1) * S], ident)
                ins.then_inc(sT, 1)

            def weigh(b, slot, g):
                t = NKV * b + g
                pe.wait_ge(sV, t + 1)
                if g == 0:
                    pe.wait_ge(yn, b)
                for q in range(REP):
                    c = (REP * g + q) * (HD + 1)
                    ins = pe.matmul(bank[:, 4 + slot, c:c + HD + 1], PT[:, g % 2, q * S:(q + 1) * S],
                                    Vn[:, b, g, :], start=(g == 0 and q == 0), stop=(g == NKV - 1 and q == REP - 1),
                                    skip_group_check=True)
                ins.then_inc(sY, 1)

            def earlier(step, b, slot, g, back):
                if g >= back:
                    step(b, slot, g - back)
                elif not isinstance(b, int) or b > 0:
                    step(b - 1, 1 - slot, g - back + NKV)

            def attn1(b, slot):
                for g in range(NKV):
                    scores1(b, slot, g)
                    earlier(turn_probs, b, slot, g, 2)
                    earlier(weigh, b, slot, g, 3)

            two_at_a_time(pe, B, attn1)
            turn_probs(B - 1, 1, NKV - 2)
            weigh(B - 1, 1, NKV - 3)
            turn_probs(B - 1, 1, NKV - 1)
            weigh(B - 1, 1, NKV - 2)
            weigh(B - 1, 1, NKV - 1)
            for b in range(B):
                pe.wait_ge(yn, b + 2)
                for k in range(DK):
                    ins = pe.transpose(bank[:, 2 * k + b // 4, (b % 4) * S:(b % 4 + 1) * S],
                                       yN[:, b, k * P:(k + 1) * P], ident)
                    if b % 4 == 3:
                        ins.then_inc(y_psum, 1)
            for b in range(B):
                pe.wait_ge(yt_evac, 2 + 2 * (b // 4))
                for k in range(DK):
                    ins = pe.matmul(bank[:, 4 + b // 2, (b % 2) * D:(b % 2 + 1) * D], yT[:, k, b, :],
                                    wq1[:, k, O_W:O_W + D], start=(k == 0), stop=(k == DK - 1))
                if b % 2 == 1:
                    ins.then_inc(wo_done, 1)
            turn(3)

            pe.wait_ge(xt_act, 16)
            conv_layer(1)
            pe.wait_ge(sum_done, 1)
            turn_back()
            turn(4)

            pe.wait_ge(xt_act, 20)
            for b in range(B):
                for k in range(DK):
                    ins = pe.matmul(bank[:, 4, b * NE1:(b + 1) * NE1], xT[:, k, b * S:(b + 1) * S],
                                    wres[:, k, R_WR:R_WR + NE1], start=(k == 0), stop=(k == DK - 1))
            ins.then_inc(l1_done, 1)
            for n in range(4):
                col = (R_AG, R_AU)[n // 2]
                for k in range(DK):
                    ins = pe.matmul(bank[:, n, :], wres[:, k, col:col + P], xT[:, k, halves[n % 2]],
                                    start=(k == 0), stop=(k == DK - 1))
                ins.then_inc(a_psum, 1)
            pe.wait_ge(l1_sub, 1)
            pe.wait_ge(sel_low_done, 1)
            for n in range(4):
                pe.wait_ge(a_lo, n + 1)
                for e in range(NE1):
                    m = NE1 * n + e
                    if e % 2 == 0:
                        pe.wait_ge(stack_act, count(m // 2 - 1))
                    else:
                        pe.wait_ge(stack_dve, count(m // 2 - 1))
                    pe.matmul(bank[:, 4 + e % 4, :], selp[:, e, 0, :], ahl[:, n % 2, 0, :], start=True, stop=False)
                    pe.matmul(bank[:, 4 + e % 4, :], selp[:, e, 1, :], ahl[:, n % 2, 1, :], start=False, stop=True)\
                        .then_inc(stack_psum, 1)
            pe.wait_ge(stack_act, 2 * NE1)
            pe.wait_ge(stack_dve, 2 * NE1)
            pe.wait_ge(xt_hl, 8)

            def down1(f, slot, c, e):
                pe.wait_ge(f_mul, 18 * f + 9 * c + e + 1)
                first = isinstance(f, int) and f == 0
                if e == 0:
                    for b in range(4 * c, 4 * c + 4):
                        ins = pe.matmul(bank[:, 2 + b // 2, (b % 2) * D:(b % 2 + 1) * D],
                                        HF[:, c, (b % 4) * S:(b % 4 + 1) * S], ring[:, slot, F_WD:F_WD + D],
                                        start=(first and b % 2 == 0), stop=False, skip_group_check=True)
                else:
                    if c == 0 and e == 1:
                        pe.wait_ge(adp_done, f + 1)
                    ins = pe.matmul(bank[:, 6 + c, :], adp[:, slot, e - 1, :], HF[:, (c + e) % 2, :],
                                    start=(first and e == 1), stop=(isinstance(f, int) and f == FB - 1 and e == NE1),
                                    skip_group_check=True)
                ins.then_inc(f_down, 1)

            def two_before(f, slot, c, e):
                n = (NE1 + 1) * c + e - 2
                if n >= 0:
                    return f, slot, n // (NE1 + 1), n % (NE1 + 1)
                return None if isinstance(f, int) and f == 0 else (f - 1, 1 - slot, 1, NE1 + 1 + n)

            def ffn1(f, slot):
                pe.wait_ge(w_split, NH + NB0 + f + 1)
                pe.wait_ge(low_split, f + 1)
                for c in range(2):
                    for e in range(NE1 + 1):
                        k = 18 * f + 9 * c + e
                        for g, done in ((0, fG), (1, fU)):
                            if g == 0:
                                pe.wait_ge(f_silu, k)
                            else:
                                pe.wait_ge(f_mul, k)
                            if e == 0:
                                ins = split_product(bank[:, g, :], slot, g * DK * P, c)
                            else:
                                w = (g * NE1 + e - 1) * P
                                ins = pe.matmul(bank[:, g, :], bstk[:, slot, w:w + P], astk[:, g, e - 1, halves[c]],
                                                start=False, stop=True, skip_group_check=True)
                            ins.then_inc(done, 1)
                            last = two_before(f, slot, c, e)
                            if g == 0 and last:
                                down1(*last)

            two_at_a_time(pe, FB, ffn1)
            down1(FB - 1, 1, 1, NE1 - 1)
            down1(FB - 1, 1, 1, NE1)
            pe.wait_ge(wrep_done, 1)
            for c in range(2):
                for t in range(4):
                    w = rN[:, 2 * c:2 * c + 2, :].rearrange("p a d -> p (a d)")[:, t * P:(t + 1) * P]
                    ins = pe.transpose(bank[:, c, t * P:(t + 1) * P], w, ident)
                ins.then_inc(wt_psum, 1)
            pe.wait_ge(bd_in, 16)
            for b in range(B):
                pe.wait_ge(dw_done, b // 4 + 1)
                ins = pe.matmul(bank[:, 2 + b // 2, (b % 2) * D:(b % 2 + 1) * D], xT[:, 0, b * S:(b + 1) * S], bd[:],
                                start=False, stop=True, skip_group_check=True)
                if b % 2 == 1:
                    ins.then_inc(bd_done, 1)


def kernel(**inputs):
    import numpy as np
    import concourse.bacc as bacc
    from concourse.bass_utils import run_bass_kernel_spmd

    a = {k: np.asarray(v) for k, v in inputs.items()}

    def blocks(w, n):
        return w.reshape(DK, P, n).transpose(1, 0, 2)

    def toeplitz(k):
        padded = np.zeros((CH, P - 1 + D), np.float32)
        padded[:, P - 1:] = k
        at = P - 1 - np.arange(P)[:, None] + np.arange(D)[None, :]
        return padded[:, at]

    w_attn0 = a["L0_attn_w_qkv"].reshape(DK, P, 3, NH, DH).transpose(3, 1, 2, 0, 4).reshape(NH, P, A_WO)

    gu = a["L0_ffn_gate_up_proj"].reshape(NE0, D, 2, INTER).transpose(2, 1, 0, 3).reshape(2, DK, P, NB0, P)
    w_moe = gu.transpose(3, 2, 0, 1, 4).reshape(NB0, P, C_DOWN)

    swap = np.arange(D) ^ 1
    wq, wo = a["L1_attn_wq"], a["L1_attn_wo"]
    wk = np.repeat(a["L1_attn_wk"].reshape(NKV, 1, HD, D), REP, axis=1).reshape(D, D)
    w_attn1 = np.concatenate([blocks(m.T, m.shape[0]) for m in (wq, wq[swap], wk, wk[swap], a["L1_attn_wv"], wo)],
                             axis=2)
    w_res = np.concatenate([blocks(a["L0_ffn_gate"], NE0), blocks(a["L1_ffn_Wr"].T, NE1),
                            blocks(a["L1_ffn_Ag"].reshape(P, D).T, P), blocks(a["L1_ffn_Au"].reshape(P, D).T, P)],
                           axis=2)

    def padded(m):
        z = np.zeros((FB * P, m.shape[1]), np.float32)
        z[:DFF] = m
        return z.reshape(FB, P, m.shape[1])

    def stationary(m):
        return padded(m).reshape(FB, P, DK, P).transpose(0, 3, 2, 1).reshape(FB, P, DK * P)

    def stacked(m):
        rows = padded(m.transpose(1, 0, 2).reshape(DFF, P)).reshape(FB, P, NE1, RANK).transpose(0, 3, 2, 1)
        pair = np.zeros((FB, 2, RANK, NE1, P), np.float32)
        pair[:, 0] = rows
        pair[:, 1, :, 1:] = rows[:, :, :-1]
        return np.tile(pair.reshape(FB, 2 * RANK, NE1 * P), (1, 4, 1))

    w_low = np.concatenate([stacked(a["L1_ffn_Bg"]), stacked(a["L1_ffn_Bu"])], axis=2)
    w_ffn1 = np.concatenate([stationary(a["L1_ffn_Wg"]), stationary(a["L1_ffn_Wu"]),
                             padded(a["L1_ffn_Wd"].T), padded(a["L1_ffn_Ad"].reshape(P, DFF).T)], axis=2)
    w_bd = a["L1_ffn_Bd"].transpose(0, 2, 1).reshape(P, D)

    consts = np.zeros((P, CONST_COLS), np.float32)
    consts[:, C_ID:C_ID + P] = np.eye(P)
    theta = np.float32(1.0) / np.float32(10000.0) ** (np.arange(0, HD, 2, dtype=np.float32) / np.float32(HD))
    freqs = np.arange(S, dtype=np.float32)[None, :] * theta[(np.arange(P) % HD) // 2][:, None]
    consts[:, C_COS:C_COS + P] = np.cos(freqs)
    consts[:, C_SIN:C_SIN + P] = np.sin(freqs) * np.where(np.arange(P) % 2 == 0, -1, 1)[:, None]
    consts[:, C_CAUSAL:C_CAUSAL + P] = np.where(np.arange(P)[None, :] > np.arange(P)[:, None], MASKED, 0)
    consts[:, C_HQ:C_HQ + REP] = (np.arange(P) % 32 // HD)[:, None] == np.arange(REP)[None, :]
    consts[:, C_GROUP:C_GROUP + NKV // 2] = (np.arange(P) // 32)[:, None] == np.arange(NKV // 2)[None, :]
    selp = np.zeros((P, NE1, 2, 4, 2, RANK), np.float32)
    rank = np.arange(RANK)
    for e in range(NE1):
        for part in range(2):
            for quarter in (part, part + 2):
                selp[e * RANK + rank, e, part, quarter, 0, rank] = SCALING
                if e > 0:
                    selp[(e - 1) * RANK + rank, e, part, quarter, 1, rank] = -SCALING
    consts[:, C_IOTA:C_IOTA + NE0] = np.arange(NE0)
    sel3 = np.tile((np.arange(NE0)[:, None] == np.arange(NB0 * P)[None, :] // INTER).astype(np.float32), (3, 1))

    arrays = {
        "x_nat": a["x"].transpose(1, 0, 2), "x_t": a["x"].reshape(TOK, D).T,
        "ctx_t": a["ctx_2048"].transpose(2, 0, 1), "w_attn0": w_attn0,
        "wo_attn0": a["L0_attn_w_o"].reshape(NH, DH, D),
        "toep0": toeplitz(a["L0_xattn_ssm_kernel"]), "skip0": a["L0_xattn_D"],
        "w_res": w_res, "w_moe": w_moe, "w_down0": a["L0_ffn_down_proj"].reshape(NB0, P, D), "sel3": sel3, "w_attn1": w_attn1,
        "toep1": toeplitz(a["L1_xattn_k"]), "bias1": a["fside_S2_0"], "w_ffn1": w_ffn1, "w_low": w_low, "sel_low": selp.reshape(P, LOW), "w_bd": w_bd,
        "consts": consts,
    }
    arrays = {k: np.ascontiguousarray(v) for k, v in arrays.items()}
    nc = bacc.Bacc("TRN2", target_bir_lowering=False, num_devices=1)
    args = [nc.dram_tensor(k, v.shape, mybir.dt.from_np(v.dtype), kind="ExternalInput").ap() for k, v in arrays.items()]
    out = nc.dram_tensor("out", (P, B, D), F32, kind="ExternalOutput").ap()
    decoder_layers(nc, *args, out)
    result = run_bass_kernel_spmd(nc, [arrays], core_ids=[0])
    return np.ascontiguousarray(result.results[0]["out"].transpose(1, 0, 2))
```

```python
from contextlib import ExitStack

import concourse.bass as bass
from concourse import mybir

F32 = mybir.dt.float32
F32R = mybir.dt.float32r
BF16 = mybir.dt.bfloat16
U32 = mybir.dt.uint32
ALU = mybir.AluOpType
ACT = mybir.ActivationFunctionType
AX = mybir.AxisListType.X

P = 128
B, S, D = 8, 128, 256
DK = D // P
TOK = B * S
HALF = TOK // 2
EPS = 1e-5
NH, DH = 16, 128
CH, CI = 16, 8
NE0, TOP0, INTER = 32, 4, 96
NB0 = NE0 * INTER // P
NQ, NKV, HD = 32, 8, 8
REP = NQ // NKV
DFF, NE1, TOP1, RANK = 704, 8, 2, 16
FB = (DFF + P - 1) // P
SCALING = 2.0
MASKED = -1e30
ARENA = 16 * TOK
SHARED = ARENA - 4 * TOK - P

A_WO = 3 * DK * P
C_DOWN = 2 * DK * P
F_BASE = 2 * DK * P
F_WD = F_BASE
F_AD = F_WD + D
F_COLS = F_AD + P
LOW = 2 * NE1 * P
R_GATE, R_WR, R_AG, R_AU = 0, NE0, NE0 + NE1, NE0 + NE1 + P
R_COLS = R_AU + P
Q_W, Q_WS, K_W, K_WS, V_W, O_W = 0, D, 2 * D, 3 * D, 4 * D, 4 * D + NKV * HD
Q_COLS = O_W + D
C_ID, C_COS, C_SIN, C_CAUSAL, C_HQ = 0, P, 2 * P, 3 * P, 4 * P
C_GROUP = C_HQ + REP
C_IOTA = C_GROUP + NKV // 2
CONST_COLS = C_IOTA + NE0


def count(value):
    return max(value, 0) if isinstance(value, int) else value


def settle(eng, sem):
    eng.sem_inc(sem, 1)


def two_at_a_time(eng, n, body):
    body(0, 0)
    body(1, 1)
    with eng.Fori(1, n // 2 - 1) as i:
        body(2 * i, 0)
        body(2 * i + 1, 1)
    body(n - 2, 0)
    body(n - 1, 1)


def decoder_layers(nc, x_nat, x_t, ctx_t, w_attn0, wo_attn0, toep0, skip0, w_res, w_moe, w_down0, sel3,
                   w_attn1, toep1, bias1, w_ffn1, w_low, sel_low, w_bd, consts, out):
    with ExitStack() as ctx:
        def sb(name, shape, dt=F32):
            return ctx.enter_context(nc.sbuf_tensor(name, shape, dt))

        def sem(name):
            return ctx.enter_context(nc.semaphore(name))

        bank = ctx.enter_context(nc.psum_tensor("bank", [P, 8, 512], F32))

        xN = sb("xN", [P, B, D])
        rN = sb("rN", [P, B, D])
        xT = sb("xT", [P, DK, TOK])
        xTh = sb("xTh", [P, DK, TOK], F32R)
        xTl = sb("xTl", [P, DK, TOK], F32R)
        cst = sb("cst", [P, CONST_COLS])
        wres = sb("wres", [P, DK, R_COLS])
        agh = sb("agh", [P, DK, 2 * P], F32R)
        agl = sb("agl", [P, DK, 2 * P], F32R)
        bd = sb("bd", [P, D])
        ring = sb("ring", [P, 2, F_COLS])
        outring = sb("outring", [P, 2, D])
        ringh = sb("ringh", [P, 2, A_WO], F32R)
        ringl = sb("ringl", [P, 2, A_WO], F32R)
        st = sb("st", [P, B, 6])
        mv = sb("mv", [P, B, 2])
        ve = sb("ve", [P, B])
        sd = sb("sd", [P, B])
        rstd = sb("rstd", [P, B])
        nmean = sb("nmean", [P, B // 2])
        shift = sb("shift", [P, B // 2])
        ident = cst[:, C_ID:C_ID + P]
        lowraw = sb("lowraw", [P, 2, LOW])
        SF = sb("SF", [P, 2, 512])
        HF = sb("HF", [P, 2, 512])

        m1 = sb("m1", [P, B])
        r1 = sb("r1", [P, B])
        s1 = sb("s1", [P, B])
        top8 = sb("top8", [P, B, 8])
        idx8 = sb("idx8", [P, B, 8], U32)
        idxf = sb("idxf", [P, B, 8])
        we1 = sb("we1", [P, B, NE1])
        hit1 = sb("hit1", [P, B, NE1])
        rest1 = sb("rest1", [P, B, NE1])

        wrep = rN[:, 0:B // 2, :].rearrange("p n (c r) -> p (n c) r", r=RANK)
        with ExitStack() as last_stage:
            def sb_last(name, shape, dt=F32):
                return last_stage.enter_context(nc.sbuf_tensor(name, shape, dt))
            astk = sb_last("astk", [P, 2, NE1, TOK], F32R)
            bstk = sb_last("bstk", [P, 2, LOW], F32R)
            ahl = sb_last("ahl", [P, 2, 2, HALF], F32R)
            selp = sb_last("selp", [P, NE1, 2, P], F32R)
            adp = sb_last("adp", [P, 2, NE1, P])

        with ExitStack() as first_stages:
            def sb_first(name, shape, dt=F32R):
                return first_stages.enter_context(nc.sbuf_tensor(name, shape, dt))
            sb_first("arena_start", [P, SHARED], F32)
            ones = sb_first("ones", [P, P])
            Eh = sb_first("Eh", [P, TOK])
            El = sb_first("El", [P, TOK])
            VTch = sb_first("VTch", [P, TOK])
            VTcl = sb_first("VTcl", [P, TOK])

        arena = sb("arena", [P, ARENA])
        cT = sb("cT", [P, DK, B, S])
        wq1 = sb("wq1", [P, DK, Q_COLS])
        cut = [0]
        limit = [SHARED]

        def take(cols, fresh=False):
            if fresh:
                cut[0] = 0
            a = arena[:, cut[0]:cut[0] + cols]
            cut[0] += cols
            assert cut[0] <= limit[0]
            return a

        QT = take(2 * TOK, True).rearrange("p (s t) -> p s t", s=2)
        KT = take(2 * TOK).rearrange("p (s t) -> p s t", s=2)
        VT = take(2 * TOK).rearrange("p (s t) -> p s t", s=2)
        VTc = take(TOK)
        E = take(TOK)
        outh = sb("outh", [P, 2, D], F32R)
        outl = sb("outl", [P, 2, D], F32R)
        nmax = sb("nmax", [P, B])
        mx = sb("mx", [P, B])
        rowsum = sb("rowsum", [P, B])
        rinv = sb("rinv", [P, B])
        oT = take(2 * TOK, True).rearrange("p (l b s) -> p l b s", l=2, b=B)
        kv = take(4 * 512).rearrange("p (s m n) -> p s m n", s=2, m=2)
        prod = take(2 * 512).rearrange("p (s n) -> p s n", s=2)
        bx1 = take(2 * TOK).rearrange("p (l b s) -> p l b s", l=2, b=B)
        bx1v = take(2 * TOK).rearrange("p (l b s) -> p l b s", l=2, b=B)
        skr = take(2 * B * CH).rearrange("p (l n) -> p l n", l=2)
        toep = sb("toep", [P, 4, D])
        dskip = sb("dskip", [P, CH])
        bias_bc = sb("bias_bc", [P, S])
        SG = take(2 * 512, True).rearrange("p (s n) -> p s n", s=2)
        H1 = take(2 * 512).rearrange("p (s n) -> p s n", s=2)
        HT = take(2 * 512).rearrange("p (s n) -> p s n", s=2)
        e0 = take(B * NE0).rearrange("p (b e) -> p b e", b=B)
        rest = take(B * NE0).rearrange("p (b e) -> p b e", b=B)
        hit = take(B * NE0).rearrange("p (b e) -> p b e", b=B)
        rw = take(B * NE0).rearrange("p (b e) -> p b e", b=B)
        rwT = sb("rwT", [P, TOK], BF16)
        rw3 = sb("rw3", [P, B, 3, NE0], BF16)
        sel = sb("sel", [P, NB0 * P], BF16)
        selstage = take(NB0 * P)
        HTh = Eh[:].rearrange("p (s n) -> p s n", s=2)
        HTl = El[:].rearrange("p (s n) -> p s n", s=2)
        identb = sb("identb", [P, P], BF16)
        causalb = sb("causalb", [P, P], BF16)
        wqh, wql = (VTch, VTcl), (Eh, El)
        limit[0] = ARENA - 4 * TOK
        TC = take(4 * TOK, True).rearrange("p (w r b t) -> p w r b t", w=2, r=2, b=B)
        TS = take(4 * TOK).rearrange("p (w r b t) -> p w r b t", w=2, r=2, b=B)
        qb = take(2 * 2 * S).rearrange("p (s r t) -> p s r t", s=2, r=2)
        kb = take(2 * 2 * S).rearrange("p (s r t) -> p s r t", s=2, r=2)
        qh = outh[:].rearrange("p s (r t) -> p s r t", r=2)
        kh = outl[:].rearrange("p s (r t) -> p s r t", r=2)
        qeh, qel = (x[:].rearrange("p s (r g t) -> p s r g t", r=2, g=NKV // 2) for x in (xTh, xTl))
        keh = [x[:].rearrange("p (r q t) -> p r q t", r=2, q=REP) for x in (Eh, El)]
        kel = [x[:].rearrange("p (r q t) -> p r q t", r=2, q=REP) for x in (VTch, VTcl)]
        Pe = take(4 * 512).rearrange("p (s n) -> p s n", s=4)
        PT = take(2 * 512).rearrange("p (s n) -> p s n", s=2)
        mx1 = sb("mx1", [P, 4, REP])
        Vn = sb("Vn", [P, B, NKV, HD + 1])
        yr = sb("yr", [P, 2, NQ])
        yN = rN
        yT = TC[:, 0, :, :, :]

        x_in = sem("x_in")
        xt_in = sem("xt_in")
        const_in = sem("const_in")
        ctx_in = sem("ctx_in")
        wres_in = sem("wres_in")
        wq1_in = sem("wq1_in")
        bd_in = sem("bd_in")
        sel_in = sem("sel_in")
        skip0_in = sem("skip0_in")
        bias1_in = sem("bias1_in")
        x_split = sem("x_split")
        w_split = sem("w_split")
        proj_done = sem("proj_done")
        act_evac = sem("act_evac")
        dve_evac = sem("dve_evac")
        s_done = sem("s_done")
        mx_done = sem("mx_done")
        nmax_done = sem("nmax_done")
        exp_done = sem("exp_done")
        rinv_done = sem("rinv_done")
        csum_done = sem("csum_done")
        vc_done = sem("vc_done")
        en_done = sem("en_done")
        eh_done = sem("eh_done")
        el_done = sem("el_done")
        vh_done = sem("vh_done")
        vl_done = sem("vl_done")
        ones_done = sem("ones_done")
        wo_hi = sem("wo_hi")
        wo_split = sem("wo_split")
        hh_done = sem("hh_done")
        hl_done = sem("hl_done")
        out0_done = sem("out0_done")
        out0_banks = sem("out0_banks")
        sum_done = sem("sum_done")
        ln_var = sem("ln_var")
        ln_sd = sem("ln_sd")
        ln_scale = sem("ln_scale")
        ln_x0 = sem("ln_x0")
        ln_x1 = sem("ln_x1")
        xt_high = sem("xt_high")
        xt_psum = sem("xt_psum")
        xt_act = sem("xt_act")
        xt_hl = sem("xt_hl")
        toep_fix = sem("toep_fix")
        kv_done = sem("kv_done")
        conv_done = sem("conv_done")
        prod_done = sem("prod_done")
        osum_done = sem("osum_done")
        ot_psum = sem("ot_psum")
        bx1_done = sem("bx1_done")
        bx1v_done = sem("bx1v_done")
        skr_done = sem("skr_done")
        skip_add = sem("skip_add")
        logit_done = sem("logit_done")
        logits_shifted = sem("logits_shifted")
        logits_exp = sem("logits_exp")
        rw3_done = sem("rw3_done")
        rwt_psum = sem("rwt_psum")
        rwt_done = sem("rwt_done")
        g_done = sem("g_done")
        u_done = sem("u_done")
        r_done = sem("r_done")
        silu_done = sem("silu_done")
        gu_done = sem("gu_done")
        h_done = sem("h_done")
        down_done = sem("down_done")
        qkv_psum = sem("qkv_psum")
        rope_done = sem("rope_done")
        v_psum = sem("v_psum")
        vn_ones = sem("vn_ones")
        ke_ready = sem("ke_ready")
        kb_done = sem("kb_done")
        q_done = sem("q_done")
        qe_ready = sem("qe_ready")
        qh_done = sem("qh_done")
        wq_hi = sem("wq_hi")
        wq_split = sem("wq_split")
        ql_done = sem("ql_done")
        kh_done = sem("kh_done")
        kl_done = sem("kl_done")
        scores1_done = sem("scores1_done")
        max1_done = sem("max1_done")
        shifted = sem("shifted")
        exp1_done = sem("exp1_done")
        turned = sem("turned")
        turned_out = sem("turned_out")
        weighed = sem("weighed")
        y_rec = sem("y_rec")
        yn_done = sem("yn_done")
        y_psum = sem("y_psum")
        yt_evac = sem("yt_evac")
        wo_done = sem("wo_done")
        l1_done = sem("l1_done")
        l1_sub = sem("l1_sub")
        l1_exp = sem("l1_exp")
        a_psum = sem("a_psum")
        a_hi = sem("a_hi")
        ag_hi = sem("ag_hi")
        wres_split = sem("wres_split")
        a_lo = sem("a_lo")
        stack_psum = sem("stack_psum")
        stack_act = sem("stack_act")
        stack_dve = sem("stack_dve")
        sel_low_in = sem("sel_low_in")
        sel_low_done = sem("sel_low_done")
        low_hi = sem("low_hi")
        low_split = sem("low_split")
        gate1_done = sem("gate1_done")
        up1_done = sem("up1_done")
        f_silu = sem("f_silu")
        f_mul = sem("f_mul")
        f_down = sem("f_down")
        adp_zero = sem("adp_zero")
        adp_done = sem("adp_done")
        we1_done = sem("we1_done")
        wrep_done = sem("wrep_done")
        wt_psum = sem("wt_psum")
        wt_evac = sem("wt_evac")
        dw_done = sem("dw_done")
        bd_done = sem("bd_done")
        dve_chain = sem("dve_chain")
        out_done = sem("out_done")
        hi_done = sem("hi_done")
        hi_first = sem("hi_first")
        const_conv = sem("const_conv")
        pool_settled = sem("pool_settled")
        sp_settled = sem("sp_settled")
        ring_in = [sem("ring_in0"), sem("ring_in1")]
        toep_in = [sem("toep_in0"), sem("toep_in1"), sem("toep_in2"), sem("toep_in3")]
        lowraw_in = [sem("lowraw_in0"), sem("lowraw_in1")]
        outring_in = [sem("outring_in0"), sem("outring_in1")]


        block = ctx.enter_context(nc.Block())

        @block.sync
        def _(sp):
            sp.dma_start(xT[:], x_t.rearrange("(k p) t -> p k t", p=P)).then_inc(xt_in, 16)

            def load_attn0(h, slot):
                sp.wait_ge(w_split, count(h - 1))
                settle(sp, sp_settled)
                sp.dma_start(ring[:, slot, 0:A_WO], w_attn0[h, :, :]).then_inc(ring_in[slot], 16)
                sp.wait_ge(wo_split, count(h - 1))
                settle(sp, sp_settled)
                sp.dma_start(outring[:, slot, :], wo_attn0[h, :, :]).then_inc(outring_in[slot], 16)

            load_attn0(0, 0)
            load_attn0(1, 1)
            sp.dma_start(xN[:], x_nat).then_inc(x_in, 16)
            sp.dma_start(cst[:], consts).then_inc(const_in, 16)
            sp.dma_start(cT[:], ctx_t.rearrange("(k p) b s -> p k b s", p=P)).then_inc(ctx_in, 16)
            sp.dma_start(wres[:], w_res).then_inc(wres_in, 16)
            sp.dma_start(wq1[:], w_attn1).then_inc(wq1_in, 16)
            sp.dma_start(bd[:], w_bd).then_inc(bd_in, 16)
            sp.dma_start(dskip[:], skip0.partition_broadcast(P)).then_inc(skip0_in, 16)
            sp.dma_start(bias_bc[:], bias1.partition_broadcast(P)).then_inc(bias1_in, 16)
            with sp.Fori(1, NH // 2) as i:
                load_attn0(2 * i, 0)
                load_attn0(2 * i + 1, 1)

            def load_toep(src, layer, h, slot):
                sp.wait_ge(conv_done, count(2 * (CH * layer + h - 3)))
                settle(sp, sp_settled)
                flat = src[h, :, :]
                sp.dma_start(toep[:, slot, :], flat).then_inc(toep_in[slot], 16)

            def load_moe(n, slot):
                sp.wait_ge(w_split, NH + n - 1)
                settle(sp, sp_settled)
                sp.dma_start(ring[:, slot, 0:C_DOWN], w_moe[n, :, :]).then_inc(ring_in[slot], 16)
                sp.wait_ge(wo_split, NH + n - 1)
                settle(sp, sp_settled)
                sp.dma_start(outring[:, slot, :], w_down0[n, :, :]).then_inc(outring_in[slot], 16)

            def load_ffn1(f, slot):
                if isinstance(f, int) and f < 2:
                    sp.wait_ge(w_split, NH + NB0 + f - 1)
                else:
                    sp.wait_ge(f_down, 18 * (f - 1))
                settle(sp, sp_settled)
                sp.dma_start(ring[:, slot, :], w_ffn1[f, :, :]).then_inc(ring_in[slot], 16)

            def load_low(f, slot):
                sp.wait_ge(low_split, count(4 * (f - 1)))
                settle(sp, sp_settled)
                sp.dma_start(lowraw[:, slot, :], w_low[f, :, :]).then_inc(lowraw_in[slot], 16)

            for h in range(4):
                load_toep(toep0, 0, h, h)
            load_moe(0, 0)
            load_moe(1, 1)
            with sp.Fori(1, CH // 4) as i:
                for slot in range(4):
                    load_toep(toep0, 0, 4 * i + slot, slot)
            sp.wait_ge(ot_psum, 4)
            sp.dma_start(selstage[0:3 * NE0, :], sel3).then_inc(sel_in, 16)
            for h in range(4):
                load_toep(toep1, 1, h, h)
            with sp.Fori(1, NB0 // 2) as i:
                load_moe(2 * i, 0)
                load_moe(2 * i + 1, 1)
            load_ffn1(0, 0)
            load_ffn1(1, 1)
            sp.dma_start(lowraw[:, 1, :], sel_low).then_inc(sel_low_in, 16)
            load_low(0, 0)
            with sp.Fori(1, CH // 4) as i:
                for slot in range(4):
                    load_toep(toep1, 1, 4 * i + slot, slot)
            sp.wait_ge(sel_low_done, 1)
            load_low(1, 1)
            with sp.Fori(1, FB // 2) as i:
                load_low(2 * i, 0)
                load_ffn1(2 * i, 0)
                load_low(2 * i + 1, 1)
                load_ffn1(2 * i + 1, 1)
            for j, done in ((0, ln_x0), (1, ln_x1)):
                sp.wait_ge(done, 6 * B // 2)
                half = slice(j * B // 2, (j + 1) * B // 2)
                sp.dma_start(out[:, half, :], xN[:, half, :]).then_inc(out_done, 16)
            sp.wait_ge(out_done, 32)

        @block.gpsimd
        def _(pool):
            def split_attn0(h, slot):
                pool.wait_ge(ring_in[slot], 8 * (h - slot) + 16)
                pool.wait_ge(proj_done, count(6 * (h - 1)))
                settle(pool, pool_settled)
                if isinstance(h, int) and h == 0:
                    pool.wait_ge(hi_first, 1)
                else:
                    pool.tensor_copy(ringh[:, slot, :], ring[:, slot, 0:A_WO]).then_inc(hi_done, 1)
                    pool.wait_ge(hi_done, h)
                pool.tensor_tensor(ringl[:, slot, :], ring[:, slot, 0:A_WO], ringh[:, slot, :].bitcast(F32),
                                   ALU.subtract).then_inc(w_split, 1)

            split_attn0(0, 0)
            split_attn0(1, 1)
            with pool.Fori(1, NH // 2) as i:
                split_attn0(2 * i, 0)
                split_attn0(2 * i + 1, 1)

            def split_moe(n, slot):
                pool.wait_ge(ring_in[slot], 8 * (NH + n - slot) + 16)
                if isinstance(n, int) and n < 2:
                    pool.wait_ge(proj_done, 6 * NH)
                else:
                    pool.wait_ge(u_done, count(2 * (n - 1)))
                settle(pool, pool_settled)
                pool.tensor_copy(ringh[:, slot, 0:C_DOWN], ring[:, slot, 0:C_DOWN]).then_inc(hi_done, 1)
                pool.wait_ge(hi_done, NH + n)
                pool.tensor_tensor(ringl[:, slot, 0:C_DOWN], ring[:, slot, 0:C_DOWN],
                                   ringh[:, slot, 0:C_DOWN].bitcast(F32), ALU.subtract).then_inc(w_split, 1)

            def conv_products(layer, h, slot, left, right):
                pool.wait_ge(conv_done, count(2 * (CH * layer + h - 1)))
                for m in range(DK):
                    a = left[:, m, :, bass.ds(CI * h, CI)].unsqueeze(3).broadcast_to([P, B, CI, CI])
                    c = right[:, m, :, bass.ds(CI * h, CI)].unsqueeze(2).broadcast_to([P, B, CI, CI])
                    o = kv[:, slot, m, :].rearrange("p (b i j) -> p b i j", b=B, i=CI)
                    pool.tensor_tensor(o, a, c, ALU.mult).then_inc(kv_done, 1)

            xTv = xT[:].rearrange("p k (b s) -> p k b s", b=B)
            pool.wait_ge(ctx_in, 16)
            pool.wait_ge(out0_banks, 4)
            conv_products(0, 0, 0, cT, cT)
            conv_products(0, 1, 1, cT, cT)
            with pool.Fori(1, CH // 2) as i:
                conv_products(0, 2 * i, 0, cT, cT)
                conv_products(0, 2 * i + 1, 1, cT, cT)
            split_moe(0, 0)
            split_moe(1, 1)
            pool.wait_ge(wq1_in, 16)
            for k in range(DK):
                ins = pool.tensor_copy(wqh[k][:], wq1[:, k, 0:4 * D])
            ins.then_inc(wq_hi, 1)
            with pool.Fori(1, NB0 // 2) as i:
                split_moe(2 * i, 0)
                split_moe(2 * i + 1, 1)

            pool.wait_ge(down_done, 2 * NB0)
            pool.wait_ge(wq_hi, 1)
            for k in range(DK):
                pool.tensor_tensor(wql[k][:], wq1[:, k, 0:4 * D], wqh[k][:].bitcast(F32), ALU.subtract)\
                    .then_inc(wq_split, 1)

            pool.wait_ge(wres_in, 16)
            for k in range(DK):
                ins = pool.tensor_copy(agh[:, k, :], wres[:, k, R_AG:R_AG + 2 * P])
            ins.then_inc(ag_hi, 1)
            pool.wait_ge(ag_hi, 1)
            for k in range(DK):
                ins = pool.tensor_tensor(agl[:, k, :], wres[:, k, R_AG:R_AG + 2 * P], agh[:, k, :].bitcast(F32),
                                         ALU.subtract)
            ins.then_inc(wres_split, 1)

            hq = cst[:, C_HQ:C_HQ + REP].unsqueeze(2).broadcast_to([P, REP, S])

            def spread(b, slot):
                pool.wait_ge(scores1_done, count(NKV * (b - 1)))
                pool.tensor_tensor(kb[:, slot, :, :], TC[:, 1, :, b, :], TS[:, 1, :, b, :], ALU.add)\
                    .then_inc(kb_done, 1)
                pool.wait_ge(kb_done, b + 1)
                settle(pool, pool_settled)
                pool.tensor_copy(kh[:, slot, :, :], kb[:, slot, :, :]).then_inc(kh_done, 1)
                pool.wait_ge(kh_done, b + 1)
                pool.tensor_tensor(kb[:, slot, :, :], kb[:, slot, :, :], kh[:, slot, :, :].bitcast(F32), ALU.subtract)\
                    .then_inc(kl_done, 1)
                pool.wait_ge(kl_done, b + 1)
                for r in range(2):
                    k1 = kh[:, slot, r, :].bitcast(F32).unsqueeze(1).broadcast_to([P, REP, S])
                    pool.tensor_tensor(keh[slot][:, r, :, :], k1, hq, ALU.mult)
                    k1 = kb[:, slot, r, :].unsqueeze(1).broadcast_to([P, REP, S])
                    pool.tensor_tensor(kel[slot][:, r, :, :], k1, hq, ALU.mult).then_inc(ke_ready, 1)

            pool.wait_ge(rope_done, 16)
            spread(0, 0)
            spread(1, 1)
            with pool.Fori(1, B // 2) as i:
                spread(2 * i, 0)
                spread(2 * i + 1, 1)

            pool.wait_ge(wo_done, 4)
            pool.wait_ge(bias1_in, 16)
            bb = bias_bc[:].unsqueeze(1).broadcast_to([P, B, S])
            for m in range(DK):
                ins = pool.tensor_tensor(bx1[:, m, :, :], cT[:, m, :, :], bb, ALU.mult)
            ins.then_inc(bx1_done, 1)
            pool.wait_ge(xt_act, 16)
            pool.wait_ge(bx1_done, 1)
            conv_products(1, 0, 0, xTv, cT)
            conv_products(1, 1, 1, xTv, cT)
            for m in range(DK):
                ins = pool.tensor_tensor(bx1v[:, m, :, :], bx1[:, m, :, :], xTv[:, m, :, :], ALU.mult)
            ins.then_inc(bx1v_done, 1)
            with pool.Fori(1, CH // 2) as i:
                conv_products(1, 2 * i, 0, xTv, cT)
                conv_products(1, 2 * i + 1, 1, xTv, cT)
            pool.wait_ge(skr_done, 1)
            for m in range(DK):
                sk = skr[:, m, :].unsqueeze(2).broadcast_to([P, B * CH, CI])
                ins = pool.tensor_tensor(bx1[:, m, :, :].rearrange("p b (h j) -> p (b h) j", j=CI),
                                         cT[:, m, :, :].rearrange("p b (h j) -> p (b h) j", j=CI), sk, ALU.mult)
            ins.then_inc(skip_add, 1)

            pool.wait_ge(a_psum, 1)
            pool.memset(adp[:], 0.0).then_inc(adp_zero, 1)
            pool.wait_ge(adp_zero, 1)

            def split_ffn1(f, slot):
                pool.wait_ge(ring_in[slot], 8 * (NH + NB0 + f - slot) + 16)
                pool.wait_ge(up1_done, count(18 * (f - 1)))
                settle(pool, pool_settled)
                pool.tensor_copy(ringh[:, slot, 0:F_BASE], ring[:, slot, 0:F_BASE]).then_inc(hi_done, 1)
                pool.wait_ge(hi_done, NH + NB0 + f)
                pool.tensor_tensor(ringl[:, slot, 0:F_BASE], ring[:, slot, 0:F_BASE],
                                   ringh[:, slot, 0:F_BASE].bitcast(F32), ALU.subtract).then_inc(w_split, 1)
                pool.wait_ge(f_down, count(18 * (f - 1)))
                settle(pool, pool_settled)
                pool.tensor_copy(adp[:, slot, :, :].rearrange("p e (c r) -> p (e c) r", r=RANK)[:, ::NE1 + 1, :],
                                 ring[:, slot, F_AD:F_AD + P].rearrange("p (e r) -> p e r", r=RANK))\
                    .then_inc(adp_done, 1)

            split_ffn1(0, 0)
            split_ffn1(1, 1)
            with pool.Fori(1, FB // 2) as i:
                split_ffn1(2 * i, 0)
                split_ffn1(2 * i + 1, 1)

        @block.scalar
        def _(act):
            act.wait_ge(ring_in[0], 16)
            act.activation(ringh[:, 0, :], ring[:, 0, 0:A_WO], ACT.Copy).then_inc(hi_first, 1)

            def evac_q(h, slot, j):
                act.wait_ge(proj_done, 6 * h + 1 + j)
                act.wait_ge(s_done, count(2 * (h - 1)))
                act.activation(QT[:, slot, j * HALF:(j + 1) * HALF], bank[:, j, :], ACT.Copy)\
                    .then_inc(act_evac, 1)

            def evac_v(h, slot, j):
                act.wait_ge(proj_done, 6 * h + 5 + j)
                act.wait_ge(vc_done, count(2 * (h - 1)))
                act.activation(VT[:, slot, j * HALF:(j + 1) * HALF], bank[:, j, :], ACT.Copy)\
                    .then_inc(act_evac, 1)

            def exps(h, j):
                act.wait_ge(nmax_done, 2 * h + j + 1)
                act.wait_ge(el_done, count(2 * (h - 1) + j + 1))
                for b in range(4 * j, 4 * j + 4):
                    ins = act.activation(E[:, b * S:(b + 1) * S], bank[:, 2 + j, (b % 4) * S:(b % 4 + 1) * S], ACT.Exp,
                                         bias=nmax[:, b:b + 1], scale=DH ** -0.5, accum_out=rowsum[:, b:b + 1])
                ins.then_inc(exp_done, 1)

            def high_e(h, j):
                act.wait_ge(en_done, 2 * h + j + 1)
                act.wait_ge(csum_done, count(2 * (h - 1) + j + 1))
                half = slice(j * HALF, (j + 1) * HALF)
                act.activation(Eh[:, half], E[:, half], ACT.Copy).then_inc(eh_done, 1)

            def high_v(h, j):
                act.wait_ge(vc_done, 2 * h + j + 1)
                act.wait_ge(out0_done, h)
                half = slice(j * HALF, (j + 1) * HALF)
                act.activation(VTch[:, half], VTc[:, half], ACT.Copy).then_inc(vh_done, 1)

            def high_out(n, slot, used, at):
                act.wait_ge(outring_in[slot], 8 * (n - slot) + 16)
                act.wait_ge(used, at)
                act.activation(outh[:, slot, :], outring[:, slot, :], ACT.Copy).then_inc(wo_hi, 1)

            def head(h, slot):
                last = isinstance(h, int) and h == NH - 1
                if not last:
                    evac_q(h + 1, 1 - slot, 0)
                exps(h, 0)
                if not last:
                    evac_q(h + 1, 1 - slot, 1)
                exps(h, 1)
                high_e(h, 0)
                high_e(h, 1)
                high_out(h, slot, out0_done, count(h - 1))
                high_v(h, 0)
                high_v(h, 1)
                if not last:
                    evac_v(h + 1, 1 - slot, 0)
                    evac_v(h + 1, 1 - slot, 1)

            for j in range(2):
                evac_q(0, 0, j)
            for j in range(2):
                evac_v(0, 0, j)
            two_at_a_time(act, NH, head)

            def norm_and_turn(layer_norm, turn=True, high=False):
                def deviations(j):
                    half = slice(j * B // 2, (j + 1) * B // 2)
                    act.wait_ge(ln_var, 2 * layer_norm + j + 1)
                    act.activation(sd[:, half], ve[:, half], ACT.Sqrt).then_inc(ln_sd, 1)

                deviations(0)
                act.wait_ge(ln_scale, layer_norm + 1)
                for b in range(B // 2):
                    act.activation(xN[:, b, :], rN[:, b, :], ACT.Identity, bias=shift[:, b:b + 1],
                                   scale=rstd[:, b:b + 1]).then_inc(ln_x0, 1)
                deviations(1)
                if not turn:
                    return
                for n, (k, j) in enumerate(((0, 0), (1, 0), (0, 1), (1, 1))):
                    act.wait_ge(xt_psum, 4 * layer_norm + n + 1)
                    act.activation(xT[:, k, j * HALF:(j + 1) * HALF], bank[:, 2 * k + j, :], ACT.Copy)\
                        .then_inc(xt_act, 1)
                    if high:
                        act.activation(xTh[:, k, j * HALF:(j + 1) * HALF], bank[:, 2 * k + j, :], ACT.Copy)\
                            .then_inc(xt_high, 1)

            norm_and_turn(0)
            norm_and_turn(1, high=True)

            act.wait_ge(logits_shifted, 1)
            act.activation(e0, e0, ACT.Exp).then_inc(logits_exp, 1)

            def silus(n, slot):
                for j in range(2):
                    s = 2 * n + j
                    act.wait_ge(g_done, s + 1)
                    act.wait_ge(gu_done, count(s - 1))
                    act.activation(SG[:, j, :], bank[:, 3 * j, :], ACT.Silu).then_inc(silu_done, 1)
                    if j == 0:
                        if isinstance(n, int) and n < 2:
                            high_out(NH + n, slot, out0_banks, 4)
                        else:
                            high_out(NH + n, slot, down_done, 2 * (n - 1))
                    act.wait_ge(h_done, s + 1)
                    act.wait_ge(down_done, count(s - 1))
                    act.activation(HTh[:, j, :], HT[:, j, :], ACT.Copy).then_inc(hh_done, 1)

            two_at_a_time(act, NB0, silus)
            norm_and_turn(2, high=True)

            def evac_pt(b, g):
                t = NKV * b + g
                act.wait_ge(turned, t + 1)
                act.wait_ge(weighed, count(t - 1))
                act.activation(PT[:, g % 2, :], bank[:, 6 + g % 2, :], ACT.Copy).then_inc(turned_out, 1)

            def attn1(b, slot):
                for g in range(NKV):
                    t = NKV * b + g
                    if g > 1:
                        evac_pt(b, g - 2)
                    elif not isinstance(b, int) or b > 0:
                        evac_pt(b - 1, NKV - 2 + g)
                    act.wait_ge(shifted, t + 1)
                    act.activation(Pe[:, g % 4, :], Pe[:, g % 4, :], ACT.Exp, scale=HD ** -0.5).then_inc(exp1_done, 1)

            two_at_a_time(act, B, attn1)
            evac_pt(B - 1, NKV - 2)
            evac_pt(B - 1, NKV - 1)
            for n, (k, j) in enumerate(((0, 0), (1, 0), (0, 1), (1, 1))):
                act.wait_ge(y_psum, n + 1)
                act.activation(yT[:, k, 4 * j:4 * j + 4, :], bank[:, 2 * k + j, :].rearrange("p (b t) -> p b t", b=4),
                               ACT.Copy).then_inc(yt_evac, 1)
            norm_and_turn(3)
            norm_and_turn(4, high=True)
            def high_input(n):
                act.wait_ge(a_psum, n + 1)
                act.wait_ge(stack_psum, count(NE1 * (n - 1)))
                act.activation(ahl[:, n % 2, 0, :], bank[:, n, :], ACT.Copy).then_inc(a_hi, 1)

            high_input(0)
            high_input(1)
            act.wait_ge(l1_sub, 1)
            act.activation(we1[:], we1[:], ACT.Exp).then_inc(l1_exp, 1)
            for n in range(4):
                for e in range(0, NE1, 2):
                    act.wait_ge(stack_psum, NE1 * n + e + 1)
                    act.activation(astk[:, n // 2, e, (n % 2) * HALF:(n % 2 + 1) * HALF], bank[:, 4 + (e + 1) % 4, :],
                                   ACT.Copy).then_inc(stack_act, 1)
                if n < 2:
                    high_input(n + 2)

            def silus1(f, slot):
                for c in range(2):
                    for e in range(NE1 + 1):
                        k = 18 * f + 9 * c + e
                        act.wait_ge(gate1_done, k + 1)
                        act.wait_ge(f_mul, count(k - 1))
                        act.activation(SF[:, (c + e) % 2, :], bank[:, 0, :], ACT.Silu).then_inc(f_silu, 1)

            two_at_a_time(act, FB, silus1)
            for c in range(2):
                act.wait_ge(wt_psum, c + 1)
                act.activation(SF[:, c, :], bank[:, c, :], ACT.Copy).then_inc(wt_evac, 1)
            norm_and_turn(5, turn=False)

        @block.vector
        def _(dve):
            chained = [0]

            def link(ins):
                chained[0] += 1
                ins.then_inc(dve_chain, 1)
                dve.wait_ge(dve_chain, chained[0])

            dve.wait_ge(xt_in, 16)
            for k in range(DK):
                ins = dve.tensor_copy(xTh[:, k, :], xT[:, k, :])
            link(ins)
            for k in range(DK):
                ins = dve.tensor_tensor(xTl[:, k, :], xT[:, k, :], xTh[:, k, :].bitcast(F32), ALU.subtract)
            ins.then_inc(x_split, 1)
            dve.memset(Vn[:], 1.0).then_inc(vn_ones, 1)
            dve.wait_ge(vn_ones, 1)
            dve.tensor_copy(ones[:], Vn[:].rearrange("p b g d -> p (b g d)")[:, 0:P]).then_inc(ones_done, 1)

            def evac_k(h, slot, j):
                dve.wait_ge(proj_done, 6 * h + 3 + j)
                dve.wait_ge(s_done, count(2 * (h - 1)))
                dve.tensor_copy(KT[:, slot, j * HALF:(j + 1) * HALF], bank[:, j, :]).then_inc(dve_evac, 1)

            def row_max(h, j):
                dve.wait_ge(s_done, 2 * h + j + 1)
                dve.tensor_reduce(mx[:, 4 * j:4 * j + 4], bank[:, 2 + j, :].rearrange("p (b k) -> p b k", b=4),
                                  AX, ALU.max).then_inc(mx_done, 1)
                dve.wait_ge(mx_done, 2 * h + j + 1)
                dve.tensor_scalar(nmax[:, 4 * j:4 * j + 4], mx[:, 4 * j:4 * j + 4], -(DH ** -0.5), None, ALU.mult)\
                    .then_inc(nmax_done, 1)

            def recip(h, j):
                dve.wait_ge(exp_done, 2 * h + j + 1)
                dve.reciprocal(rinv[:, 4 * j:4 * j + 4], rowsum[:, 4 * j:4 * j + 4]).then_inc(rinv_done, 1)
                dve.wait_ge(rinv_done, 2 * h + j + 1)
                e = E[:, j * HALF:(j + 1) * HALF].rearrange("p (b k) -> p b k", b=4)
                dve.tensor_tensor(e, e, rinv[:, 4 * j:4 * j + 4].unsqueeze(2).broadcast_to([P, 4, S]), ALU.mult)\
                    .then_inc(en_done, 1)

            def low_e(h, j):
                dve.wait_ge(eh_done, 2 * h + j + 1)
                half = slice(j * HALF, (j + 1) * HALF)
                dve.tensor_tensor(El[:, half], E[:, half], Eh[:, half].bitcast(F32), ALU.subtract)\
                    .then_inc(el_done, 1)

            def low_v(h, j):
                dve.wait_ge(vh_done, 2 * h + j + 1)
                half = slice(j * HALF, (j + 1) * HALF)
                dve.tensor_tensor(VTcl[:, half], VTc[:, half], VTch[:, half].bitcast(F32), ALU.subtract)\
                    .then_inc(vl_done, 1)

            def low_out(n, slot):
                dve.wait_ge(wo_hi, n + 1)
                dve.tensor_tensor(outl[:, slot, :], outring[:, slot, :], outh[:, slot, :].bitcast(F32), ALU.subtract)\
                    .then_inc(wo_split, 1)

            def scale_v(h, slot, j):
                dve.wait_ge(csum_done, 2 * h + j + 1)
                dve.wait_ge(act_evac, 4 * h + 3 + j)
                dve.wait_ge(vl_done, count(2 * (h - 1) + j + 1))
                dve.tensor_tensor(VTc[:, j * HALF:(j + 1) * HALF], bank[:, 2 + j, :],
                                  VT[:, slot, j * HALF:(j + 1) * HALF], ALU.mult).then_inc(vc_done, 1)

            def head(h, slot):
                last = isinstance(h, int) and h == NH - 1
                row_max(h, 0)
                row_max(h, 1)
                recip(h, 0)
                recip(h, 1)
                low_e(h, 0)
                if not last:
                    evac_k(h + 1, 1 - slot, 0)
                low_e(h, 1)
                low_out(h, slot)
                scale_v(h, slot, 0)
                if not last:
                    evac_k(h + 1, 1 - slot, 1)
                low_v(h, 0)
                scale_v(h, slot, 1)
                low_v(h, 1)

            evac_k(0, 0, 0)
            evac_k(0, 0, 1)
            two_at_a_time(dve, NH, head)

            def norm(layer_norm, produced, steps, first_bank=4):
                if layer_norm == 0:
                    dve.wait_ge(x_in, 16)
                if layer_norm > 0:
                    dve.wait_ge(ln_x0, 4 * layer_norm)

                def add(q):
                    dve.wait_ge(produced, steps[q])
                    return dve.tensor_tensor(rN[:, 2 * q:2 * q + 2, :],
                                             bank[:, first_bank + q, :].rearrange("p (b d) -> p b d", b=2),
                                             xN[:, 2 * q:2 * q + 2, :], ALU.add)

                def statistics(j):
                    for b in range(4 * j, 4 * j + 4):
                        ins = dve.bn_stats(st[:, b, :], rN[:, b, :])
                    link(ins)
                    for b in range(4 * j, 4 * j + 4):
                        ins = dve.bn_aggr(mv[:, b, :], st[:, b, :])
                    link(ins)
                    half = slice(4 * j, 4 * j + 4)
                    dve.tensor_scalar(ve[:, half], mv[:, half, 1], EPS, None, ALU.add).then_inc(ln_var, 1)
                    if j == 0:
                        link(dve.tensor_scalar(nmean[:], mv[:, half, 0], -1.0, None, ALU.mult))

                def deviation_inverse(j):
                    half = slice(4 * j, 4 * j + 4)
                    dve.wait_ge(ln_sd, 2 * layer_norm + j + 1)
                    link(dve.reciprocal(rstd[:, half], sd[:, half]))

                add(0)
                link(add(1))
                statistics(0)
                add(2)
                link(add(3))
                deviation_inverse(0)
                dve.tensor_tensor(shift[:], nmean[:], rstd[:, 0:4], ALU.mult).then_inc(ln_scale, 1)
                statistics(1)
                deviation_inverse(1)
                for b in range(4, B):
                    dve.tensor_scalar(xN[:, b, :], rN[:, b, :], mv[:, b, 0:1], rstd[:, b:b + 1],
                                      ALU.subtract, ALU.mult).then_inc(ln_x1, 1)

            def split_x(n_split):
                for n, (k, j) in enumerate(((0, 0), (1, 0), (0, 1), (1, 1))):
                    dve.wait_ge(xt_high, 4 * n_split + n + 1)
                    half = slice(j * HALF, (j + 1) * HALF)
                    dve.tensor_tensor(xTl[:, k, half], xT[:, k, half], xTh[:, k, half].bitcast(F32), ALU.subtract)\
                        .then_inc(xt_hl, 1)

            norm(0, out0_banks, [1, 2, 3, 4])

            def conv_fix(layer, h, slot):
                dve.wait_ge(toep_in[slot], 4 * (CH * layer + h - slot) + 16)
                dve.scalar_tensor_tensor(toep[:, slot, 0:P], ident, dskip[:, bass.ds(h, 1)], toep[:, slot, 0:P],
                                         ALU.mult, ALU.add).then_inc(toep_fix, 1)

            def conv_reduce(layer, h, slot, gate):
                for l in range(DK):
                    s = 2 * (CH * layer + h) + l
                    dve.wait_ge(conv_done, s + 1)
                    dve.wait_ge(osum_done, count(s - 1))
                    g = gate[:, l, :, bass.ds(CI * h, CI)].unsqueeze(3).broadcast_to([P, B, CI, CI])
                    dve.tensor_tensor(prod[:, l, :].rearrange("p (b j i) -> p b i j", b=B, j=CI),
                                      bank[:, 2 * slot + l, :].rearrange("p (b i j) -> p b i j", b=B, i=CI),
                                      g, ALU.mult).then_inc(prod_done, 1)
                for l in range(DK):
                    s = 2 * (CH * layer + h) + l
                    dve.wait_ge(prod_done, s + 1)
                    dve.tensor_reduce(oT[:, l, :, bass.ds(CI * h, CI)],
                                      prod[:, l, :].rearrange("p (b j i) -> p b j i", b=B, j=CI), AX, ALU.add)\
                        .then_inc(osum_done, 1)

            xTv = xT[:].rearrange("p k (b s) -> p k b s", b=B)
            dve.wait_ge(skip0_in, 16)
            for h in range(3):
                conv_fix(0, h, h)
            dve.wait_ge(xt_act, 4)

            def conv0(i):
                for slot in range(4):
                    conv_reduce(0, 4 * i + slot, slot % 2, xTv)
                    if not isinstance(i, int) or i < CH // 4 - 1 or slot == 0:
                        conv_fix(0, 4 * i + slot + 3, (slot + 3) % 4)

            conv0(0)
            with dve.Fori(1, CH // 4 - 1) as i:
                conv0(i)
            conv0(CH // 4 - 1)
            norm(1, ot_psum, [1, 2, 3, 4])
            split_x(0)

            dve.wait_ge(sel_in, 16)
            dve.tensor_copy(sel[0:3 * NE0, :], selstage[0:3 * NE0, :]).then_inc(const_conv, 1)
            dve.tensor_copy(causalb[:], cst[:, C_CAUSAL:C_CAUSAL + P]).then_inc(const_conv, 1)
            link(dve.tensor_copy(identb[:], ident))

            def chosen(values, n, top, mask, scratch):
                for b in range(B):
                    ins = dve.max(top8[:, b, :], values[:, b, :])
                link(ins)
                for b in range(B):
                    ins = dve.max_index(idx8[:, b, :], top8[:, b, :], values[:, b, :])
                link(ins)
                link(dve.tensor_copy(idxf[:], idx8[:]))
                iota = cst[:, C_IOTA:C_IOTA + n].unsqueeze(1).broadcast_to([P, B, n])
                for r in range(top):
                    at = idxf[:, :, r:r + 1].broadcast_to([P, B, n])
                    link(dve.tensor_tensor(scratch if r else mask, iota, at, ALU.is_equal))
                    if r:
                        link(dve.tensor_tensor(mask, mask, scratch, ALU.add))

            dve.wait_ge(logit_done, 1)
            lg = bank[:, 4, 0:B * NE0].rearrange("p (b e) -> p b e", b=B)
            link(dve.tensor_reduce(m1[:], lg, AX, ALU.max))
            dve.tensor_tensor(e0, lg, m1[:].unsqueeze(2).broadcast_to([P, B, NE0]), ALU.subtract)\
                .then_inc(logits_shifted, 1)
            dve.wait_ge(logits_exp, 1)
            chosen(e0, NE0, TOP0, hit, rest)
            link(dve.tensor_tensor(rw, hit, e0, ALU.mult))
            link(dve.tensor_reduce(s1[:], rw, AX, ALU.add))
            link(dve.reciprocal(r1[:], s1[:]))
            link(dve.tensor_tensor(rw, rw, r1[:].unsqueeze(2).broadcast_to([P, B, NE0]), ALU.mult))
            link(dve.tensor_copy(rw3[:, :, 0, :], rw))
            link(dve.tensor_tensor(rest, rw, rw3[:, :, 0, :], ALU.subtract))
            link(dve.tensor_copy(rw3[:, :, 1, :], rest))
            dve.tensor_tensor(rw3[:, :, 2, :], rest, rw3[:, :, 1, :], ALU.subtract).then_inc(rw3_done, 1)
            dve.wait_ge(rwt_psum, 1)
            dve.tensor_copy(rwT[0:3 * NE0, :], bank[0:3 * NE0, 5, :].bitcast(BF16)).then_inc(rwt_done, 1)

            def experts(n, slot):
                for j in range(2):
                    s = 2 * n + j
                    dve.wait_ge(silu_done, s + 1)
                    dve.wait_ge(u_done, s + 1)
                    dve.tensor_tensor(H1[:, j, :], bank[:, 1, :], SG[:, j, :], ALU.mult).then_inc(gu_done, 1)
                    dve.wait_ge(r_done, s + 1)
                    dve.wait_ge(gu_done, s + 1)
                    dve.wait_ge(hl_done, count(s - 1))
                    dve.tensor_tensor(HT[:, j, :], bank[:, 2, :], H1[:, j, :], ALU.mult).then_inc(h_done, 1)
                    if j == 0:
                        low_out(NH + n, slot)
                    dve.wait_ge(hh_done, s + 1)
                    dve.tensor_tensor(HTl[:, j, :], HT[:, j, :], HTh[:, j, :].bitcast(F32), ALU.subtract)\
                        .then_inc(hl_done, 1)

            two_at_a_time(dve, NB0, experts)
            norm(2, down_done, [2 * NB0 - 1] * 2 + [2 * NB0] * 2)
            split_x(1)

            dve.wait_ge(wq1_in, 16)
            cos = cst[:, C_COS:C_COS + P].unsqueeze(1).broadcast_to([P, 4, S])
            sin = cst[:, C_SIN:C_SIN + P].unsqueeze(1).broadcast_to([P, 4, S])
            n = 0
            for w in range(2):
                for r in range(2):
                    for j in range(2):
                        for dst, table in ((TC, cos), (TS, sin)):
                            dve.wait_ge(qkv_psum, n + 1)
                            dve.tensor_tensor(dst[:, w, r, 4 * j:4 * j + 4, :],
                                              bank[:, n % 4, :].rearrange("p (b t) -> p b t", b=4),
                                              table, ALU.mult).then_inc(rope_done, 1)
                            n += 1
            dve.wait_ge(v_psum, 1)
            dve.wait_ge(vn_ones, 1)
            dve.tensor_copy(Vn[:, :, :, 0:HD], bank[:, 6, :].rearrange("p (b g d) -> p b g d", b=B, g=NKV))\
                .then_inc(yn_done, 1)

            def norm_y(b, slot):
                dve.wait_ge(weighed, NKV * b + NKV)
                y = bank[:, 4 + slot, 0:NQ * (HD + 1)].rearrange("p (h d) -> p h d", h=NQ)
                dve.reciprocal(yr[:, slot, :], y[:, :, HD]).then_inc(y_rec, 1)
                dve.wait_ge(y_rec, b + 1)
                dve.tensor_tensor(yN[:, b, :].rearrange("p (h d) -> p h d", h=NQ), y[:, :, 0:HD],
                                  yr[:, slot, :].unsqueeze(2).broadcast_to([P, NQ, HD]), ALU.mult)\
                    .then_inc(yn_done, 1)

            group = cst[:, C_GROUP:C_GROUP + NKV // 2].unsqueeze(2).broadcast_to([P, NKV // 2, S])

            def rotate_q(b, slot):
                dve.wait_ge(rope_done, 16)
                dve.wait_ge(scores1_done, count(NKV * (b - 1)))
                dve.tensor_tensor(qb[:, slot, :, :], TC[:, 0, :, b, :], TS[:, 0, :, b, :], ALU.add)\
                    .then_inc(q_done, 1)

            def split_q(b, slot):
                dve.wait_ge(q_done, b + 1)
                dve.tensor_copy(qh[:, slot, :, :], qb[:, slot, :, :]).then_inc(qh_done, 1)
                dve.wait_ge(qh_done, b + 1)
                dve.tensor_tensor(qb[:, slot, :, :], qb[:, slot, :, :], qh[:, slot, :, :].bitcast(F32), ALU.subtract)\
                    .then_inc(ql_done, 1)

            def spread_q(b, slot, low, r):
                if low:
                    dve.wait_ge(ql_done, b + 1)
                q1 = (qb[:, slot, r, :] if low else qh[:, slot, r, :].bitcast(F32))
                ins = dve.tensor_tensor((qel if low else qeh)[:, slot, r, :, :],
                                        q1.unsqueeze(1).broadcast_to([P, NKV // 2, S]), group, ALU.mult)
                if low:
                    ins.then_inc(qe_ready, 1)

            def ready_q(b, slot, step):
                if step == 1:
                    rotate_q(b, slot)
                elif step == 2:
                    split_q(b, slot)
                elif step in (3, 4, 5, 6):
                    spread_q(b, slot, (step - 3) % 2, (step - 3) // 2)

            for step in range(1, 7):
                ready_q(0, 0, step)

            def attn1(b, slot):
                for g in range(NKV):
                    if not isinstance(b, int) or b < B - 1:
                        ready_q(b + 1, 1 - slot, g)
                    t = NKV * b + g
                    sc = bank[:, g % 4, :].rearrange("p (q s) -> p q s", q=REP)
                    dve.wait_ge(scores1_done, t + 1)
                    dve.tensor_reduce(mx1[:, g % 4, :], sc, AX, ALU.max).then_inc(max1_done, 1)
                    dve.wait_ge(max1_done, t + 1)
                    dve.wait_ge(turned, count(t - 3))
                    dve.tensor_tensor(Pe[:, g % 4, :].rearrange("p (q s) -> p q s", q=REP), sc,
                                      mx1[:, g % 4, :].unsqueeze(2).broadcast_to([P, REP, S]), ALU.subtract)\
                        .then_inc(shifted, 1)
                    if g == NKV - 1 and (not isinstance(b, int) or b > 0):
                        norm_y(b - 1, 1 - slot)

            two_at_a_time(dve, B, attn1)
            norm_y(B - 1, 1)
            norm(3, wo_done, [1, 2, 3, 4])

            dve.wait_ge(xt_act, 16)

            def conv1(h, slot):
                conv_reduce(1, h, slot, cT)

            conv1(0, 0)
            conv1(1, 1)
            dve.wait_ge(bx1v_done, 1)
            for m in range(DK):
                ins = dve.tensor_reduce(skr[:, m, :], bx1v[:, m, :, :].rearrange("p b (h i) -> p (b h) i", i=CI),
                                        AX, ALU.add)
            ins.then_inc(skr_done, 1)
            with dve.Fori(1, CH // 2) as i:
                conv1(2 * i, 0)
                conv1(2 * i + 1, 1)
            dve.wait_ge(skip_add, 1)
            dve.wait_ge(osum_done, 4 * CH)
            for m in range(DK):
                ins = dve.tensor_tensor(oT[:, m, :, :], oT[:, m, :, :], bx1[:, m, :, :], ALU.add)
            ins.then_inc(sum_done, 1)
            norm(4, ot_psum, [5, 6, 7, 8])

            split_x(2)
            dve.wait_ge(sel_low_in, 16)
            dve.tensor_copy(selp[:].rearrange("p e h c -> p (e h c)"), lowraw[:, 1, :]).then_inc(sel_low_done, 1)

            QL = LOW // 4

            def stack_high(f, slot, q):
                if q == 0:
                    dve.wait_ge(lowraw_in[slot], 8 * (f - slot) + 16)
                    dve.wait_ge(up1_done, count(18 * (f - 1)))
                cols = slice(q * QL, (q + 1) * QL)
                dve.tensor_copy(bstk[:, slot, cols], lowraw[:, slot, cols]).then_inc(low_hi, 1)

            def stack_low(f, slot, q):
                dve.wait_ge(low_hi, 4 * f + q + 1)
                low = bstk[P // 2:P, slot, q * QL:(q + 1) * QL]
                dve.tensor_tensor(low, lowraw[P // 2:P, slot, q * QL:(q + 1) * QL], low.bitcast(F32), ALU.subtract)\
                    .then_inc(low_split, 1)

            for q in range(4):
                stack_high(0, 0, q)

            def low_input(n):
                dve.wait_ge(a_hi, n + 1)
                dve.tensor_tensor(ahl[:, n % 2, 1, :], bank[:, n, :], ahl[:, n % 2, 0, :].bitcast(F32),
                                  ALU.subtract).then_inc(a_lo, 1)

            low_input(0)
            low_input(1)
            for q in range(4):
                stack_low(0, 0, q)
            dve.wait_ge(l1_done, 1)
            lg1 = bank[:, 4, 0:B * NE1].rearrange("p (b e) -> p b e", b=B)
            link(dve.tensor_reduce(m1[:], lg1, AX, ALU.max))
            dve.tensor_tensor(we1[:], lg1, m1[:].unsqueeze(2).broadcast_to([P, B, NE1]), ALU.subtract)\
                .then_inc(l1_sub, 1)
            for n in range(4):
                for e in range(1, NE1, 2):
                    dve.wait_ge(stack_psum, NE1 * n + e + 1)
                    dve.tensor_copy(astk[:, n // 2, e, (n % 2) * HALF:(n % 2 + 1) * HALF], bank[:, 4 + (e + 1) % 4, :])\
                        .then_inc(stack_dve, 1)
                if n < 2:
                    low_input(n + 2)
            dve.wait_ge(l1_exp, 1)
            link(dve.tensor_reduce(s1[:], we1[:], AX, ALU.add))
            link(dve.reciprocal(r1[:], s1[:]))
            link(dve.tensor_scalar(r1[:], r1[:], SCALING, None, ALU.mult))
            chosen(we1[:], NE1, TOP1, hit1[:], rest1[:])
            link(dve.tensor_tensor(we1[:], we1[:], hit1[:], ALU.mult))
            dve.tensor_tensor(we1[:], we1[:], r1[:].unsqueeze(2).broadcast_to([P, B, NE1]), ALU.mult)\
                .then_inc(we1_done, 1)
            dve.wait_ge(we1_done, 1)
            dve.tensor_copy(wrep.rearrange("p (b e) r -> p b e r", b=B),
                            we1[:].unsqueeze(3).broadcast_to([P, B, NE1, RANK])).then_inc(wrep_done, 1)

            def gated(f, slot):
                for c in range(2):
                    for e in range(NE1 + 1):
                        k = 18 * f + 9 * c + e
                        dve.wait_ge(f_silu, k + 1)
                        dve.wait_ge(up1_done, k + 1)
                        dve.wait_ge(f_down, count(k - 1))
                        dve.tensor_tensor(HF[:, (c + e) % 2, :], bank[:, 1, :], SF[:, (c + e) % 2, :], ALU.mult)\
                            .then_inc(f_mul, 1)
                        if not isinstance(f, int) or f + 1 < FB:
                            if c == 1 and e < 4:
                                stack_high(f + 1, 1 - slot, e)
                            elif c == 1 and e < NE1:
                                stack_low(f + 1, 1 - slot, e - 4)

            two_at_a_time(dve, FB, gated)
            dve.wait_ge(f_down, 18 * FB)
            for c in range(2):
                dve.wait_ge(wt_evac, c + 1)
                dve.tensor_tensor(xT[:, 0, c * HALF:(c + 1) * HALF], bank[:, 6 + c, :], SF[:, c, :], ALU.mult)\
                    .then_inc(dw_done, 1)
            norm(5, bd_done, [1, 2, 3, 4], first_bank=2)

        @block.tensor
        def _(pe):
            halves = [slice(0, HALF), slice(HALF, TOK)]

            def split_product(o, slot, col, j):
                for k in range(DK):
                    wc = slice(col + k * P, col + (k + 1) * P)
                    pe.matmul(o, ringh[:, slot, wc], xTh[:, k, halves[j]], start=(k == 0), stop=False)
                    pe.matmul(o, ringh[:, slot, wc], xTl[:, k, halves[j]], start=False, stop=False)
                    ins = pe.matmul(o, ringl[:, slot, wc], xTh[:, k, halves[j]], start=False, stop=(k == DK - 1))
                return ins

            def project(h, slot, c):
                if c == 0:
                    pe.wait_ge(w_split, h + 1)
                if c < 4:
                    pe.wait_ge(act_evac, count(4 * h - 1 + c))
                else:
                    pe.wait_ge(dve_evac, count(2 * h + c - 3))
                split_product(bank[:, c % 2, :], slot, (c // 2) * DK * P, c % 2).then_inc(proj_done, 1)

            def scores(h, slot, j):
                pe.wait_ge(act_evac, 4 * h + 1 + j)
                pe.wait_ge(dve_evac, 2 * h + 1 + j)
                pe.wait_ge(vc_done, count(2 * h - 1 + j))
                for b in range(4 * j, 4 * j + 4):
                    t = slice(b * S, (b + 1) * S)
                    ins = pe.matmul(bank[:, 2 + j, (b % 4) * S:(b % 4 + 1) * S], QT[:, slot, t], KT[:, slot, t],
                                    start=True, stop=True)
                ins.then_inc(s_done, 1)

            def key_weights(h, j):
                pe.wait_ge(el_done, 2 * h + j + 1)
                half = slice(j * HALF, (j + 1) * HALF)
                pe.matmul(bank[:, 2 + j, :], ones[:], Eh[:, half], start=True, stop=False)
                pe.matmul(bank[:, 2 + j, :], ones[:], El[:, half], start=False, stop=True).then_inc(csum_done, 1)

            def out_products(o, xh, xl, wh, wl, first, final):
                pe.matmul(o, xh, wh, start=first, stop=False, skip_group_check=True)
                pe.matmul(o, xl, wh, start=False, stop=False, skip_group_check=True)
                return pe.matmul(o, xh, wl, start=False, stop=final, skip_group_check=True)

            def attn_out(h, slot):
                pe.wait_ge(wo_split, h + 1)
                for b in range(B):
                    if b % 4 == 0:
                        pe.wait_ge(vl_done, 2 * h + b // 4 + 1)
                    t = slice(b * S, (b + 1) * S)
                    ins = out_products(bank[:, 4 + b // 2, (b % 2) * D:(b % 2 + 1) * D], VTch[:, t], VTcl[:, t],
                                       outh[:, slot, :], outl[:, slot, :],
                                       isinstance(h, int) and h == 0 and b % 2 == 0,
                                       isinstance(h, int) and h == NH - 1)
                    if isinstance(h, int) and h == NH - 1 and b % 2 == 1:
                        ins.then_inc(out0_banks, 1)
                if not isinstance(h, int) or h < NH - 1:
                    ins.then_inc(out0_done, 1)

            def head(h, slot):
                def ahead(c):
                    if not isinstance(h, int) or h < NH - 1:
                        project(h + 1, 1 - slot, c)
                scores(h, slot, 0)
                ahead(0)
                scores(h, slot, 1)
                ahead(1)
                if not isinstance(h, int) or h > 0:
                    attn_out(h - 1, 1 - slot)
                ahead(2)
                key_weights(h, 0)
                ahead(3)
                key_weights(h, 1)
                ahead(4)
                ahead(5)

            pe.wait_ge(x_split, 1)
            for c in range(6):
                project(0, 0, c)
            pe.wait_ge(ones_done, 1)
            two_at_a_time(pe, NH, head)
            attn_out(NH - 1, 1)

            def turn(layer_norm):
                for b in range(B):
                    pe.wait_ge(ln_x1 if b >= 4 else ln_x0, 4 * layer_norm + b % 4 + 1)
                    for k in range(DK):
                        ins = pe.transpose(bank[:, 2 * k + b // 4, (b % 4) * S:(b % 4 + 1) * S],
                                           xN[:, b, k * P:(k + 1) * P], ident)
                        if b % 4 == 3:
                            ins.then_inc(xt_psum, 1)

            pe.wait_ge(const_in, 16)
            turn(0)

            def conv(layer, h, slot):
                n = CH * layer + h
                if layer == 0:
                    pe.wait_ge(toep_fix, h + 1)
                else:
                    pe.wait_ge(toep_in[slot], 4 * (n - slot) + 16)
                pe.wait_ge(kv_done, 2 * n + 1)
                pe.wait_ge(prod_done, count(2 * n - 2))
                diag, off = toep[:, slot, 0:P], toep[:, slot, P:D]
                slot = slot % 2
                pe.matmul(bank[:, 2 * slot, :], diag, kv[:, slot, 0, :], start=True, stop=True)\
                    .then_inc(conv_done, 1)
                pe.matmul(bank[:, 2 * slot + 1, :], off, kv[:, slot, 0, :], start=True, stop=False)
                pe.wait_ge(kv_done, 2 * n + 2)
                pe.matmul(bank[:, 2 * slot + 1, :], diag, kv[:, slot, 1, :], start=False, stop=True)\
                    .then_inc(conv_done, 1)

            def turn_back():
                for b in range(B):
                    for l in range(DK):
                        ins = pe.transpose(bank[:, 4 + b // 2, (b % 2) * D + l * P:(b % 2) * D + (l + 1) * P],
                                           oT[:, l, b, :], ident)
                    if b % 2 == 1:
                        ins.then_inc(ot_psum, 1)

            def conv_layer(layer):
                for h in range(4):
                    conv(layer, h, h)
                with pe.Fori(1, CH // 4) as i:
                    for slot in range(4):
                        conv(layer, 4 * i + slot, slot)

            pe.wait_ge(xt_act, 4)
            conv_layer(0)
            pe.wait_ge(osum_done, 2 * CH)
            turn_back()
            turn(1)

            pe.wait_ge(wres_in, 16)
            pe.wait_ge(xt_act, 8)
            for b in range(B):
                for k in range(DK):
                    ins = pe.matmul(bank[:, 4, b * NE0:(b + 1) * NE0], xT[:, k, b * S:(b + 1) * S],
                                    wres[:, k, R_GATE:R_GATE + NE0], start=(k == 0), stop=(k == DK - 1))
            ins.then_inc(logit_done, 1)
            def turn_router():
                pe.wait_ge(rw3_done, 1)
                rwt = bank[0:3 * NE0, 5, :].bitcast(BF16)
                for b in range(B):
                    ins = pe.transpose(rwt[:, b * S:(b + 1) * S], rw3[:, b, :, :].rearrange("p c e -> p (c e)"),
                                       identb[:])
                ins.then_inc(rwt_psum, 1)
                pe.wait_ge(rwt_done, 1)

            def down(n, slot, j):
                s = 2 * n + j
                if j == 0:
                    pe.wait_ge(wo_split, NH + n + 1)
                pe.wait_ge(hl_done, s + 1)
                for b in range(4 * j, 4 * j + 4):
                    t = slice((b % 4) * S, (b % 4 + 1) * S)
                    ins = out_products(bank[:, 4 + b // 2, (b % 2) * D:(b % 2 + 1) * D], HTh[:, j, t], HTl[:, j, t],
                                       outh[:, slot, :], outl[:, slot, :],
                                       isinstance(n, int) and n == 0 and b % 2 == 0,
                                       isinstance(n, int) and n == NB0 - 1)
                ins.then_inc(down_done, 1)

            def experts(n, slot):
                pe.wait_ge(w_split, NH + n + 1)
                for j in range(2):
                    s = 2 * n + j
                    start = isinstance(n, int) and n == 0
                    if not (start and j == 1):
                        pe.wait_ge(silu_done, count(s - 1))
                        split_product(bank[:, 3 * j, :], slot, 0, j).then_inc(g_done, 1)
                    pe.wait_ge(gu_done, s)
                    split_product(bank[:, 1, :], slot, DK * P, j).then_inc(u_done, 1)
                    if start and j == 0:
                        split_product(bank[:, 3, :], slot, 0, 1).then_inc(g_done, 1)
                        turn_router()
                    pe.wait_ge(h_done, s)
                    pe.matmul(bank[:, 2, :], sel[0:3 * NE0, bass.ds(n * P, P)], rwT[0:3 * NE0, halves[j]],
                              start=True, stop=True).then_inc(r_done, 1)
                    if j == 1:
                        down(n, slot, 0)
                    elif not isinstance(n, int) or n > 0:
                        down(n - 1, 1 - slot, 1)

            pe.wait_ge(xt_hl, 4)
            two_at_a_time(pe, NB0, experts)
            down(NB0 - 1, 1, 1)
            turn(2)

            pe.wait_ge(wq1_in, 16)
            pe.wait_ge(xt_act, 12)
            n = 0
            for w in range(2):
                for r in range(2):
                    for j in range(2):
                        for col in ((Q_W, Q_WS), (K_W, K_WS))[w]:
                            pe.wait_ge(rope_done, count(n - 3))
                            pe.wait_ge(xt_hl, 6 + 2 * j)
                            for k in range(DK):
                                pe.wait_ge(wq_split, k + 1)
                                c = slice(col + r * P, col + (r + 1) * P)
                                o = bank[:, n % 4, :]
                                pe.matmul(o, wqh[k][:, c], xTh[:, k, halves[j]], start=(k == 0), stop=False)
                                pe.matmul(o, wqh[k][:, c], xTl[:, k, halves[j]], start=False, stop=False)
                                ins = pe.matmul(o, wql[k][:, c], xTh[:, k, halves[j]], start=False, stop=(k == DK - 1))
                            ins.then_inc(qkv_psum, 1)
                            n += 1
            for b in range(B):
                for k in range(DK):
                    ins = pe.matmul(bank[:, 6, b * NKV * HD:(b + 1) * NKV * HD], xT[:, k, b * S:(b + 1) * S],
                                    wq1[:, k, V_W:V_W + NKV * HD], start=(k == 0), stop=(k == DK - 1))
            ins.then_inc(v_psum, 1)
            pe.wait_ge(vn_ones, 1)
            pe.wait_ge(yn_done, 1)
            causal4 = causalb[:].unsqueeze(1).broadcast_to([P, REP, S])

            def scores1(b, slot, g):
                t = NKV * b + g
                if g % 4 == 0:
                    pe.wait_ge(ke_ready, 2 * b + g // 4 + 1)
                    pe.wait_ge(qe_ready, 2 * b + g // 4 + 1)
                pe.wait_ge(shifted, count(t - 3))
                o = bank[:, g % 4, :]
                qhigh, qlow = qeh[:, slot, g // 4, g % 4, :], qel[:, slot, g // 4, g % 4, :]
                khigh = keh[slot][:, g // 4, :, :].rearrange("p q t -> p (q t)")
                klow = kel[slot][:, g // 4, :, :].rearrange("p q t -> p (q t)")
                pe.matmul(o, qhigh, khigh, start=True, stop=False)
                pe.matmul(o, qlow, khigh, start=False, stop=False)
                pe.matmul(o, qhigh, klow, start=False, stop=False)
                pe.matmul(o.rearrange("p (q s) -> p q s", q=REP), identb[:], causal4, start=False, stop=True)\
                    .then_inc(scores1_done, 1)

            def turn_probs(b, slot, g):
                t = NKV * b + g
                pe.wait_ge(exp1_done, t + 1)
                pe.wait_ge(turned_out, count(t - 1))
                for q in range(REP):
                    ins = pe.transpose(bank[:, 6 + g % 2, q * S:(q + 1) * S], Pe[:, g % 4, q * S:(q + 1) * S], ident)
                ins.then_inc(turned, 1)

            def weigh(b, slot, g):
                t = NKV * b + g
                pe.wait_ge(turned_out, t + 1)
                if g == 0:
                    pe.wait_ge(yn_done, b)
                for q in range(REP):
                    c = (REP * g + q) * (HD + 1)
                    ins = pe.matmul(bank[:, 4 + slot, c:c + HD + 1], PT[:, g % 2, q * S:(q + 1) * S],
                                    Vn[:, b, g, :], start=(g == 0 and q == 0), stop=(g == NKV - 1 and q == REP - 1),
                                    skip_group_check=True)
                ins.then_inc(weighed, 1)

            def earlier(step, b, slot, g, back):
                if g >= back:
                    step(b, slot, g - back)
                elif not isinstance(b, int) or b > 0:
                    step(b - 1, 1 - slot, g - back + NKV)

            def attn1(b, slot):
                for g in range(NKV):
                    scores1(b, slot, g)
                    earlier(turn_probs, b, slot, g, 2)
                    earlier(weigh, b, slot, g, 3)

            two_at_a_time(pe, B, attn1)
            turn_probs(B - 1, 1, NKV - 2)
            weigh(B - 1, 1, NKV - 3)
            turn_probs(B - 1, 1, NKV - 1)
            weigh(B - 1, 1, NKV - 2)
            weigh(B - 1, 1, NKV - 1)
            for b in range(B):
                pe.wait_ge(yn_done, b + 2)
                for k in range(DK):
                    ins = pe.transpose(bank[:, 2 * k + b // 4, (b % 4) * S:(b % 4 + 1) * S],
                                       yN[:, b, k * P:(k + 1) * P], ident)
                    if b % 4 == 3:
                        ins.then_inc(y_psum, 1)
            for b in range(B):
                pe.wait_ge(yt_evac, 2 + 2 * (b // 4))
                for k in range(DK):
                    ins = pe.matmul(bank[:, 4 + b // 2, (b % 2) * D:(b % 2 + 1) * D], yT[:, k, b, :],
                                    wq1[:, k, O_W:O_W + D], start=(k == 0), stop=(k == DK - 1))
                if b % 2 == 1:
                    ins.then_inc(wo_done, 1)
            turn(3)

            pe.wait_ge(xt_act, 16)
            conv_layer(1)
            pe.wait_ge(sum_done, 1)
            turn_back()
            turn(4)

            pe.wait_ge(wres_split, 1)
            for n in range(4):
                pe.wait_ge(xt_hl, 10 + 2 * (n % 2))
                for k in range(DK):
                    cols = slice((n // 2) * P, (n // 2 + 1) * P)
                    pe.matmul(bank[:, n, :], agh[:, k, cols], xTh[:, k, halves[n % 2]], start=(k == 0), stop=False)
                    pe.matmul(bank[:, n, :], agh[:, k, cols], xTl[:, k, halves[n % 2]], start=False, stop=False)
                    ins = pe.matmul(bank[:, n, :], agl[:, k, cols], xTh[:, k, halves[n % 2]],
                                    start=False, stop=(k == DK - 1))
                ins.then_inc(a_psum, 1)
            for b in range(B):
                for k in range(DK):
                    ins = pe.matmul(bank[:, 4, b * NE1:(b + 1) * NE1], xT[:, k, b * S:(b + 1) * S],
                                    wres[:, k, R_WR:R_WR + NE1], start=(k == 0), stop=(k == DK - 1))
            ins.then_inc(l1_done, 1)
            pe.wait_ge(sel_low_done, 1)
            for n in range(4):
                pe.wait_ge(a_lo, n + 1)
                for e in range(NE1):
                    m = NE1 * n + e
                    if m == 3:
                        pe.wait_ge(l1_sub, 1)
                    if e % 2 == 0:
                        pe.wait_ge(stack_act, count(m // 2 - 1))
                    else:
                        pe.wait_ge(stack_dve, count(m // 2 - 1))
                    o = bank[:, 4 + (e + 1) % 4, :]
                    pe.matmul(o, selp[:, e, 0, :], ahl[:, n % 2, 0, :], start=True, stop=False)
                    pe.matmul(o, selp[:, e, 1, :], ahl[:, n % 2, 1, :], start=False, stop=True).then_inc(stack_psum, 1)
            pe.wait_ge(stack_act, 2 * NE1)
            pe.wait_ge(stack_dve, 2 * NE1)
            pe.wait_ge(xt_hl, 12)

            def down1(f, slot, c, e):
                pe.wait_ge(f_mul, 18 * f + 9 * c + e + 1)
                first = isinstance(f, int) and f == 0
                if e == 0:
                    for b in range(4 * c, 4 * c + 4):
                        ins = pe.matmul(bank[:, 2 + b // 2, (b % 2) * D:(b % 2 + 1) * D],
                                        HF[:, c, (b % 4) * S:(b % 4 + 1) * S], ring[:, slot, F_WD:F_WD + D],
                                        start=(first and b % 2 == 0), stop=False, skip_group_check=True)
                else:
                    if c == 0 and e == 1:
                        pe.wait_ge(adp_done, f + 1)
                    ins = pe.matmul(bank[:, 6 + c, :], adp[:, slot, e - 1, :], HF[:, (c + e) % 2, :],
                                    start=(first and e == 1), stop=(isinstance(f, int) and f == FB - 1 and e == NE1),
                                    skip_group_check=True)
                ins.then_inc(f_down, 1)

            def two_before(f, slot, c, e):
                n = (NE1 + 1) * c + e - 2
                if n >= 0:
                    return f, slot, n // (NE1 + 1), n % (NE1 + 1)
                return None if isinstance(f, int) and f == 0 else (f - 1, 1 - slot, 1, NE1 + 1 + n)

            def ffn1(f, slot):
                pe.wait_ge(w_split, NH + NB0 + f + 1)
                pe.wait_ge(low_split, 4 * (f + 1))
                for c in range(2):
                    for e in range(NE1 + 1):
                        k = 18 * f + 9 * c + e
                        for g, done in ((0, gate1_done), (1, up1_done)):
                            if g == 0:
                                pe.wait_ge(f_silu, k)
                            else:
                                pe.wait_ge(f_mul, k)
                            if e == 0:
                                ins = split_product(bank[:, g, :], slot, g * DK * P, c)
                            else:
                                w = (g * NE1 + e - 1) * P
                                ins = pe.matmul(bank[:, g, :], bstk[:, slot, w:w + P], astk[:, g, e - 1, halves[c]],
                                                start=False, stop=True, skip_group_check=True)
                            ins.then_inc(done, 1)
                            last = two_before(f, slot, c, e)
                            if g == 0 and last:
                                down1(*last)

            two_at_a_time(pe, FB, ffn1)
            down1(FB - 1, 1, 1, NE1 - 1)
            down1(FB - 1, 1, 1, NE1)
            pe.wait_ge(wrep_done, 1)
            for c in range(2):
                for t in range(4):
                    w = rN[:, 2 * c:2 * c + 2, :].rearrange("p a d -> p (a d)")[:, t * P:(t + 1) * P]
                    ins = pe.transpose(bank[:, c, t * P:(t + 1) * P], w, ident)
                ins.then_inc(wt_psum, 1)
            pe.wait_ge(bd_in, 16)
            for b in range(B):
                pe.wait_ge(dw_done, b // 4 + 1)
                ins = pe.matmul(bank[:, 2 + b // 2, (b % 2) * D:(b % 2 + 1) * D], xT[:, 0, b * S:(b + 1) * S], bd[:],
                                start=False, stop=True, skip_group_check=True)
                if b % 2 == 1:
                    ins.then_inc(bd_done, 1)


def kernel(**inputs):
    import numpy as np
    import concourse.bacc as bacc
    from concourse.bass_utils import run_bass_kernel_spmd

    a = {k: np.asarray(v) for k, v in inputs.items()}

    def blocks(w, n):
        return w.reshape(DK, P, n).transpose(1, 0, 2)

    def toeplitz(k):
        padded = np.zeros((CH, P - 1 + D), np.float32)
        padded[:, P - 1:] = k
        at = P - 1 - np.arange(P)[:, None] + np.arange(D)[None, :]
        return padded[:, at]

    w_attn0 = a["L0_attn_w_qkv"].reshape(DK, P, 3, NH, DH).transpose(3, 1, 2, 0, 4).reshape(NH, P, A_WO)

    gu = a["L0_ffn_gate_up_proj"].reshape(NE0, D, 2, INTER).transpose(2, 1, 0, 3).reshape(2, DK, P, NB0, P)
    w_moe = gu.transpose(3, 2, 0, 1, 4).reshape(NB0, P, C_DOWN)

    swap = np.arange(D) ^ 1
    wq, wo = a["L1_attn_wq"], a["L1_attn_wo"]
    wk = np.repeat(a["L1_attn_wk"].reshape(NKV, 1, HD, D), REP, axis=1).reshape(D, D)
    w_attn1 = np.concatenate([blocks(m.T, m.shape[0]) for m in (wq, wq[swap], wk, wk[swap], a["L1_attn_wv"], wo)],
                             axis=2)
    w_res = np.concatenate([blocks(a["L0_ffn_gate"], NE0), blocks(a["L1_ffn_Wr"].T, NE1),
                            blocks(a["L1_ffn_Ag"].reshape(P, D).T, P), blocks(a["L1_ffn_Au"].reshape(P, D).T, P)],
                           axis=2)

    def padded(m):
        z = np.zeros((FB * P, m.shape[1]), np.float32)
        z[:DFF] = m
        return z.reshape(FB, P, m.shape[1])

    def stationary(m):
        return padded(m).reshape(FB, P, DK, P).transpose(0, 3, 2, 1).reshape(FB, P, DK * P)

    def stacked(m):
        rows = padded(m.transpose(1, 0, 2).reshape(DFF, P)).reshape(FB, P, NE1, RANK).transpose(0, 3, 2, 1)
        pair = np.zeros((FB, 2, RANK, NE1, P), np.float32)
        pair[:, 0] = rows
        pair[:, 1, :, 1:] = rows[:, :, :-1]
        return np.tile(pair.reshape(FB, 2 * RANK, NE1 * P), (1, 4, 1))

    w_low = np.concatenate([stacked(a["L1_ffn_Bg"]), stacked(a["L1_ffn_Bu"])], axis=2)
    w_ffn1 = np.concatenate([stationary(a["L1_ffn_Wg"]), stationary(a["L1_ffn_Wu"]),
                             padded(a["L1_ffn_Wd"].T), padded(a["L1_ffn_Ad"].reshape(P, DFF).T)], axis=2)
    w_bd = a["L1_ffn_Bd"].transpose(0, 2, 1).reshape(P, D)

    consts = np.zeros((P, CONST_COLS), np.float32)
    consts[:, C_ID:C_ID + P] = np.eye(P)
    theta = np.float32(1.0) / np.float32(10000.0) ** (np.arange(0, HD, 2, dtype=np.float32) / np.float32(HD))
    freqs = np.arange(S, dtype=np.float32)[None, :] * theta[(np.arange(P) % HD) // 2][:, None]
    consts[:, C_COS:C_COS + P] = np.cos(freqs)
    consts[:, C_SIN:C_SIN + P] = np.sin(freqs) * np.where(np.arange(P) % 2 == 0, -1, 1)[:, None]
    consts[:, C_CAUSAL:C_CAUSAL + P] = np.where(np.arange(P)[None, :] > np.arange(P)[:, None], MASKED, 0)
    consts[:, C_HQ:C_HQ + REP] = (np.arange(P) % 32 // HD)[:, None] == np.arange(REP)[None, :]
    consts[:, C_GROUP:C_GROUP + NKV // 2] = (np.arange(P) // 32)[:, None] == np.arange(NKV // 2)[None, :]
    selp = np.zeros((P, NE1, 2, 4, 2, RANK), np.float32)
    rank = np.arange(RANK)
    for e in range(NE1):
        for part in range(2):
            for quarter in (part, part + 2):
                selp[e * RANK + rank, e, part, quarter, 0, rank] = SCALING
                if e > 0:
                    selp[(e - 1) * RANK + rank, e, part, quarter, 1, rank] = -SCALING
    consts[:, C_IOTA:C_IOTA + NE0] = np.arange(NE0)
    sel3 = np.tile((np.arange(NE0)[:, None] == np.arange(NB0 * P)[None, :] // INTER).astype(np.float32), (3, 1))

    arrays = {
        "x_nat": a["x"].transpose(1, 0, 2), "x_t": a["x"].reshape(TOK, D).T,
        "ctx_t": a["ctx_2048"].transpose(2, 0, 1), "w_attn0": w_attn0,
        "wo_attn0": a["L0_attn_w_o"].reshape(NH, DH, D),
        "toep0": toeplitz(a["L0_xattn_ssm_kernel"]), "skip0": a["L0_xattn_D"],
        "w_res": w_res, "w_moe": w_moe, "w_down0": a["L0_ffn_down_proj"].reshape(NB0, P, D),
        "sel3": sel3, "w_attn1": w_attn1,
        "toep1": toeplitz(a["L1_xattn_k"]), "bias1": a["fside_S2_0"], "w_ffn1": w_ffn1,
        "w_low": w_low, "sel_low": selp.reshape(P, LOW), "w_bd": w_bd,
        "consts": consts,
    }
    arrays = {k: np.ascontiguousarray(v) for k, v in arrays.items()}
    nc = bacc.Bacc("TRN2", target_bir_lowering=False, num_devices=1)
    args = [nc.dram_tensor(k, v.shape, mybir.dt.from_np(v.dtype), kind="ExternalInput").ap() for k, v in arrays.items()]
    out = nc.dram_tensor("out", (P, B, D), F32, kind="ExternalOutput").ap()
    decoder_layers(nc, *args, out)
    result = run_bass_kernel_spmd(nc, [arrays], core_ids=[0])
    return np.ascontiguousarray(result.results[0]["out"].transpose(1, 0, 2))
```
